# Optimizing a Trainium2 kernel written in Bass

```python
import numpy as np
import jax
import jax.numpy as jnp

def _softmax(x, axis=-1):
    return jax.nn.softmax(x, axis=axis)

def _gelu(x):
    return jax.nn.gelu(x, approximate=True)

def _silu(x):
    return jax.nn.silu(x)

def _sigmoid(x):
    return jax.nn.sigmoid(x)

def _layernorm(x, axis=-1, eps=1e-05):
    m = jnp.mean(x, axis=axis, keepdims=True)
    v = jnp.var(x, axis=axis, keepdims=True)
    return (x - m) / jnp.sqrt(v + eps)

def _scatter_add(tgt, idx, src, axis=0):
    return tgt.at[idx].add(src)

def _segment_sum(src, seg, n):
    return jax.ops.segment_sum(src, seg, n)
kernel_name = 'mk_gps_d1_gnn_r8_5834b6'

def setup_inputs(seed: int=0):
    np.random.seed(seed)
    _w = jnp.asarray

    def _rec_inputs():
        import jax
        import jax.numpy as jnp
        _gk = jax.random.key(seed)
        x = -0.0001074 + 0.9999 * jax.random.normal(jax.random.fold_in(_gk, 1), (6250, 256), jnp.float32)
        _s = jax.random.randint(jax.random.fold_in(_gk, 2), (50000,), 0, 6250, jnp.int32)
        _d = jax.random.randint(jax.random.fold_in(_gk, 3), (50000,), 0, 6250, jnp.int32)
        _loop = jnp.arange(6250, dtype=jnp.int32)
        src = jnp.concatenate([_s, _d, _loop])
        dst = jnp.concatenate([_d, _s, _loop])
        _o = jnp.argsort(dst, stable=True)
        src = src[_o]
        dst = dst[_o]
        return (x, src, dst)
    x, src, dst = _rec_inputs()

    def _L0_gnn_setup():
        import jax, jax.numpy as jnp
        import numpy as np
        N_ENT = 6250
        N_EDGE = 62500
        D = 256
        H1, C1 = (8, 64)
        NEG_SLOPE = 0.2
        LN_EPS = 1e-05

        def _gat_conv(x, edge_index, W, att_src, att_dst, bias, heads, out_ch, concat):
            n = x.shape[0]
            loops = jnp.arange(n)
            src = jnp.concatenate([edge_index[0], loops])
            dst = jnp.concatenate([edge_index[1], loops])
            h = (x @ W).reshape(n, heads, out_ch)
            a_src = jnp.sum(h * att_src[None], axis=-1)
            a_dst = jnp.sum(h * att_dst[None], axis=-1)
            e = jax.nn.leaky_relu(a_src[src] + a_dst[dst], NEG_SLOPE)
            m = jax.lax.stop_gradient(jax.ops.segment_max(e, dst, num_segments=n))
            p = jnp.exp(e - m[dst])
            denom = jax.ops.segment_sum(p, dst, num_segments=n)
            alpha = p / denom[dst]
            out = jax.ops.segment_sum(h[src] * alpha[..., None], dst, num_segments=n)
            out = out.reshape(n, heads * out_ch) if concat else out.mean(axis=1)
            return out + bias
        key = jax.random.key(seed)
        ks = jax.random.split(key, 12)
        s = 0.05
        return {'edge_index': jax.random.randint(ks[0], (2, N_EDGE), 0, N_ENT), 'x': jax.random.normal(ks[1], (N_ENT, D), dtype=jnp.float32), 'ln_w': jnp.ones((D,), jnp.float32), 'ln_b': jnp.zeros((D,), jnp.float32), 'W1': jax.random.normal(ks[2], (D, H1 * C1), dtype=jnp.float32) * s, 'att_src1': jax.random.normal(ks[3], (H1, C1), dtype=jnp.float32) * s, 'att_dst1': jax.random.normal(ks[4], (H1, C1), dtype=jnp.float32) * s, 'b1': jnp.zeros((H1 * C1,), jnp.float32), 'W2': jax.random.normal(ks[5], (H1 * C1, D), dtype=jnp.float32) * s, 'att_src2': jax.random.normal(ks[6], (1, D), dtype=jnp.float32) * s, 'att_dst2': jax.random.normal(ks[7], (1, D), dtype=jnp.float32) * s, 'b2': jnp.zeros((D,), jnp.float32)}
    _L0_gnn_all = _L0_gnn_setup()
    _L0_gnn_in = {k: v for k, v in _L0_gnn_all.items() if k in ('ln_w', 'ln_b', 'W1', 'att_src1', 'att_dst1', 'b1', 'W2', 'att_src2', 'att_dst2', 'b2')}
    del _L0_gnn_all

    def _L0_mix_setup():
        import jax, jax.numpy as jnp
        import numpy as np
        DIM = 256
        HEADS = 4
        DIM_HEAD = 32
        NUM_MEM = 4
        HIDDEN = HEADS * DIM_HEAD
        SCALE = DIM_HEAD ** (-0.5)

        def rmsnorm(x, g):
            n = jnp.linalg.norm(x, axis=-1, keepdims=True)
            return x / jnp.maximum(n, 1e-12) * g * x.shape[-1] ** 0.5
        key = jax.random.key(seed)
        ks = jax.random.split(key, 8)
        B, N = (4, 2048)
        return {'x': jax.random.normal(ks[0], (B, N, DIM), jnp.float32), 't': jax.random.normal(ks[1], (B,), jnp.float32), 'w_qkv': jax.random.normal(ks[2], (DIM, 3 * HIDDEN), jnp.float32) * 0.02, 'mem_kv': jax.random.normal(ks[3], (2, HEADS, DIM_HEAD, NUM_MEM), jnp.float32), 'w_out': jax.random.normal(ks[4], (HIDDEN, DIM), jnp.float32) * 0.02, 'b_out': jnp.zeros((DIM,), jnp.float32), 'g_out': jnp.ones((DIM,), jnp.float32), 'g_pre': jnp.ones((DIM,), jnp.float32)}
    _L0_mix_all = _L0_mix_setup()
    _L0_mix_in = {k: v for k, v in _L0_mix_all.items() if k in ('t', 'w_qkv', 'mem_kv', 'w_out', 'b_out', 'g_out', 'g_pre')}
    del _L0_mix_all

    def _L0_ffn_setup():
        import math
        import jax, jax.numpy as jnp
        import numpy as np
        CAPACITY_FACTOR = 1.25
        key = jax.random.key(seed)
        ks = jax.random.split(key, 5)
        B, L, D, F, E = (8, 1024, 256, 1024, 8)
        h = jax.random.normal(ks[0], (B, L, D), dtype=jnp.float32)
        gate_w = jax.random.normal(ks[1], (D, E), dtype=jnp.float32) * 0.02
        gate_b = jnp.zeros((E,), dtype=jnp.float32)
        w1 = jax.random.normal(ks[2], (E, D, F), dtype=jnp.float32) * (1.0 / math.sqrt(D))
        b1 = jnp.zeros((E, F), dtype=jnp.float32)
        w2 = jax.random.normal(ks[3], (E, F, D), dtype=jnp.float32) * (1.0 / math.sqrt(F))
        b2 = jnp.zeros((E, D), dtype=jnp.float32)
        return {'h': h, 'gate_w': gate_w, 'gate_b': gate_b, 'w1': w1, 'b1': b1, 'w2': w2, 'b2': b2}
    _L0_ffn_all = _L0_ffn_setup()
    _L0_ffn_in = {k: v for k, v in _L0_ffn_all.items() if k in ('gate_w', 'gate_b', 'w1', 'b1', 'w2', 'b2')}
    del _L0_ffn_all
    return {'x': x, 'src': src, 'dst': dst, 'L0_gnn_ln_w': _L0_gnn_in['ln_w'], 'L0_gnn_ln_b': _L0_gnn_in['ln_b'], 'L0_gnn_W1': _L0_gnn_in['W1'], 'L0_gnn_att_src1': _L0_gnn_in['att_src1'], 'L0_gnn_att_dst1': _L0_gnn_in['att_dst1'], 'L0_gnn_b1': _L0_gnn_in['b1'], 'L0_gnn_W2': _L0_gnn_in['W2'], 'L0_gnn_att_src2': _L0_gnn_in['att_src2'], 'L0_gnn_att_dst2': _L0_gnn_in['att_dst2'], 'L0_gnn_b2': _L0_gnn_in['b2'], 'L0_mix_t': _L0_mix_in['t'], 'L0_mix_w_qkv': _L0_mix_in['w_qkv'], 'L0_mix_mem_kv': _L0_mix_in['mem_kv'], 'L0_mix_w_out': _L0_mix_in['w_out'], 'L0_mix_b_out': _L0_mix_in['b_out'], 'L0_mix_g_out': _L0_mix_in['g_out'], 'L0_mix_g_pre': _L0_mix_in['g_pre'], 'L0_ffn_gate_w': _L0_ffn_in['gate_w'], 'L0_ffn_gate_b': _L0_ffn_in['gate_b'], 'L0_ffn_w1': _L0_ffn_in['w1'], 'L0_ffn_b1': _L0_ffn_in['b1'], 'L0_ffn_w2': _L0_ffn_in['w2'], 'L0_ffn_b2': _L0_ffn_in['b2']}

def reference(x, src, dst, L0_gnn_ln_w, L0_gnn_ln_b, L0_gnn_W1, L0_gnn_att_src1, L0_gnn_att_dst1, L0_gnn_b1, L0_gnn_W2, L0_gnn_att_src2, L0_gnn_att_dst2, L0_gnn_b2, L0_mix_t, L0_mix_w_qkv, L0_mix_mem_kv, L0_mix_w_out, L0_mix_b_out, L0_mix_g_out, L0_mix_g_pre, L0_ffn_gate_w, L0_ffn_gate_b, L0_ffn_w1, L0_ffn_b1, L0_ffn_w2, L0_ffn_b2):
    import jax
    import jax.numpy as jnp

    def _L0_gnn_ref(edge_index, x, ln_w, ln_b, W1, att_src1, att_dst1, b1, W2, att_src2, att_dst2, b2):
        import jax, jax.numpy as jnp
        import numpy as np
        N_ENT = 6250
        N_EDGE = 62500
        D = 256
        H1, C1 = (8, 64)
        NEG_SLOPE = 0.2
        LN_EPS = 1e-05

        def _gat_conv(x, edge_index, W, att_src, att_dst, bias, heads, out_ch, concat):
            n = x.shape[0]
            loops = jnp.arange(n)
            src = jnp.concatenate([edge_index[0], loops])
            dst = jnp.concatenate([edge_index[1], loops])
            h = (x @ W).reshape(n, heads, out_ch)
            a_src = jnp.sum(h * att_src[None], axis=-1)
            a_dst = jnp.sum(h * att_dst[None], axis=-1)
            e = jax.nn.leaky_relu(a_src[src] + a_dst[dst], NEG_SLOPE)
            m = jax.lax.stop_gradient(jax.ops.segment_max(e, dst, num_segments=n))
            p = jnp.exp(e - m[dst])
            denom = jax.ops.segment_sum(p, dst, num_segments=n)
            alpha = p / denom[dst]
            out = jax.ops.segment_sum(h[src] * alpha[..., None], dst, num_segments=n)
            out = out.reshape(n, heads * out_ch) if concat else out.mean(axis=1)
            return out + bias
        mu = jnp.mean(x, axis=-1, keepdims=True)
        var = jnp.var(x, axis=-1, keepdims=True)
        h = (x - mu) / jnp.sqrt(var + LN_EPS) * ln_w + ln_b
        h = jax.nn.elu(_gat_conv(h, edge_index, W1, att_src1, att_dst1, b1, H1, C1, True))
        return _gat_conv(h, edge_index, W2, att_src2, att_dst2, b2, 1, D, False)

    def _L0_mix_ref(x, t, w_qkv, mem_kv, w_out, b_out, g_out, g_pre):
        import jax, jax.numpy as jnp
        import numpy as np
        DIM = 256
        HEADS = 4
        DIM_HEAD = 32
        NUM_MEM = 4
        HIDDEN = HEADS * DIM_HEAD
        SCALE = DIM_HEAD ** (-0.5)

        def rmsnorm(x, g):
            n = jnp.linalg.norm(x, axis=-1, keepdims=True)
            return x / jnp.maximum(n, 1e-12) * g * x.shape[-1] ** 0.5
        b, n, c = x.shape
        xn = rmsnorm(x, g_pre)
        qkv = xn @ w_qkv
        q, k, v = jnp.split(qkv, 3, axis=-1)

        def to_heads(z):
            return z.reshape(b, n, HEADS, DIM_HEAD).transpose(0, 2, 3, 1)
        q, k, v = map(to_heads, (q, k, v))
        mk = jnp.broadcast_to(mem_kv[0], (b, HEADS, DIM_HEAD, NUM_MEM))
        mv = jnp.broadcast_to(mem_kv[1], (b, HEADS, DIM_HEAD, NUM_MEM))
        k = jnp.concatenate([mk, k], axis=-1)
        v = jnp.concatenate([mv, v], axis=-1)
        q = jax.nn.softmax(q, axis=-2) * SCALE
        k = jax.nn.softmax(k, axis=-1)
        context = jnp.einsum('bhdn,bhen->bhde', k, v)
        out = jnp.einsum('bhde,bhdn->bhen', context, q)
        out = out.transpose(0, 3, 1, 2).reshape(b, n, HIDDEN)
        out = rmsnorm(out @ w_out + b_out, g_out)
        return out + x

    def _L0_ffn_ref(h, gate_w, gate_b, w1, b1, w2, b2):
        import math
        import jax, jax.numpy as jnp
        import numpy as np
        CAPACITY_FACTOR = 1.25
        B, L, D = h.shape
        E = gate_w.shape[1]
        T = B * L
        C = max(1, math.ceil(CAPACITY_FACTOR * T / E))
        x = h.reshape(T, D)
        logits = x @ gate_w + gate_b
        probs = jax.nn.softmax(logits, axis=-1)
        idx = jnp.argmax(probs, axis=-1)
        prb = jnp.take_along_axis(probs, idx[:, None], axis=1)[:, 0]
        one_hot = jax.nn.one_hot(idx, E, dtype=jnp.float32)
        pos = (jnp.cumsum(one_hot, axis=0) * one_hot).sum(-1).astype(jnp.int32) - 1
        kept = pos < C
        pos_safe = jnp.where(kept, pos, C)
        buf = jnp.zeros((E, C, D), dtype=h.dtype).at[idx, pos_safe].set(x, mode='drop')
        hmid = jax.nn.relu(jnp.einsum('ecd,edf->ecf', buf, w1) + b1[:, None, :])
        ybuf = jnp.einsum('ecf,efd->ecd', hmid, w2) + b2[:, None, :]
        pos_g = jnp.minimum(pos, C - 1)
        y_tok = ybuf[idx, pos_g] * (prb * kept)[:, None]
        y = y_tok.reshape(B, L, D)
        y = jnp.nan_to_num(y, nan=0.0, posinf=10000.0, neginf=-10000.0)
        return y
    edge_index = jnp.stack([src, dst])
    xn = _layernorm(x, axis=-1)
    x = x + _L0_gnn_ref(edge_index, xn, L0_gnn_ln_w, L0_gnn_ln_b, L0_gnn_W1, L0_gnn_att_src1, L0_gnn_att_dst1, L0_gnn_b1, L0_gnn_W2, L0_gnn_att_src2, L0_gnn_att_dst2, L0_gnn_b2) + _L0_mix_ref(xn[None], L0_mix_t, L0_mix_w_qkv, L0_mix_mem_kv, L0_mix_w_out, L0_mix_b_out, L0_mix_g_out, L0_mix_g_pre)[0]
    x = x + _L0_ffn_ref(_layernorm(x, axis=-1)[None], L0_ffn_gate_w, L0_ffn_gate_b, L0_ffn_w1, L0_ffn_b1, L0_ffn_w2, L0_ffn_b2)[0]
    return x

_drawn_inputs = setup_inputs


def setup_inputs(seed=0):
    import zlib

    import numpy as np

    out = dict(_drawn_inputs(seed))
    spreads = {'L0_gnn_ln_w': (1.0, 0.6),
     'L0_gnn_ln_b': (0.0, 0.1),
     'L0_gnn_b1': (0.0, 0.1),
     'L0_gnn_b2': (0.0, 0.1),
     'L0_mix_b_out': (0.0, 0.1),
     'L0_mix_g_out': (1.0, 0.2),
     'L0_mix_g_pre': (1.0, 0.6),
     'L0_ffn_gate_b': (0.0, 0.1),
     'L0_ffn_b1': (0.0, 0.8),
     'L0_ffn_b2': (0.0, 0.8)}
    factors = {'L0_gnn_att_src1': 3.736,
     'L0_gnn_att_dst1': 8.0,
     'L0_gnn_att_src2': 8.0,
     'L0_gnn_att_dst2': 8.0,
     'L0_mix_w_qkv': 8.0,
     'L0_mix_mem_kv': 8.0,
     'L0_mix_w_out': 8.0}
    for name, (base, spread) in spreads.items():
        noise = np.random.default_rng([zlib.crc32(name.encode()), seed]).standard_normal(out[name].shape)
        drawn = base * np.exp(spread * noise) if base else spread * noise
        out[name] = jnp.asarray(drawn.astype(out[name].dtype))
    for name, factor in factors.items():
        out[name] = (out[name] * factor).astype(out[name].dtype)
    return out
```

```python
from contextlib import ExitStack

import concourse.bass as bass
from concourse import mybir

F32 = mybir.dt.float32
I32 = mybir.dt.int32
BF16 = mybir.dt.bfloat16
ALU = mybir.AluOpType
ACT = mybir.ActivationFunctionType
X = mybir.AxisListType.X
RMAX = bass.bass_isa.ReduceOp.max
IndexOn = bass.IndirectOffsetOnAxis

P = 128
N, D = 6250, 256
TILES = -(-N // P)
NP = TILES * P
LAST = N - (TILES - 1) * P
E = 106250
GROUP = 2 * P
GROUPS = -(-E // GROUP)
STEPS = GROUPS + TILES - 1
SLOTS = 2 * STEPS
KT = -(-STEPS // P)
H1, C1 = 8, 64
F1 = H1 * C1
HALF = 4 * C1 + 4
ROW1 = 2 * HALF
ROW2 = D + 2
SLOPE = 0.2
EPS = 1e-5
SPREAD = 60.0
BIG = 2.0 ** 100
MH, MD, MEM = 4, 32, 4
QK = MH * MD
KCH = -(-N // 512)
EXPERTS, FF = 8, 1024
CAP = -(-5 * N // (4 * EXPERTS))
CT = -(-CAP // P)


def tiles(eng, first, last, unroll):
    whole = (last - first) // unroll
    if whole > 1:
        with eng.Fori(0, whole) as i:
            for u in range(unroll):
                yield i * unroll + (first + u), (first + u) % unroll
    else:
        whole = 0
    for s in range(first + whole * unroll, last):
        yield s, s % unroll


def turns(eng, first, last, ring):
    whole = (last - first) // ring
    with eng.Fori(0, whole) as i:
        for u in range(ring):
            yield i * ring + (first + u), (first + u) % ring, i + (first + u) // ring
    for s in range(first + whole * ring, last):
        yield s, s % ring, s // ring


def ring4(eng):
    yield from ((t, t) for t in range(4))
    yield from tiles(eng, 4, TILES, 4)


class Chain:

    def __init__(self, eng, sem):
        self.eng, self.sem, self.base, self.n = eng, sem, 0, 0

    def at(self, base):
        self.base, self.n = base, 0

    def link(self, ins):
        self.n += 1
        ins.then_inc(self.sem, 1)
        self.eng.wait_ge(self.sem, self.base + self.n)

    def closed(self, per_step):
        assert self.n == per_step, self.n


def one(ap, axis, n):
    shape = list(ap.shape)
    shape.insert(axis, n)
    return ap.unsqueeze(axis).to_broadcast(shape)


def gps_program(nc, x, src, dst, ln_w, ln_b, W1, att_s1, att_d1, b1, W2, att_s2, att_d2, b2,
                w_qkv, mem_kv, w_out, b_out, g_out, g_pre,
                gate_w, gate_b, ew1, eb1, ew2, eb2, out):
    root = ExitStack()
    with root:
        def dram(name, shape):
            return nc.dram_tensor(name, shape, F32).ap()

        table1 = dram("table1", [NP, ROW1])
        table2 = dram("table2", [NP, ROW2])
        resid = dram("resid", [NP, D])
        xbuf = dram("xbuf", [EXPERTS * CT * P, D])
        ybuf = dram("ybuf", [EXPERTS * CAP, D])

        taken = []

        def recycle():
            nc.all_engine_barrier()
            nc.clear_and_free_semaphores(taken)
            taken.clear()
            nc.all_engine_barrier()

        def allocator(stack):
            def sb(name, shape, dt=F32):
                return stack.enter_context(nc.sbuf_tensor(name, shape, dt))

            def sem(name):
                taken.append(nc.alloc_semaphore(name=name))
                return taken[-1]
            return sb, sem

        sb, sem = allocator(root)
        PS = root.enter_context(nc.psum_tensor("PS", [P, 8, 512], F32))
        ident = sb("ident", [P, P])
        iota_row = sb("iota_row", [P, P])
        ones = sb("ones", [P, P])
        mean = sb("mean", [P, TILES])
        rstd = sb("rstd", [P, TILES])
        SRC = sb("SRC", [P, SLOTS], I32)
        DST = sb("DST", [P, SLOTS])
        TK = sb("TK", [1, KT * P], I32)
        AD1 = sb("AD1", [P, TILES, 16])
        AD2 = sb("AD2", [P, TILES, 2])
        dev = locals()

        edge_tables(nc, allocator, dev)
        node_phase(nc, allocator, dev)
        with ExitStack() as mid:
            sb1, _ = allocator(mid)
            ADM = sb1("ADM1", [P, TILES, 2 * H1])
            SELF = sb1("SELF1", [P, TILES, H1])
            bounds(nc, allocator, dev, LAYER1, table1, AD1, ADM, SELF)
            ACC = sb1("ACC1", [P, TILES, ROW1])
            walk(nc, allocator, dev, LAYER1, table1, ADM, ACC)
            between(nc, allocator, dev, ACC, SELF, AD2)
        X1 = sb("X1", [P, TILES, D])
        bn1 = sb("bn1", [P, TILES, 6])
        with ExitStack() as mid:
            sb2, _ = allocator(mid)
            ADM = sb2("ADM2", [P, TILES, 2])
            SELF = sb2("SELF2", [P, TILES, 1])
            bounds(nc, allocator, dev, LAYER2, table2, AD2, ADM, SELF)
            ACC = sb2("ACC2", [P, TILES, D + 1])
            walk(nc, allocator, dev, LAYER2, table2, ADM, ACC)
            residual(nc, allocator, dev, ACC, SELF, X1, bn1)
        recycle()
        m1 = sb("m1", [P, TILES])
        r1 = sb("r1_", [P, TILES])
        weight = sb("weight", [P, TILES])
        put = sb("put", [P, TILES], I32)
        take = sb("take", [P, TILES], I32)
        with ExitStack() as mid:
            LG = allocator(mid)[0]("LG", [P, TILES, EXPERTS])
            gate(nc, allocator, dev, X1, bn1, m1, r1, LG)
            route(nc, allocator, dev, LG, weight, put, take)
        dispatch(nc, allocator, dev, X1, m1, r1, put)
        experts(nc, allocator, dev)
        combine(nc, allocator, dev, X1, weight, take)
        return dev


def edge_tables(nc, allocator, dev):
    PS, ident, iota_row, ones, SRC, DST, TK = (dev[k] for k in (
        "PS", "ident", "iota_row", "ones", "SRC", "DST", "TK"))
    src, dst = dev["src"], dev["dst"]
    with ExitStack() as st:
        sb, sem = allocator(st)
        last_i = sb("last_i", [1, GROUPS], I32)
        tile_i = sb("tile_i", [1, GROUPS], I32)
        tile_f = sb("tile_f", [1, GROUPS])
        grp = sb("grp", [P, GROUPS])
        leave = sb("leave", [P, GROUPS])
        junk = sb("junk", [P, GROUPS])
        step_f = sb("step_f", [P, KT])
        c_f = sb("c_f", [P, KT])
        c_i = sb("c_i", [P, KT], I32)
        t_f = sb("t_f", [P, KT])
        first_f = sb("first_f", [P, KT])
        SE = sb("SE", [P, KT, GROUP], I32)
        DE = sb("DE", [P, KT, GROUP], I32)
        SF = sb("SF", [P, KT, GROUP])
        DF = sb("DF", [P, KT, GROUP])
        ends_loaded = sem("ends_loaded")
        zeroed, consts = sem("zeroed"), sem("consts")
        own = sem("edge_vector_own")
        tiles_ready, tiles_spread = sem("tiles_ready"), sem("tiles_spread")
        groups_ready, edges_in, edges_float = sem("groups_ready"), sem("edges_in"), sem("edges_float")
        turned, copied = sem("turned"), sem("turned_copied")

        block = st.enter_context(nc.Block())

        @block.sync
        def _(sp):
            with nc.allow_non_contiguous_dma(reason="one destination per group"):
                sp.dma_start(last_i[:, :], dst[:, GROUP - 1:GROUP].rearrange("g a -> a g")).then_inc(ends_loaded, 16)

        @block.gpsimd
        def _(pool):
            pool.memset(ident[:, :], 0.0).then_inc(zeroed, 1)
            pool.memset(ones[:, :], 1.0).then_inc(consts, 1)
            pool.iota(iota_row[:, :], [[1, P]], base=0, channel_multiplier=0,
                      allow_small_or_imprecise_dtypes=True).then_inc(consts, 1)
            pool.iota(grp[:, :], [[1, GROUPS]], base=0, channel_multiplier=0,
                      allow_small_or_imprecise_dtypes=True).then_inc(consts, 1)
            pool.iota(step_f[:, :], [[P, KT]], base=0, channel_multiplier=1,
                      allow_small_or_imprecise_dtypes=True).then_inc(consts, 1)
            pool.wait_ge(zeroed, 1)
            pool.affine_select(out=ident[:, :], in_=ident[:, :], compare_op=ALU.not_equal, fill=1.0,
                               base=0, pattern=[[-1, P]], channel_multiplier=1).then_inc(consts, 1)
            pool.wait_ge(groups_ready, 1)
            for k in range(KT):
                pool.indirect_dma_start(SE[:, k, :], None, src, IndexOn(ap=c_i[:, k:k + 1], axis=0)).then_inc(edges_in, 16)
                pool.indirect_dma_start(DE[:, k, :], None, dst, IndexOn(ap=c_i[:, k:k + 1], axis=0)).then_inc(edges_in, 16)

        @block.vector
        def _(dve):
            own_ = Chain(dve, own)
            dve.wait_ge(ends_loaded, 16)
            own_.link(dve.tensor_scalar(tile_i[:, :], last_i[:, :], 7, None, ALU.arith_shift_right))
            dve.tensor_copy(tile_f[:, :], tile_i[:, :]).then_inc(tiles_ready, 1)
            dve.wait_ge(tiles_spread, 1)
            dve.wait_ge(consts, 5)
            own_.link(dve.tensor_tensor(leave[:, :], PS[:, 0, 0:GROUPS], grp[:, :], ALU.add))
            for k in range(KT):
                own_.link(dve.tensor_scalar(junk[:, :], leave[:, :], step_f[:, k:k + 1], None, ALU.is_lt,
                                            ALU.add, accum_out=c_f[:, k:k + 1]))
            own_.link(dve.tensor_scalar(c_f[:, :], c_f[:, :], float(GROUPS - 1), None, ALU.min))
            own_.link(dve.tensor_tensor(t_f[:, :], step_f[:, :], c_f[:, :], ALU.subtract))
            own_.link(dve.tensor_scalar(t_f[:, :], t_f[:, :], float(TILES - 1), None, ALU.min))
            own_.link(dve.tensor_scalar(first_f[:, :], t_f[:, :], float(P), None, ALU.mult))
            dve.tensor_copy(c_i[:, :], c_f[:, :]).then_inc(groups_ready, 1)
            dve.wait_ge(edges_in, 32 * KT)
            own_.link(dve.tensor_copy(SF[:, :, :], SE[:, :, :]))
            own_.link(dve.tensor_copy(DF[:, :, :], DE[:, :, :]))
            for k in range(KT):
                own_.link(dve.tensor_scalar(DF[:, k, :], DF[:, k, :], first_f[:, k:k + 1], None, ALU.subtract))
            dve.engine_nop().then_inc(edges_float, 1)
            for k in range(KT):
                n = min(P, STEPS - k * P)
                dve.wait_ge(turned, k + 1)
                part = slice(2 * k * P, 2 * (k * P + n))
                dve.tensor_copy(SRC[:, part].rearrange("p (k h) -> p h k", h=2), PS[:, k % 2, 0:256].rearrange("p (h k) -> p h k", h=2)[:, :, 0:n])
                dve.tensor_copy(DST[:, part].rearrange("p (k h) -> p h k", h=2), PS[:, k % 2, 256:512].rearrange("p (h k) -> p h k", h=2)[:, :, 0:n]).then_inc(copied, 1)
            dve.wait_ge(turned, KT + 1)
            dve.tensor_copy(TK[:, :], PS[0:1, 2, 0:KT * P])

        @block.tensor
        def _(pe):
            pe.wait_ge(consts, 5)
            pe.wait_ge(tiles_ready, 1)
            pe.matmul(PS[:, 0, 0:GROUPS], ones[0:1, :], tile_f[:, :], start=True, stop=True).then_inc(tiles_spread, 1)
            pe.wait_ge(edges_float, 1)
            for k in range(KT):
                if k >= 2:
                    pe.wait_ge(copied, k - 1)
                for j, half in ((0, SF[:, k, 0:P]), (1, SF[:, k, P:GROUP]), (2, DF[:, k, 0:P]), (3, DF[:, k, P:GROUP])):
                    last = pe.transpose(PS[:, k % 2, j * P:(j + 1) * P], half, ident[:, :])
                last.then_inc(turned, 1)
            for k in range(KT):
                last = pe.transpose(PS[0:1, 2, k * P:(k + 1) * P], t_f[:, k:k + 1], ident[:, :])
            last.then_inc(turned, 1)


def node_phase(nc, allocator, dev):
    PS, ident, ones, mean, rstd, AD1 = (dev[k] for k in ("PS", "ident", "ones", "mean", "rstd", "AD1"))
    with ExitStack() as outer:
        sb, _ = allocator(outer)
        xt = sb("xt", [P, TILES, D])
        QT = sb("QT", [P, NP])
        V = sb("V", [P, TILES, QK])
        KE = sb("KE", [P, N + MEM])
        with ExitStack() as inner:
            sb, _ = allocator(inner)
            WA = sb("WA", [P, 2, ROW1 + 16])
            WQ = sb("WQ", [P, 2, 3 * QK])
            BA = sb("BA", [P, ROW1 + 16])
            unit = sb("unit", [P, TILES])
            back = sb("back", [P, TILES])
            fold_weights(nc, allocator, dev, WA, WQ, BA, KE, V, xt)
            normalise(nc, allocator, dev, xt, unit, back)
            project(nc, allocator, dev, xt, WA, WQ, BA, unit, back, QT, V, KE)
        mixer(nc, allocator, dev, xt, QT, V, KE)


def fold_weights(nc, allocator, dev, WA, WQ, BA, KE, V, xt):
    PS, ones = dev["PS"], dev["ones"]
    W1, w_qkv, mem_kv, x = dev["W1"], dev["w_qkv"], dev["mem_kv"], dev["x"]
    with ExitStack() as st:
        sb, sem = allocator(st)
        att = sb("att", [P, 2, F1])
        lw = sb("lw", [P, 2])
        lb = sb("lb", [P, 2])
        gp = sb("gp", [P, 2])
        prod = sb("prod", [P, 2, F1])
        lbw = sb("lbw", [P, 2, P])
        w1_in, rest_in, x_in = sem("w1_in"), sem("rest_in"), sem("x_in")
        own, bias_cols, bias_done = sem("fold_own"), sem("bias_cols"), sem("bias_done")
        block = st.enter_context(nc.Block())

        @block.sync
        def _(sp):
            with nc.allow_non_contiguous_dma(reason="small vectors"):
                for k in range(2):
                    for a in range(2):
                        sp.dma_start(WA[:, k, a * HALF:a * HALF + 256],
                                     W1[k * P:(k + 1) * P, a * 256:(a + 1) * 256]).then_inc(w1_in, 16)
                for j, v in enumerate((dev["att_s1"], dev["att_d1"])):
                    sp.dma_start(att[:, j, :], v.rearrange("h c -> (h c)").partition_broadcast(P)).then_inc(w1_in, 16)
                for tile, v in ((lw, dev["ln_w"]), (lb, dev["ln_b"]), (gp, dev["g_pre"])):
                    sp.dma_start(tile[:, :], v.rearrange("(k p) -> p k", p=P)).then_inc(rest_in, 16)
                sp.dma_start(WQ[:, :, :], w_qkv.rearrange("(k p) n -> p k n", p=P)).then_inc(rest_in, 16)
                sp.dma_start(KE[:, N:N + MEM], mem_kv[0].rearrange("h d m -> (h d) m")).then_inc(rest_in, 16)
                for h in range(MH):
                    sp.dma_start(V[LAST:LAST + MEM, TILES - 1, h * MD:(h + 1) * MD],
                                 mem_kv[1, h].rearrange("d m -> m d")).then_inc(rest_in, 16)
            for c in range(6):
                sp.dma_start(xt[:, 8 * c:8 * (c + 1), :],
                             x[8 * c * P:8 * (c + 1) * P, :].rearrange("(t p) n -> p t n", p=P)).then_inc(x_in, 16)
            sp.wait_ge(own, 1)
            sp.dma_start(xt[0:LAST, TILES - 1, :], x[(TILES - 1) * P:N, :]).then_inc(x_in, 16)
            sp.wait_ge(x_in, 7 * 16)
            sp.wait_ge(rest_in, 9 * 16)

        @block.vector
        def _(dve):
            own_ = Chain(dve, own)
            own_.link(dve.memset(xt[:, TILES - 1, :], 0.0))
            dve.wait_ge(w1_in, 6 * 16)
            cols = [WA[:, k, 0:ROW1].rearrange("p (a b) -> p a b", a=2) for k in range(2)]
            for k in range(2):
                for j in range(2):
                    own_.link(dve.tensor_tensor(prod[:, j, :].rearrange("p (a b) -> p a b", a=2), cols[k][:, :, 0:256],
                                                att[:, j, :].rearrange("p (a b) -> p a b", a=2), ALU.mult))
                    own_.link(dve.tensor_reduce(WA[:, k, ROW1 + 8 * j:ROW1 + 8 * j + 8],
                                                prod[:, j, :].rearrange("p (h c) -> p h c", c=C1), X, ALU.add))
                own_.link(dve.tensor_copy(cols[k][:, :, 256:260], WA[:, k, ROW1:ROW1 + 8].rearrange("p (a b) -> p a b", a=2)))
            dve.wait_ge(rest_in, 9 * 16)
            for k in range(2):
                own_.link(dve.tensor_scalar(lbw[:, k, :], ones[:, :], lb[:, k:k + 1], None, ALU.mult))
            dve.engine_nop().then_inc(bias_cols, 1)
            dve.wait_ge(bias_done, 1)
            half = (ROW1 + 16) // 2
            for a in range(2):
                own_.link(dve.tensor_copy(BA[:, a * half:(a + 1) * half], PS[:, a, 0:half]))
            for k in range(2):
                own_.link(dve.tensor_scalar(WA[:, k, :], WA[:, k, :], lw[:, k:k + 1], None, ALU.mult))
                own_.link(dve.tensor_scalar(WQ[:, k, :], WQ[:, k, :], gp[:, k:k + 1], None, ALU.mult))

        @block.tensor
        def _(pe):
            half = (ROW1 + 16) // 2
            pe.wait_ge(bias_cols, 1)
            for a in range(2):
                for k in range(2):
                    last = pe.matmul(PS[:, a, 0:half], lbw[:, k, :], WA[:, k, a * half:(a + 1) * half],
                                     start=k == 0, stop=k == 1)
            last.then_inc(bias_done, 1)


def normalise(nc, allocator, dev, xt, unit, back):
    PS, ident, mean, rstd = dev["PS"], dev["ident"], dev["mean"], dev["rstd"]
    with ExitStack() as st:
        sb, sem = allocator(st)
        bn = sb("bn", [P, TILES, 6])
        va = sb("va", [P, TILES])
        v2 = sb("v2", [P, TILES])
        ta = sb("ta", [P, TILES])
        tb = sb("tb", [P, TILES])
        own, to_root, rooted = sem("norm_own"), sem("to_root"), sem("rooted")
        block = st.enter_context(nc.Block())

        @block.vector
        def _(dve):
            own_ = Chain(dve, own)
            for t, u in tiles(dve, 0, TILES, 4):
                last = dve.bn_stats(bn[:, bass.ds(t, 1), :].rearrange("p a b -> p (a b)"),
                                    xt[:, bass.ds(t, 1), :].rearrange("p a b -> p (a b)"))
            own_.link(last)
            moments(dve, own_, bn, mean, va, ta)
            own_.link(dve.tensor_scalar(ta[:, :], va[:, :], EPS, None, ALU.add))
            dve.engine_nop().then_inc(to_root, 1)
            dve.wait_ge(rooted, 1)
            own_.link(dve.reciprocal(rstd[:, :], ta[:, :]))
            own_.link(dve.tensor_tensor(v2[:, :], rstd[:, :], rstd[:, :], ALU.mult))
            own_.link(dve.tensor_tensor(v2[:, :], v2[:, :], va[:, :], ALU.mult))
            own_.link(dve.tensor_scalar(ta[:, :], v2[:, :], EPS, None, ALU.add))
            own_.link(dve.tensor_scalar(tb[:, :], v2[:, :], float(D), None, ALU.mult))
            dve.engine_nop().then_inc(to_root, 1)
            dve.wait_ge(rooted, 3)
            own_.link(dve.tensor_scalar(tb[:, :], tb[:, :], 1e-12, 1.0 / 16.0, ALU.max, ALU.mult))
            own_.link(dve.reciprocal(unit[:, :], tb[:, :]))
            own_.link(dve.tensor_tensor(unit[:, :], unit[:, :], rstd[:, :], ALU.mult))
            own_.link(dve.reciprocal(ta[:, :], ta[:, :]))
            own_.link(dve.tensor_tensor(back[:, :], tb[:, :], ta[:, :], ALU.mult))

        @block.scalar
        def _(act):
            act.wait_ge(to_root, 1)
            act.activation(ta[:, :], ta[:, :], ACT.Sqrt).then_inc(rooted, 1)
            act.wait_ge(to_root, 2)
            act.activation(ta[:, :], ta[:, :], ACT.Sqrt).then_inc(rooted, 1)
            act.activation(tb[:, :], tb[:, :], ACT.Sqrt).then_inc(rooted, 1)


def moments(dve, own_, bn, mean, va, ta):
    me, mo, ve, vo = bn[:, :, 1], bn[:, :, 4], bn[:, :, 2], bn[:, :, 5]
    own_.link(dve.tensor_tensor(mean[:, :], me, mo, ALU.add))
    own_.link(dve.tensor_scalar(mean[:, :], mean[:, :], 0.5, None, ALU.mult))
    own_.link(dve.tensor_tensor(ta[:, :], me, mo, ALU.subtract))
    own_.link(dve.tensor_tensor(ta[:, :], ta[:, :], ta[:, :], ALU.mult))
    own_.link(dve.tensor_tensor(va[:, :], ve, vo, ALU.add))
    own_.link(dve.tensor_scalar(va[:, :], va[:, :], 1.0 / D, None, ALU.mult))
    own_.link(dve.tensor_scalar(ta[:, :], ta[:, :], 0.25, None, ALU.mult))
    own_.link(dve.tensor_tensor(va[:, :], va[:, :], ta[:, :], ALU.add))


def project(nc, allocator, dev, xt, WA, WQ, BA, unit, back, QT, V, KE):
    PS, ident, AD1, table1, mean = (dev[k] for k in ("PS", "ident", "AD1", "table1", "mean"))
    with ExitStack() as st:
        sb, sem = allocator(st)
        Y = sb("Y", [P, 2, D])
        YT = sb("YT", [P, 2, 2, P])
        row = sb("row", [P, 2, ROW1])
        q = sb("q", [P, 2, QK])
        qm = sb("qm", [P, 2, MH])
        qs = sb("qs", [P, 2, MH])
        y_ready, y_turned, y_copied = sem("y_ready"), sem("y_turned"), sem("y_copied")
        tile_done = sem("tile_done")
        rows_ready = sem("rows_ready")
        rows_stored = [sem(f"rows_stored{u}") for u in range(2)]
        max_own, norm_own = sem("qmax_own"), sem("qnorm_own")
        q_ready, q_exp, q_normed = sem("q_ready"), sem("q_exp"), sem("q_normed")
        vk_copied, q_turned, q_copied = sem("vk_copied"), sem("q_turned"), sem("q_copied")
        block = st.enter_context(nc.Block())

        @block.tensor
        def _(pe):
            def turn_y(t, u):
                pe.wait_ge(y_ready, t + 1)
                pe.wait_ge(y_copied, t + 1)
                for k in range(2):
                    last = pe.transpose(PS[:, 6, k * P:(k + 1) * P], Y[:, u, k * P:(k + 1) * P], ident[:, :])
                last.then_inc(y_turned, 1)

            def tile(t, u):
                pe.wait_ge(y_copied, t + 2)
                pe.wait_ge(q_ready, t + 1)
                pe.wait_ge(vk_copied, t + 1)
                for k in range(2):
                    pe.matmul(PS[:, 3 * u, 0:HALF], YT[:, u, k, :], WA[:, k, 0:HALF], start=k == 0, stop=k == 1)
                for k in range(2):
                    pe.matmul(PS[:, 3 * u + 1, 0:HALF + 16], YT[:, u, k, :], WA[:, k, HALF:ROW1 + 16], start=k == 0, stop=k == 1)
                for k in range(2):
                    pe.matmul(PS[:, 3 * u + 2, 0:2 * QK].rearrange("p (a b) -> p a b", b=QK), YT[:, u, k, :],
                              WQ[:, k, :].rearrange("p (a b) -> p a b", b=QK)[:, 0:3:2, :], start=k == 0, stop=k == 1)
                for k in range(2):
                    last = pe.matmul(PS[:, 3 * u + 2, 2 * QK:2 * QK + P], WQ[:, k, QK:2 * QK], YT[:, u, k, :],
                                     start=k == 0, stop=k == 1)
                last.then_inc(tile_done, 1)

            def turn_q(t, u):
                pe.wait_ge(q_normed, t + 1)
                pe.wait_ge(q_copied, t + 1)
                pe.transpose(PS[:, 7, 0:P], q[:, u, :], ident[:, :]).then_inc(q_turned, 1)

            for free in (q_ready, vk_copied):
                pe.sem_inc(free, 2)
            for free in (y_copied, q_copied):
                pe.sem_inc(free, 1)
            turn_y(0, 0)
            for t in range(2):
                turn_y(t + 1, 1 - t)
                tile(t, t)
            for t, u in tiles(pe, 2, TILES - 1, 2):
                turn_y(t + 1, 1 - u)
                tile(t, u)
                turn_q(t - 2, u)
            t = TILES - 1
            tile(t, t % 2)
            for t in (TILES - 3, TILES - 2, TILES - 1):
                turn_q(t, t % 2)

        @block.vector
        def _(dve):
            mx, nm = Chain(dve, max_own), Chain(dve, norm_own)

            def rms(t, u):
                dve.wait_ge(y_turned, t + 1)
                dve.tensor_scalar(Y[:, u, :], xt[:, bass.ds(t, 1), :].rearrange("p a b -> p (a b)"),
                                  mean[:, bass.ds(t, 1)], unit[:, bass.ds(t, 1)], ALU.subtract, ALU.mult).then_inc(y_ready, 1)

            def first(t, u):
                mx.at(t)
                dve.wait_ge(tile_done, t + 1)
                dve.wait_ge(rows_stored[u], rounds(t, u))
                g = back[:, bass.ds(t, 1)]
                dve.scalar_tensor_tensor(row[:, u, :].rearrange("p (a b) -> p a b", a=2), PS[:, 3 * u:3 * u + 2, 0:HALF], g,
                                         BA[:, 0:ROW1].rearrange("p (a b) -> p a b", a=2), ALU.mult, ALU.add).then_inc(rows_ready, 1)
                dve.scalar_tensor_tensor(AD1[:, bass.ds(t, 1), :].rearrange("p a b -> p (a b)"), PS[:, 3 * u + 1, HALF:HALF + 16], g,
                                         BA[:, ROW1:ROW1 + 16], ALU.mult, ALU.add)
                qq = PS[:, 3 * u + 2, 0:QK].rearrange("p (h d) -> p h d", h=MH)
                mx.link(dve.tensor_reduce(qm[:, u, :], qq, X, ALU.max))
                dve.wait_ge(q_turned, t + 1)
                dve.tensor_tensor(q[:, u, :].rearrange("p (h d) -> p h d", h=MH), qq, one(qm[:, u, :], 2, MD),
                                  ALU.subtract).then_inc(q_ready, 1)

            def second(t, u):
                nm.at(t * 2)
                qv = q[:, u, :].rearrange("p (h d) -> p h d", h=MH)
                dve.wait_ge(q_exp, t + 1)
                nm.link(dve.tensor_reduce(qs[:, u, :], qv, X, ALU.add))
                nm.link(dve.reciprocal(qs[:, u, :], qs[:, u, :]))
                dve.tensor_tensor(qv, qv, one(qs[:, u, :], 2, MD), ALU.mult).then_inc(q_normed, 1)

            for free in (y_turned, q_turned):
                dve.sem_inc(free, 2)
            rms(0, 0)
            rms(1, 1)
            first(0, 0)
            for t, u in tiles(dve, 1, TILES - 1, 2):
                rms(t + 1, 1 - u)
                first(t, u)
                second(t - 1, 1 - u)
            t = TILES - 1
            first(t, t % 2)
            second(t - 1, 1 - t % 2)
            second(t, t % 2)

        @block.scalar
        def _(act):
            def copy_y(t, u):
                act.wait_ge(y_turned, t + 3)
                if not isinstance(t, int) or t > 1:
                    act.wait_ge(tile_done, t - 1)
                act.activation(YT[:, u, :, :], PS[:, 6, 0:2 * P].rearrange("p (k q) -> p k q", k=2), ACT.Copy).then_inc(y_copied, 1)

            def first(t, u, rows=P):
                act.wait_ge(q_ready, t + 3)
                act.activation(q[:, u, :], q[:, u, :], ACT.Exp).then_inc(q_exp, 1)
                act.activation(KE[:, bass.ds(t * P, rows)], PS[:, 3 * u + 2, 2 * QK:2 * QK + rows], ACT.Copy)
                act.activation(V[0:rows, bass.ds(t, 1), :].rearrange("p a b -> p (a b)"), PS[0:rows, 3 * u + 2, QK:2 * QK],
                               ACT.Copy).then_inc(vk_copied, 1)

            def second(t, u):
                act.wait_ge(q_turned, t + 3)
                act.activation(QT[:, bass.ds(t * P, P)], PS[:, 7, 0:P], ACT.Copy).then_inc(q_copied, 1)

            copy_y(0, 0)
            for t in range(2):
                copy_y(t + 1, 1 - t)
                first(t, t)
            for t, u in tiles(act, 2, TILES - 1, 2):
                copy_y(t + 1, 1 - u)
                first(t, u)
                second(t - 2, u)
            t = TILES - 1
            first(t, t % 2, LAST)
            for t in (TILES - 3, TILES - 2, TILES - 1):
                second(t, t % 2)

        @block.sync
        def _(sp):
            for u in range(2):
                sp.sem_inc(rows_stored[u], 16)
            for t, u in tiles(sp, 0, TILES, 2):
                sp.wait_ge(rows_ready, t + 1)
                sp.dma_start(table1[bass.ds(t * P, P), :], row[:, u, :]).then_inc(rows_stored[u], 16)
            for u in range(2):
                sp.wait_ge(rows_stored[u], 16 + 16 * len(range(u, TILES, 2)))


def rounds(t, u, ring=2):
    return 16 * ((t - u) // ring) + 16 if isinstance(t, int) else (t - u) * (16 // ring) + 16


def mixer(nc, allocator, dev, xt, QT, V, KE):
    PS, ident, mean, rstd, resid = (dev[k] for k in ("PS", "ident", "mean", "rstd", "resid"))
    with ExitStack() as st:
        sb, sem = allocator(st)
        O = sb("O", [P, TILES, D])
        EK = sb("EK", [P, 2, 4, QK])
        nkm = sb("nkm", [P, 1])
        ks = sb("ks", [P, 1])
        kg = sb("kg", [P, TILES // 4 + 1])
        KX = sb("KX", [P, 2, 512])
        QX = sb("QX", [P, 2, 512])
        mask = sb("mask", [P, P])
        ctx = sb("ctx", [P, P])
        WO = sb("WO", [P, D])
        CW = sb("CW", [P, D])
        bo, go, bb2 = (sb(n, [P, D]) for n in ("bo", "go", "bb2"))
        sq = sb("sq", [P, 2, D])
        ss = sb("ss", [P, TILES])
        r1 = sb("r1", [P, TILES])
        nmr = sb("nmr", [P, TILES])
        loaded, own, max_ready, exped = sem("mix_loaded"), sem("mix_own"), sem("kmax_ready"), sem("keys_exped")
        k_turned, k_copied, ctx_done = sem("k_turned"), sem("k_copied"), sem("ctx_done")
        ctx_ready, cw_done, cw_ready = sem("ctx_ready"), sem("cw_done"), sem("cw_ready")
        o_done, o_ready, squared = sem("o_done"), sem("o_ready"), sem("squared")
        norm_in, rooted, x_ready, r_ready, stored = sem("norm_in"), sem("rooted2"), sem("x_ready"), sem("r_ready"), sem("r_stored")
        scales, k_used, q_staged = sem("scales"), sem("k_used"), sem("q_staged")
        o_own = sem("o_own")
        block = st.enter_context(nc.Block())
        GRP = TILES // 4

        @block.sync
        def _(sp):
            sp.dma_start(WO[:, :], dev["w_out"]).then_inc(loaded, 16)
            for tile, v in ((bo, "b_out"), (go, "g_out"), (bb2, "b2")):
                sp.dma_start(tile[:, :], dev[v].partition_broadcast(P)).then_inc(loaded, 16)
            for c, _ in tiles(sp, 0, 7, 1):
                sp.wait_ge(r_ready, c * 7 + 7)
                sp.dma_start(resid[bass.ds(c * 7 * P, 7 * P), :].rearrange("(t p) n -> p t n", p=P),
                             xt[:, bass.ds(c * 7, 7), :]).then_inc(stored, 16)
            sp.wait_ge(stored, 7 * 16)

        @block.vector
        def _(dve):
            own_ = Chain(dve, own)
            own_.link(dve.tensor_reduce(nkm[:, :], KE[:, :], X, ALU.max, negate=True))
            dve.engine_nop().then_inc(max_ready, 1)
            own_.link(dve.memset(mask[:, :], 0.0))
            for h in range(MH):
                own_.link(dve.memset(mask[h * MD:(h + 1) * MD, h * MD:(h + 1) * MD], 1.0))
            own_.link(dve.tensor_scalar(r1[:, :], rstd[:, :], 1.0, None, ALU.add))
            own_.link(dve.tensor_tensor(nmr[:, :], mean[:, :], rstd[:, :], ALU.mult))
            own_.link(dve.tensor_scalar(nmr[:, :], nmr[:, :], -1.0, None, ALU.mult))
            dve.engine_nop().then_inc(scales, 1)
            dve.wait_ge(exped, GRP + 1)
            own_.link(dve.tensor_reduce(ks[:, :], kg[:, :], X, ALU.add))
            own_.link(dve.reciprocal(ks[:, :], ks[:, :]))
            dve.wait_ge(loaded, 4 * 16)
            own_.link(dve.tensor_scalar(go[:, :], go[:, :], 16.0, None, ALU.mult))
            dve.wait_ge(ctx_done, 1)
            dve.tensor_tensor(ctx[:, :], PS[:, 2, 0:P], mask[:, :], ALU.mult).then_inc(ctx_ready, 1)
            dve.wait_ge(ctx_done, 2)
            dve.tensor_copy(ctx[:, :], PS[:, 3, 0:P]).then_inc(ctx_ready, 1)
            dve.wait_ge(cw_done, 1)
            dve.tensor_scalar(CW[:, :], PS[:, 2, 0:D], ks[:, :], MD ** -0.5, ALU.mult, ALU.mult).then_inc(cw_ready, 1)
            for t, u in tiles(dve, 0, TILES, 2):
                dve.wait_ge(o_done, t + 1)
                dve.tensor_tensor(O[:, bass.ds(t, 1), :].rearrange("p a b -> p (a b)"), PS[:, 4 + u, 0:D], bo[:, :],
                                  ALU.add).then_inc(o_ready, 1)
            dve.wait_ge(squared, TILES + 3)
            own_.link(dve.tensor_scalar(ss[:, :], ss[:, :], 1e-12, None, ALU.max))
            own_.link(dve.reciprocal(ss[:, :], ss[:, :]))
            oo_ = Chain(dve, o_own)
            for t, u in tiles(dve, 0, TILES, 2):
                oo_.at(t * 2)
                o = O[:, bass.ds(t, 1), :].rearrange("p a b -> p (a b)")
                r = xt[:, bass.ds(t, 1), :].rearrange("p a b -> p (a b)")
                oo_.link(dve.scalar_tensor_tensor(o, o, ss[:, bass.ds(t, 1)], go[:, :], ALU.mult, ALU.mult))
                dve.wait_ge(x_ready, t + 1)
                oo_.link(dve.tensor_tensor(r, r, o, ALU.add))
                dve.tensor_tensor(r, r, bb2[:, :], ALU.add).then_inc(r_ready, 1)

        @block.scalar
        def _(act):
            act.wait_ge(max_ready, 1)

            def exps(g, u, n=512):
                if not isinstance(g, int) or g > 1:
                    act.wait_ge(k_turned, g - 1)
                act.activation(KX[:, u, 0:n], KE[:, bass.ds(g * 512, n)], ACT.Exp, bias=nkm[:, :],
                               accum_out=kg[:, bass.ds(g, 1)]).then_inc(exped, 1)

            def copy(g, u, rows=P, n=4):
                act.wait_ge(k_turned, g + 1)
                if not isinstance(g, int) or g > 1:
                    act.wait_ge(k_used, g - 1)
                act.activation(EK[0:rows, u, 0:n, :], PS[0:rows, u, 0:n * P].rearrange("p (j c) -> p j c", j=n), ACT.Copy).then_inc(k_copied, 1)

            exps(0, 0)
            exps(1, 1)
            copy(0, 0)
            for g, u in tiles(act, 2, GRP, 2):
                exps(g, u)
                copy(g - 1, 1 - u)
            exps(GRP, GRP % 2, N + MEM - GRP * 512)
            copy(GRP - 1, (GRP - 1) % 2)
            copy(GRP, GRP % 2, LAST + MEM, 1)

            def stage(g, u, n=512):
                if not isinstance(g, int) or g > 1:
                    act.wait_ge(o_done, 4 * g - 4)
                act.activation(QX[:, u, 0:n], QT[:, bass.ds(g * 512, n)], ACT.Copy).then_inc(q_staged, 1)

            act.wait_ge(scales, 1)

            def square(t, u):
                r = xt[:, bass.ds(t, 1), :].rearrange("p a b -> p (a b)")
                act.activation(r, r, ACT.Identity, bias=nmr[:, bass.ds(t, 1)], scale=r1[:, bass.ds(t, 1)]).then_inc(x_ready, 1)
                act.wait_ge(o_ready, t + 1)
                act.wait_ge(squared, t + 1)
                act.activation(sq[:, u, :], O[:, bass.ds(t, 1), :].rearrange("p a b -> p (a b)"), ACT.Square,
                               accum_out=ss[:, bass.ds(t, 1)]).then_inc(squared, 1)

            act.sem_inc(squared, 2)
            stage(0, 0)
            stage(1, 1)
            for g, u in tiles(act, 2, GRP, 2):
                for j in range(4):
                    square(g * 4 - 8 + j, j % 2)
                stage(g, u)
            for t in range(4 * GRP - 8, 4 * GRP - 4):
                square(t, t % 2)
            stage(GRP, GRP % 2, P)
            for t in range(4 * GRP - 4, TILES):
                square(t, t % 2)
            act.wait_ge(squared, TILES + 2)
            act.activation(ss[:, :], ss[:, :], ACT.Sqrt).then_inc(squared, 1)

        @block.tensor
        def _(pe):
            def turn(g, u):
                pe.wait_ge(exped, g + 1)
                if not isinstance(g, int) or g > 1:
                    pe.wait_ge(k_copied, g - 1)
                for j in range(4):
                    last = pe.transpose(PS[:, u, j * P:(j + 1) * P], KX[:, u, j * P:(j + 1) * P], ident[:, :])
                last.then_inc(k_turned, 1)

            def gather(g, u, start=False):
                pe.wait_ge(k_copied, g + 1)
                for j in range(4):
                    last = pe.matmul(PS[:, 2, 0:P], EK[:, u, j, :], V[:, bass.ds(g * 4 + j, 1), :].rearrange("p a b -> p (a b)"),
                                     start=start and j == 0, stop=False)
                last.then_inc(k_used, 1)

            turn(0, 0)
            turn(1, 1)
            gather(0, 0, start=True)
            for g, u in tiles(pe, 2, GRP, 2):
                turn(g, u)
                gather(g - 1, 1 - u)
            rows = LAST + MEM
            pe.wait_ge(exped, GRP + 1)
            pe.wait_ge(k_copied, GRP - 1)
            pe.transpose(PS[0:rows, GRP % 2, 0:P], KX[:, GRP % 2, 0:rows], ident[:, :]).then_inc(k_turned, 1)
            gather(GRP - 1, (GRP - 1) % 2)
            pe.wait_ge(k_copied, GRP + 1)
            pe.matmul(PS[:, 2, 0:P], EK[0:rows, GRP % 2, 0, :], V[0:rows, TILES - 1, :], start=False, stop=True).then_inc(ctx_done, 1)
            pe.wait_ge(ctx_ready, 1)
            pe.transpose(PS[:, 3, 0:P], ctx[:, :], ident[:, :]).then_inc(ctx_done, 1)
            pe.wait_ge(ctx_ready, 2)
            pe.wait_ge(loaded, 4 * 16)
            pe.matmul(PS[:, 2, 0:D], ctx[:, :], WO[:, :], start=True, stop=True).then_inc(cw_done, 1)
            pe.wait_ge(cw_ready, 1)

            def out_tile(t, u, ring, j):
                if not isinstance(t, int) or t > 1:
                    pe.wait_ge(o_ready, t - 1)
                pe.matmul(PS[:, 4 + u, 0:D], QX[:, ring, j * P:(j + 1) * P], CW[:, :], start=True, stop=True).then_inc(o_done, 1)

            for g in range(2):
                pe.wait_ge(q_staged, g + 1)
                for j in range(4):
                    out_tile(4 * g + j, j % 2, g, j)
            for g, u in tiles(pe, 2, GRP, 2):
                pe.wait_ge(q_staged, g + 1)
                for j in range(4):
                    out_tile(4 * g + j, j % 2, u, j)
            pe.wait_ge(q_staged, GRP + 1)
            out_tile(4 * GRP, 0, GRP % 2, 0)


class Layer:

    def __init__(self, heads, row, wide, banks, logit_cols):
        self.heads = heads
        self.row = row
        self.wide = wide
        self.banks = banks
        self.logit_cols = logit_cols


LAYER1 = Layer(H1, ROW1, ROW1, 2, [256 + a * HALF + j for a in range(2) for j in range(4)])
LAYER2 = Layer(1, ROW2, D + 1, 1, [D + 1])


def bounds(nc, allocator, dev, layer, table, AD, ADM, SELF):
    PS, ident, iota_row, ones, SRC, DST, TK = (dev[k] for k in (
        "PS", "ident", "iota_row", "ones", "SRC", "DST", "TK"))
    H = layer.heads
    tag = f"h{H}_"
    with ExitStack() as st:
        sb, sem = allocator(st)
        ext = sb(tag + "ext", [P, 2 * H])
        exta = sb(tag + "exta", [P, 2 * H])
        MX = sb(tag + "MX", [P, TILES, H])
        Z = sb(tag + "Zb", [P, TILES, H])
        spread = sb(tag + "spread", [P, H])
        widest = sb(tag + "widest", [P, 1])
        wide = sb(tag + "wide", [P, 1], I32)
        ext_ready, ext_all, own = sem(tag + "ext_ready"), sem(tag + "ext_all"), sem(tag + "bound_own")
        flag_ready, z_ready = sem(tag + "flag_ready"), sem(tag + "self_logits")
        G = sb(tag + "Gx", [P, layer.row])
        idx = sb(tag + "idx", [P, 1], I32)
        S = sb(tag + "Sx", [P, P])
        off = sb(tag + "off", [P, P])
        diag = sb(tag + "diag", [P, H, P])
        mxs = sb(tag + "mxs", [P, H])
        released = sem(tag + "x_released")
        staged, fetched, used = sem(tag + "x_staged"), sem(tag + "x_fetched"), sem(tag + "x_used")
        cols, spread_out, xown = sem(tag + "x_cols"), sem(tag + "x_ps"), sem(tag + "x_own")
        block = st.enter_context(nc.Block())

        @block.gpsimd
        def _(pool):
            pool.wait_ge(ext_ready, 1)
            pool.partition_all_reduce(exta[:, :], ext[:, :], P, RMAX).then_inc(ext_all, 1)
            pool.wait_ge(flag_ready, 1)
            with pool.If(pool.value_load(wide[0:1, 0:1], min_val=0, max_val=1) > 0):
                for s, _ in tiles(pool, 0, SLOTS, 1):
                    pool.wait_ge(used, s + 1)
                    pool.wait_ge(staged, s + 1)
                    pool.sem_inc(released, 1)
                    pool.indirect_dma_start(G[:, :], None, table, IndexOn(ap=idx[:, 0:1], axis=0)).then_inc(fetched, 16)

        @block.scalar
        def _(act):
            act.wait_ge(flag_ready, 1)
            with act.If(act.value_load(wide[0:1, 0:1], min_val=0, max_val=1) > 0):
                act.activation(idx[:, :], SRC[:, 0:1], ACT.Copy).then_inc(staged, 1)
                for s, _ in tiles(act, 1, SLOTS, 1):
                    act.wait_ge(fetched, 16 * s)
                    act.activation(idx[:, :], SRC[:, bass.ds(s, 1)], ACT.Copy).then_inc(staged, 1)
            act.wait_ge(z_ready, 1)
            act.activation(SELF[:, :, :], Z[:, :, :], ACT.Exp)

        @block.tensor
        def _(pe):
            pe.wait_ge(flag_ready, 1)
            with pe.If(pe.value_load(wide[0:1, 0:1], min_val=0, max_val=1) > 0):
                for s, _ in tiles(pe, 0, SLOTS, 1):
                    pe.wait_ge(cols, s + 1)
                    for h in range(H):
                        o = PS[:, h // 4, (h % 4) * P:(h % 4 + 1) * P]
                        pe.matmul(o, ones[:, :], diag[:, h, :], start=True, stop=False)
                        last = pe.matmul(o, off[:, :], ident[:, :], start=False, stop=True)
                    last.then_inc(spread_out, 1)

        @block.vector
        def _(dve):
            own_ = Chain(dve, own)
            by_head = AD[:, :, 0:H].rearrange("p t h -> p h t")
            dve.tensor_reduce(ext[:, 0:H], by_head, X, ALU.max)
            dve.tensor_reduce(ext[:, H:2 * H], by_head, X, ALU.min, negate=True).then_inc(ext_ready, 1)
            dve.wait_ge(ext_all, 1)
            own_.link(dve.tensor_copy(MX[:, :, :], one(exta[:, 0:H], 1, TILES)))
            own_.link(dve.tensor_tensor(spread[:, :], exta[:, 0:H], exta[:, H:2 * H], ALU.add))
            own_.link(dve.tensor_reduce(widest[:, :], spread[:, :], X, ALU.max))
            dve.tensor_scalar(wide[:, :], widest[:, :], SPREAD, None, ALU.is_gt).then_inc(flag_ready, 1)
            dve.wait_ge(flag_ready, 1)
            with dve.If(dve.value_load(wide[0:1, 0:1], min_val=0, max_val=1) > 0):
                xown_ = Chain(dve, xown)
                xown_.link(dve.tensor_copy(MX[:, :, :], AD[:, :, 0:H]))
                dve.sem_inc(used, 1)
                per = H + 4
                for k, _ in tiles(dve, 0, STEPS, 1):
                    t = dve.value_load(TK[0:1, bass.ds(k, 1)], min_val=0, max_val=TILES - 1)
                    xown_.at(1 + k * 2 * per)
                    for j in range(2):
                        s = 2 * k + j
                        dve.wait_ge(fetched, 16 * s + 16)
                        xown_.link(dve.tensor_scalar(S[:, :], iota_row[:, :], DST[:, bass.ds(s, 1)], None, ALU.is_equal))
                        xown_.link(dve.tensor_scalar(off[:, :], S[:, :], 1.0, BIG, ALU.subtract, ALU.mult))
                        for h, c in enumerate(layer.logit_cols):
                            xown_.link(dve.tensor_scalar(diag[:, h, :], ident[:, :], G[:, c:c + 1], None, ALU.mult))
                        dve.sem_inc(used, 1)
                        dve.sem_inc(cols, 1)
                        dve.wait_ge(spread_out, s + 1)
                        if H == 8:
                            xown_.link(dve.tensor_reduce(mxs[:, :].rearrange("p (a b) -> p a b", a=2),
                                                         PS[:, 0:2, :].rearrange("p a (b e) -> p a b e", b=4), X, ALU.max))
                        else:
                            xown_.link(dve.tensor_reduce(mxs[:, :], PS[:, 0, 0:P], X, ALU.max))
                        m = MX[:, bass.ds(t, 1), :].rearrange("p a b -> p (a b)")
                        xown_.link(dve.tensor_tensor(m, m, mxs[:, :], ALU.max))
                    xown_.closed(2 * per)
            own_.link(dve.tensor_copy(ADM[:, :, 0:H], AD[:, :, H:2 * H]))
            own_.link(dve.tensor_tensor(Z[:, :, :], MX[:, :, :], AD[:, :, H:2 * H], ALU.add))
            own_.link(dve.scalar_tensor_tensor(ADM[:, :, H:2 * H], Z[:, :, :], SLOPE, Z[:, :, :], ALU.mult, ALU.max))
            own_.link(dve.tensor_tensor(Z[:, :, :], AD[:, :, 0:H], AD[:, :, H:2 * H], ALU.add))
            own_.link(dve.scalar_tensor_tensor(Z[:, :, :], Z[:, :, :], SLOPE, Z[:, :, :], ALU.mult, ALU.max))
            dve.tensor_tensor(Z[:, :, :], Z[:, :, :], ADM[:, :, H:2 * H], ALU.subtract).then_inc(z_ready, 1)


def walk(nc, allocator, dev, layer, table, ADM, ACC):
    PS, ident, iota_row, SRC, DST, TK = (dev[k] for k in ("PS", "ident", "iota_row", "SRC", "DST", "TK"))
    H, W = layer.heads, layer.wide
    tag = f"w{H}_"
    B = 4
    NB = SLOTS // B
    RING = 6
    assert SLOTS % B == 0
    with ExitStack() as st:
        sb, sem = allocator(st)
        G = sb(tag + "G", [P, RING, B, layer.row])
        idx = sb(tag + "idx", [P, RING, B], I32)
        S = sb(tag + "S", [P, RING, B, P])
        ident16 = sb(tag + "ident16", [P, P], BF16)
        ST = sb(tag + "ST", [P, 2, B, P])
        Z = sb(tag + "Z", [P, 2, B, H])
        PW = sb(tag + "PW", [P, RING, B, H])
        SW = None if H > 1 else sb(tag + "SW", [P, 2, B, P])
        fetched = [sem(f"{tag}fetched{r}") for r in range(RING)]
        staged = sem(tag + "staged")
        hot = sem(tag + "hot")
        turned, st_ready = sem(tag + "turned"), sem(tag + "st_ready")
        spread = sem(tag + "spread")
        z_ready, weighed = sem(tag + "z_ready"), sem(tag + "weighed")
        scaled = sem(tag + "scaled")
        summed = sem(tag + "summed")
        merged = sem(tag + "merged")
        own = sem(tag + "logit_own")
        ident_ready = sem(tag + "ident16_ready")
        act_scaled = sem(tag + "act_scaled")
        released = sem(tag + "released")
        block = st.enter_context(nc.Block())

        def filled(q):
            return q * (16 * B) + 16 * B

        def tile_of(eng, k):
            return eng.value_load(TK[0:1, bass.ds(k, 1)], min_val=0, max_val=TILES - 1)

        def tiles_of(eng, n):
            return tile_of(eng, 2 * n), tile_of(eng, 2 * n + 1)

        @block.gpsimd
        def _(pool):
            def fetch(n, r):
                pool.wait_ge(staged, n + 1)
                if not isinstance(n, int) or n >= RING:
                    pool.wait_ge(summed, 2 * (n - RING) + 2)
                pool.sem_inc(released, 1)
                for b in range(B):
                    pool.indirect_dma_start(G[:, r, b, :], None, table, IndexOn(ap=idx[:, r, b:b + 1], axis=0)).then_inc(fetched[r], 16)

            for n in range(RING):
                fetch(n, n)
            for n, r in tiles(pool, RING, NB, RING):
                fetch(n, r)

        @block.scalar
        def _(act):
            def stage(n, r):
                act.activation(idx[:, r, :], SRC[:, bass.ds(n * B, B)], ACT.Copy).then_inc(staged, 1)

            def copy_turned(n, r):
                act.wait_ge(turned, n + 1)
                if not isinstance(n, int) or n > 1:
                    act.wait_ge(spread, n - 1)
                act.activation(ST[:, r % 2, :, :], PS[:, 4 + r % 2, :].bitcast(BF16)[:, 0:B * P].rearrange("p (b q) -> p b q", b=B), ACT.Copy).then_inc(st_ready, 1)

            def weigh(n, r):
                act.wait_ge(z_ready, n + 1)
                if H == 8:
                    out = G[:, r, :, :].rearrange("p b (a c) -> p b a c", a=2)[:, :, :, 4 * C1:]
                    act.activation(out, Z[:, r % 2, :, :].rearrange("p b (a c) -> p b a c", a=2), ACT.Exp).then_inc(weighed, 1)
                else:
                    act.activation(PW[:, r, :, :], Z[:, r % 2, :, :], ACT.Exp).then_inc(weighed, 1)

            def scale_last(n, r):
                if H == 8:
                    act.wait_ge(weighed, n + 1)
                    for h in range(H):
                        at, w = h // 4 * HALF + h % 4 * C1, h // 4 * HALF + 4 * C1 + h % 4
                        feat = G[:, r, B - 1, at:at + C1]
                        last = act.activation(feat, feat, ACT.Copy, scale=G[:, r, B - 1, w:w + 1])
                    last.then_inc(act_scaled, 1)

            for n in range(RING):
                stage(n, n)
            copy_turned(0, 0)
            copy_turned(1, 1)
            weigh(0, 0)
            copy_turned(2, 2)
            weigh(1, 1)
            scale_last(0, 0)

            def step(n, r):
                scale_last(n + 1, (r + 1) % RING)
                weigh(n + 2, (r + 2) % RING)
                copy_turned(n + 3, (r + 3) % RING)

            for n, r, q in turns(act, 0, NB - RING, RING):
                step(n, r)
                act.wait_ge(fetched[r], filled(q))
                stage(n + RING, r)
            for n in range(NB - RING, NB - 3):
                step(n, n % RING)
            scale_last(NB - 2, (NB - 2) % RING)
            weigh(NB - 1, (NB - 1) % RING)
            scale_last(NB - 1, (NB - 1) % RING)

        @block.tensor
        def _(pe):
            def turn(n, r):
                pe.wait_ge(hot, n + 1)
                if not isinstance(n, int) or n > 1:
                    pe.wait_ge(st_ready, n - 1)
                out = PS[:, 4 + r % 2, :].bitcast(BF16)
                for b in range(B):
                    upper = S[:, r, b, :].bitcast(BF16).rearrange("p (q two) -> p q two", two=2)[:, :, 1]
                    last = pe.transpose(out[:, b * P:(b + 1) * P], upper, ident16[:, :])
                last.then_inc(turned, 1)

            def spread_nodes(n, r, t=None):
                t = tiles_of(pe, n) if t is None else t
                pe.wait_ge(st_ready, n + 1)
                if not isinstance(n, int) or n > 1:
                    pe.wait_ge(z_ready, n - 1)
                for j in range(2):
                    for b in (2 * j, 2 * j + 1):
                        last = pe.matmul(PS[:, 6 + r % 2, b * 2 * H:(b + 1) * 2 * H], ST[:, r % 2, b, :],
                                         ADM[:, bass.ds(t[j], 1), :].rearrange("p a b -> p (a b)"), start=True, stop=True)
                last.then_inc(spread, 1)

            def sum_up(n, r, j):
                k = 2 * n + j
                pe.wait_ge(scaled, k + 1)
                if H == 8 and j == 1:
                    pe.wait_ge(act_scaled, n + 1)
                if not isinstance(n, int) or k > 1:
                    pe.wait_ge(merged, k)
                for b in (2 * j, 2 * j + 1):
                    for a in range(layer.banks):
                        if H == 8:
                            lhsT, rhs = S[:, r, b, :], G[:, r, b, a * HALF:(a + 1) * HALF]
                        else:
                            lhsT, rhs = SW[:, r % 2, b, :], G[:, r, b, 0:W]
                        last = pe.matmul(PS[:, 2 * j + a, 0:W // layer.banks], lhsT, rhs, start=b % 2 == 0, stop=b % 2 == 1)
                last.then_inc(summed, 1)

            def step(n, r):
                t = tiles_of(pe, n + 2)
                sum_up(n, r, 0)
                spread_nodes(n + 2, (r + 2) % RING, t)
                sum_up(n, r, 1)
                turn(n + 3, (r + 3) % RING)

            pe.wait_ge(ident_ready, 1)
            turn(0, 0)
            turn(1, 1)
            spread_nodes(0, 0)
            turn(2, 2)
            spread_nodes(1, 1)
            step(0, 0)
            for n, r in tiles(pe, 1, NB - 3, RING):
                step(n, r)
            spread_nodes(NB - 1, (NB - 1) % RING)
            for n in range(NB - 3, NB):
                for j in range(2):
                    sum_up(n, n % RING, j)

        @block.vector
        def _(dve):
            def one_hot(n, r, slots=range(B)):
                for b in slots:
                    last = dve.tensor_scalar(S[:, r, b, :], iota_row[:, :], DST[:, bass.ds(n * B + b, 1)], None, ALU.is_equal)
                if B - 1 in slots:
                    last.then_inc(hot, 1)

            def logits(n, r, q, between=lambda b: None):
                dve.wait_ge(spread, n + 1)
                dve.wait_ge(fetched[r], filled(q))
                node = PS[:, 6 + r % 2, 0:B * 2 * H].rearrange("p (b c) -> p b c", b=B)
                if H == 8:
                    a_src = G[:, r, :, :].rearrange("p b (a c) -> p b a c", a=2)[:, :, :, 4 * C1:]
                    a_dst = node[:, :, 0:H].rearrange("p b (a c) -> p b a c", a=2)
                    z4 = Z[:, r % 2, :, :].rearrange("p b (a c) -> p b a c", a=2)
                else:
                    a_src, a_dst, z4 = G[:, r, :, D + 1:D + 2], node[:, :, 0:H], Z[:, r % 2, :, :]
                z = Z[:, r % 2, :, :]
                dve.tensor_tensor(z4, a_src, a_dst, ALU.add).then_inc(own, 1)
                between(0)
                dve.wait_ge(own, 3 * n + 1)
                dve.scalar_tensor_tensor(z, z, SLOPE, z, ALU.mult, ALU.max).then_inc(own, 1)
                between(1)
                dve.wait_ge(own, 3 * n + 2)
                dve.tensor_tensor(z, z, node[:, :, H:2 * H], ALU.subtract).then_inc(own, 1)
                between(2)
                dve.wait_ge(own, 3 * n + 3)
                dve.tensor_scalar(z, z, 1.0, None, ALU.min).then_inc(z_ready, 1)
                between(3)

            def scale(n, r, j):
                dve.wait_ge(weighed, n + 1)
                for b in (2 * j, 2 * j + 1)[:1 if H == 8 and j == 1 else 2]:
                    if H == 8:
                        row = G[:, r, b, :].rearrange("p (a c) -> p a c", a=2)
                        feat = row[:, :, 0:4 * C1].rearrange("p a (h c) -> p a h c", h=4)
                        last = dve.tensor_tensor(feat, feat, one(row[:, :, 4 * C1:], 3, C1), ALU.mult)
                    else:
                        last = dve.tensor_scalar(SW[:, r % 2, b, :], iota_row[:, :], DST[:, bass.ds(n * B + b, 1)],
                                                 PW[:, r, b, :], ALU.is_equal, ALU.mult)
                last.then_inc(scaled, 1)

            def merge(k, j):
                t = tile_of(dve, k)
                dve.wait_ge(summed, k + 1)
                dve.wait_ge(merged, k + 1)
                if H == 8:
                    acc = ACC[:, bass.ds(t, 1), :].rearrange("p t (a c) -> p (t a) c", a=2)
                    dve.tensor_tensor(acc, acc, PS[:, 2 * j:2 * j + 2, 0:HALF], ALU.add).then_inc(merged, 1)
                else:
                    acc = ACC[:, bass.ds(t, 1), :].rearrange("p t c -> p (t c)")
                    dve.tensor_tensor(acc, acc, PS[:, 2 * j, 0:W], ALU.add).then_inc(merged, 1)

            def step(n, r, q, hots=True, more=True):
                scale(n + 1, (r + 1) % RING, 0)
                if not isinstance(n, int) or n > 0:
                    merge(2 * n - 1, 1)
                scale(n + 1, (r + 1) % RING, 1)
                merge(2 * n, 0)
                if more:
                    logits(n + 2, (r + 2) % RING, q + (r + 2) // RING,
                           (lambda b: one_hot(n + 4, (r + 4) % RING, (b,))) if hots else lambda b: None)

            dve.tensor_copy(ident16[:, :], ident[:, :]).then_inc(ident_ready, 1)
            for n in range(4):
                one_hot(n, n)
                if n == 2:
                    dve.memset(ACC[:, :, :], 0.0).then_inc(merged, 1)
            logits(0, 0, 0)
            logits(1, 1, 0)
            scale(0, 0, 0)
            scale(0, 0, 1)
            step(0, 0, 0)
            for n, r, q in turns(dve, 1, NB - 4, RING):
                step(n, r, q)
            for n in (NB - 4, NB - 3):
                step(n, n % RING, n // RING, hots=False)
            step(NB - 2, (NB - 2) % RING, 0, more=False)
            merge(2 * NB - 3, 1)
            merge(2 * NB - 2, 0)
            merge(2 * NB - 1, 1)


def between(nc, allocator, dev, ACC, SELF, AD2):
    PS, ident, table1, table2 = (dev[k] for k in ("PS", "ident", "table1", "table2"))
    FT = F1 // P
    with ExitStack() as st:
        sb, sem = allocator(st)
        W2A = sb("W2A", [P, FT, ROW2 + 1])
        att2 = sb("att2", [P, 2, D])
        prod = sb("prod2", [P, D])
        b1b = sb("b1b", [P, F1])
        unit_col = sb("unit_col", [P, ROW2])
        RD = sb("RD", [P, TILES, H1])
        HR = sb("HR", [P, 2, ROW1])
        HP = sb("HP", [P, 3, F1])
        EX = sb("EX", [P, 2, F1])
        EL = sb("EL", [P, 2, F1])
        ELT = sb("ELT", [P, 2, FT, P])
        row = sb("row2", [P, 2, ROW2])
        loaded, own, folded = sem("f_loaded"), sem("f_own"), sem("f_folded")
        mine_in = [sem(f"mine_in{u}") for u in range(2)]
        mine_scaled, o_ready, o_exp, el_ready, fown = sem("mine_scaled"), sem("f_o_ready"), sem("f_o_exp"), sem("el_ready"), sem("fo_own")
        el_turned, elt_ready, rows_done, rows_ready = sem("el_turned"), sem("elt_ready"), sem("rows2_done"), sem("rows2_ready")
        stored = [sem(f"rows2_stored{u}") for u in range(2)]
        block = st.enter_context(nc.Block())

        @block.sync
        def _(sp):
            sp.dma_start(W2A[:, :, 0:D], dev["W2"].rearrange("(k p) n -> p k n", p=P)).then_inc(loaded, 16)
            for j, v in enumerate(("att_s2", "att_d2")):
                sp.dma_start(att2[:, j, :], dev[v].rearrange("a c -> (a c)").partition_broadcast(P)).then_inc(loaded, 16)
            sp.dma_start(b1b[:, :], dev["b1"].partition_broadcast(P)).then_inc(loaded, 16)
            for u in range(2):
                sp.sem_inc(stored[u], 16)

            def fetch(t, u):
                sp.dma_start(HR[:, u, :], table1[bass.ds(t * P, P), :]).then_inc(mine_in[u], 16)

            def store(t, u):
                sp.wait_ge(rows_ready, t + 1)
                sp.dma_start(table2[bass.ds(t * P, P), :], row[:, u, :]).then_inc(stored[u], 16)

            fetch(0, 0)
            fetch(1, 1)
            for t, u in tiles(sp, 2, TILES, 2):
                sp.wait_ge(mine_scaled, t - 1)
                fetch(t, u)
                store(t - 2, u)
            for t in (TILES - 2, TILES - 1):
                store(t, t % 2)
            for u in range(2):
                sp.wait_ge(stored[u], 16 + 16 * len(range(u, TILES, 2)))

        @block.gpsimd
        def _(pool):
            def mine(t, u, h):
                pool.wait_ge(mine_in[u], rounds(t, u))
                pool.tensor_tensor(HP[:, h, :].rearrange("p (a h c) -> p a h c", a=2, h=4),
                                   HR[:, u, :].rearrange("p (a c) -> p a c", a=2)[:, :, 0:4 * C1].rearrange("p a (h c) -> p a h c", h=4),
                                   one(SELF[:, bass.ds(t, 1), :].rearrange("p t (a h) -> p (t a) h", a=2), 3, C1),
                                   ALU.mult).then_inc(mine_scaled, 1)

            for t in range(3):
                mine(t, t % 2, t)
            for t, u in tiles(pool, 3, TILES, 6):
                pool.wait_ge(el_ready, t - 2)
                mine(t, u % 2, u % 3)

        @block.vector
        def _(dve):
            own_, fown_ = Chain(dve, own), Chain(dve, fown)
            own_.link(dve.memset(W2A[:, :, D:D + 1], 0.0))
            own_.link(dve.memset(unit_col[:, :], 0.0))
            own_.link(dve.memset(unit_col[:, D:D + 1], 1.0))
            dve.wait_ge(loaded, 4 * 16)
            for k in range(FT):
                for j in range(2):
                    own_.link(dve.tensor_tensor(prod[:, :], W2A[:, k, 0:D], att2[:, j, :], ALU.mult))
                    own_.link(dve.tensor_reduce(W2A[:, k, D + 1 + j:D + 2 + j], prod[:, :], X, ALU.add))
            sums = ACC[:, :, :].rearrange("p t (a c) -> p t a c", a=2)[:, :, :, 4 * C1:]
            own_.link(dve.tensor_tensor(RD[:, :, :].rearrange("p t (a h) -> p t a h", a=2), sums,
                                        SELF[:, :, :].rearrange("p t (a h) -> p t a h", a=2), ALU.add))
            own_.link(dve.reciprocal(RD[:, :, :], RD[:, :, :]))
            dve.engine_nop().then_inc(folded, 1)

            def quotient(t, h):
                fown_.at(2 * t)
                o = HP[:, h, :]
                o4 = o.rearrange("p (a h c) -> p a h c", a=2, h=4)
                acc = ACC[:, bass.ds(t, 1), :].rearrange("p t (a c) -> p (t a) c", a=2)[:, :, 0:4 * C1].rearrange("p a (h c) -> p a h c", h=4)
                dve.wait_ge(mine_scaled, t + 1)
                fown_.link(dve.tensor_tensor(o4, o4, acc, ALU.add))
                fown_.link(dve.tensor_tensor(o4, o4, one(RD[:, bass.ds(t, 1), :].rearrange("p t (a h) -> p (t a) h", a=2), 3, C1), ALU.mult))
                dve.tensor_tensor(o, o, b1b[:, :], ALU.add).then_inc(o_ready, 1)

            def elu(t, u, h):
                dve.wait_ge(o_exp, 2 * t + 2)
                if not isinstance(t, int) or t > 1:
                    dve.wait_ge(el_turned, t - 1)
                dve.scalar_tensor_tensor(EL[:, u, :], EX[:, u, :], 1.0, HP[:, h, :], ALU.min, ALU.add).then_inc(el_ready, 1)

            def rows(t, u):
                dve.wait_ge(rows_done, t + 1)
                dve.wait_ge(stored[u], rounds(t, u))
                dve.tensor_copy(AD2[:, bass.ds(t, 1), :].rearrange("p a b -> p (a b)"), PS[:, 2 + u, D + 1:D + 3])
                dve.tensor_tensor(row[:, u, :], PS[:, 2 + u, 0:ROW2], unit_col[:, :], ALU.add).then_inc(rows_ready, 1)

            quotient(0, 0)
            quotient(1, 1)
            elu(0, 0, 0)
            for t, u in tiles(dve, 2, TILES, 6):
                quotient(t, u % 3)
                elu(t - 1, (u - 1) % 2, (u - 1) % 3)
                rows(t - 2, u % 2)
            t = TILES - 1
            elu(t, t % 2, t % 3)
            rows(t - 1, (t - 1) % 2)
            rows(t, t % 2)

        @block.scalar
        def _(act):
            def curve(t, u, h):
                act.wait_ge(o_ready, t + 1)
                if not isinstance(t, int) or t > 1:
                    act.wait_ge(el_ready, t - 1)
                act.activation(EX[:, u, :], HP[:, h, :], ACT.Exp).then_inc(o_exp, 1)
                act.wait_ge(o_exp, 2 * t + 1)
                act.activation(HP[:, h, :], HP[:, h, :], ACT.Relu).then_inc(o_exp, 1)

            def copy(t, u):
                act.wait_ge(el_turned, t + 1)
                if not isinstance(t, int) or t > 1:
                    act.wait_ge(rows_done, t - 1)
                act.activation(ELT[:, u, :, :], PS[:, u, :].rearrange("p (k q) -> p k q", k=FT), ACT.Copy, bias=-1.0).then_inc(elt_ready, 1)

            curve(0, 0, 0)
            curve(1, 1, 1)
            copy(0, 0)
            for t, u in tiles(act, 2, TILES, 6):
                curve(t, u % 2, u % 3)
                copy(t - 1, (u - 1) % 2)
            copy(TILES - 1, (TILES - 1) % 2)

        @block.tensor
        def _(pe):
            def turn(t, u):
                pe.wait_ge(el_ready, t + 1)
                if not isinstance(t, int) or t > 1:
                    pe.wait_ge(elt_ready, t - 1)
                for k in range(FT):
                    last = pe.transpose(PS[:, u, k * P:(k + 1) * P], EL[:, u, k * P:(k + 1) * P], ident[:, :])
                last.then_inc(el_turned, 1)

            def product(t, u):
                pe.wait_ge(elt_ready, t + 1)
                if not isinstance(t, int) or t > 1:
                    pe.wait_ge(rows_ready, t - 1)
                for k in range(FT):
                    last = pe.matmul(PS[:, 2 + u, 0:ROW2 + 1], ELT[:, u, k, :], W2A[:, k, :], start=k == 0, stop=k == FT - 1)
                last.then_inc(rows_done, 1)

            pe.wait_ge(folded, 1)
            turn(0, 0)
            turn(1, 1)
            product(0, 0)
            product(1, 1)
            for t, u in tiles(pe, 2, TILES, 2):
                turn(t, u)
                product(t, u)


def residual(nc, allocator, dev, ACC, SELF, X1, bn):
    table2, resid, xbuf = dev["table2"], dev["resid"], dev["xbuf"]
    with ExitStack() as st:
        sb, sem = allocator(st)
        HR = sb("HR2", [P, 2, ROW2])
        RS = sb("RS", [P, 2, D])
        T = sb("T", [P, 2, D + 1])
        RD = sb("RD2", [P, TILES])
        zero = sb("zero", [P, 8, D])
        own, blank, tile_own = sem("r_own"), sem("blank"), sem("r_tile_own")
        mine_in = [sem(f"r_mine_in{u}") for u in range(2)]
        used, cleared = sem("r_used"), sem("cleared")
        block = st.enter_context(nc.Block())

        @block.sync
        def _(sp):
            def fetch(t, u):
                sp.dma_start(HR[:, u, :], table2[bass.ds(t * P, P), :]).then_inc(mine_in[u], 16)
                sp.dma_start(RS[:, u, :], resid[bass.ds(t * P, P), :]).then_inc(mine_in[u], 16)

            fetch(0, 0)
            fetch(1, 1)
            for t, u in tiles(sp, 2, TILES, 2):
                sp.wait_ge(used, t - 1)
                fetch(t, u)

        @block.gpsimd
        def _(pool):
            pool.memset(zero[:, :, :], 0.0).then_inc(blank, 1)

        @block.scalar
        def _(act):
            act.wait_ge(blank, 1)
            for e in range(EXPERTS):
                act.dma_start(xbuf[e * CT * P:(e + 1) * CT * P, :].rearrange("(p j) n -> p j n", p=P), zero[:, :, :]).then_inc(cleared, 16)
            act.wait_ge(cleared, 16 * EXPERTS)

        @block.vector
        def _(dve):
            own_, tile_ = Chain(dve, own), Chain(dve, tile_own)
            own_.link(dve.tensor_tensor(RD[:, :], ACC[:, :, D], SELF[:, :, 0], ALU.add))
            own_.link(dve.reciprocal(RD[:, :], RD[:, :]))
            for t, u in tiles(dve, 0, TILES, 2):
                tile_.at(2 * t)
                dve.wait_ge(mine_in[u], (t - u) * 16 + 32)
                tile_.link(dve.scalar_tensor_tensor(T[:, u, :], HR[:, u, 0:D + 1], SELF[:, bass.ds(t, 1), :].rearrange("p t a -> p (t a)"),
                                                    ACC[:, bass.ds(t, 1), :].rearrange("p t c -> p (t c)"), ALU.mult, ALU.add))
                x1 = X1[:, bass.ds(t, 1), :].rearrange("p a b -> p (a b)")
                tile_.link(dve.scalar_tensor_tensor(x1, T[:, u, 0:D], RD[:, bass.ds(t, 1)], RS[:, u, :], ALU.mult, ALU.add))
                dve.bn_stats(bn[:, bass.ds(t, 1), :].rearrange("p a b -> p (a b)"), x1).then_inc(used, 1)


def gate(nc, allocator, dev, X1, bn, m1, r1, LG):
    PS, ident = dev["PS"], dev["ident"]
    with ExitStack() as st:
        sb, sem = allocator(st)
        va = sb("va1", [P, TILES])
        ta = sb("ta1", [P, TILES])
        GW = sb("GW", [P, 2, EXPERTS])
        gb = sb("gb", [P, EXPERTS])
        XN = sb("XN", [P, 2, D])
        XNT = sb("XNT", [P, 2, 2, P])
        own, to_root, rooted, loaded = sem("g_own"), sem("g_to_root"), sem("g_rooted"), sem("g_loaded")
        xn_ready, xn_turned, xnt_ready = sem("xn_ready"), sem("xn_turned"), sem("xnt_ready")
        lg_done, lg_ready = sem("lg_done"), sem("lg_ready")
        block = st.enter_context(nc.Block())

        @block.sync
        def _(sp):
            sp.dma_start(GW[:, :, :], dev["gate_w"].rearrange("(k p) e -> p k e", p=P)).then_inc(loaded, 16)
            sp.dma_start(gb[:, :], dev["gate_b"].partition_broadcast(P)).then_inc(loaded, 16)

        @block.vector
        def _(dve):
            own_ = Chain(dve, own)
            moments(dve, own_, bn, m1, va, ta)
            own_.link(dve.tensor_scalar(ta[:, :], va[:, :], EPS, None, ALU.add))
            dve.engine_nop().then_inc(to_root, 1)
            dve.wait_ge(rooted, 1)
            own_.link(dve.reciprocal(r1[:, :], ta[:, :]))

            def norm(t, u):
                if not isinstance(t, int) or t > 1:
                    dve.wait_ge(xn_turned, t - 1)
                dve.tensor_scalar(XN[:, u, :], X1[:, bass.ds(t, 1), :].rearrange("p a b -> p (a b)"),
                                  m1[:, bass.ds(t, 1)], r1[:, bass.ds(t, 1)], ALU.subtract, ALU.mult).then_inc(xn_ready, 1)

            def logits(t, u):
                dve.wait_ge(lg_done, t + 1)
                dve.tensor_tensor(LG[:, bass.ds(t, 1), :].rearrange("p a b -> p (a b)"), PS[:, 2 + u, 0:EXPERTS], gb[:, :],
                                  ALU.add).then_inc(lg_ready, 1)

            norm(0, 0)
            norm(1, 1)
            dve.wait_ge(loaded, 32)
            for t, u in tiles(dve, 2, TILES, 2):
                norm(t, u)
                logits(t - 2, u)
            for t in (TILES - 2, TILES - 1):
                logits(t, t % 2)

        @block.scalar
        def _(act):
            act.wait_ge(to_root, 1)
            act.activation(ta[:, :], ta[:, :], ACT.Sqrt).then_inc(rooted, 1)

            def copy(t, u):
                act.wait_ge(xn_turned, t + 1)
                if not isinstance(t, int) or t > 1:
                    act.wait_ge(lg_done, t - 1)
                act.activation(XNT[:, u, :, :], PS[:, u, 0:2 * P].rearrange("p (k q) -> p k q", k=2), ACT.Copy).then_inc(xnt_ready, 1)

            copy(0, 0)
            copy(1, 1)
            for t, u in tiles(act, 2, TILES, 2):
                copy(t, u)

        @block.tensor
        def _(pe):
            def turn(t, u):
                pe.wait_ge(xn_ready, t + 1)
                if not isinstance(t, int) or t > 1:
                    pe.wait_ge(xnt_ready, t - 1)
                for k in range(2):
                    last = pe.transpose(PS[:, u, k * P:(k + 1) * P], XN[:, u, k * P:(k + 1) * P], ident[:, :])
                last.then_inc(xn_turned, 1)

            def product(t, u):
                pe.wait_ge(xnt_ready, t + 1)
                if not isinstance(t, int) or t > 1:
                    pe.wait_ge(lg_ready, t - 1)
                for k in range(2):
                    last = pe.matmul(PS[:, 2 + u, 0:EXPERTS], XNT[:, u, k, :], GW[:, k, :], start=k == 0, stop=k == 1)
                last.then_inc(lg_done, 1)

            pe.wait_ge(loaded, 32)
            turn(0, 0)
            turn(1, 1)
            product(0, 0)
            turn(2, 0)
            product(1, 1)
            for t, u in tiles(pe, 3, TILES, 2):
                turn(t, u)
                product(t - 1, 1 - u)
            product(TILES - 1, (TILES - 1) % 2)


def route(nc, allocator, dev, LG, weight, put, take):
    PS, ones, iota_row = dev["PS"], dev["ones"], dev["iota_row"]
    with ExitStack() as st:
        sb, sem = allocator(st)
        lmax = sb("lmax", [P, TILES])
        EXL = sb("EXL", [P, TILES, EXPERTS])
        OH = sb("OH", [P, TILES, EXPERTS])
        CU = sb("CU", [P, TILES, EXPERTS])
        TOT = sb("TOT", [P, EXPERTS, TILES])
        INC = sb("INC", [P, EXPERTS, TILES])
        onesT = sb("onesT", [P, TILES])
        tri = sb("tri", [P, P])
        lane = sb("lane", [P, 1])
        choice, psum_, place, kept, full = (sb(n, [P, TILES]) for n in ("choice", "psum_", "place", "kept", "full"))
        own, consts, shifted, exped = sem("t_own"), sem("t_consts"), sem("t_shifted"), sem("t_exped")
        hot, counted = sem("t_hot"), sem("counted")
        block = st.enter_context(nc.Block())
        NOWHERE = float(1 << 20)

        @block.gpsimd
        def _(pool):
            pool.memset(onesT[:, :], 1.0).then_inc(consts, 1)
            pool.iota(lane[:, :], [[0, 1]], base=0, channel_multiplier=1, allow_small_or_imprecise_dtypes=True).then_inc(consts, 1)
            pool.affine_select(out=tri[:, :], in_=ones[:, :], compare_op=ALU.is_gt, fill=0.0,
                               base=0, pattern=[[1, P]], channel_multiplier=-1).then_inc(consts, 1)

        @block.scalar
        def _(act):
            act.wait_ge(shifted, 1)
            act.activation(EXL[:, :, :], EXL[:, :, :], ACT.Exp).then_inc(exped, 1)

        @block.tensor
        def _(pe):
            pe.wait_ge(consts, 3)
            pe.wait_ge(hot, 1)
            oh = OH[:, :, :].rearrange("p t e -> p (t e)")
            pe.matmul(PS[:, 0, 0:TILES * EXPERTS], tri[:, :], oh, start=True, stop=True)
            pe.matmul(PS[:, 1, 0:TILES * EXPERTS], ones[:, :], oh, start=True, stop=True).then_inc(counted, 1)

        @block.vector
        def _(dve):
            own_ = Chain(dve, own)
            own_.link(dve.tensor_reduce(lmax[:, :], LG[:, :, :], X, ALU.max))
            dve.tensor_tensor(EXL[:, :, :], LG[:, :, :], one(lmax[:, :], 2, EXPERTS), ALU.subtract).then_inc(shifted, 1)
            own_.link(dve.tensor_tensor(OH[:, :, :], LG[:, :, :], one(lmax[:, :], 2, EXPERTS), ALU.is_equal))
            number = one(iota_row[:, 0:EXPERTS], 1, TILES)
            own_.link(dve.tensor_scalar(CU[:, :, :], OH[:, :, :], -float(EXPERTS), float(EXPERTS), ALU.mult, ALU.add))
            own_.link(dve.tensor_tensor(CU[:, :, :], CU[:, :, :], number, ALU.add))
            own_.link(dve.tensor_reduce(choice[:, :], CU[:, :, :], X, ALU.min))
            own_.link(dve.tensor_tensor(OH[:, :, :], number, one(choice[:, :], 2, EXPERTS), ALU.is_equal))
            dve.engine_nop().then_inc(hot, 1)
            dve.wait_ge(consts, 3)
            dve.wait_ge(counted, 1)
            own_.link(dve.tensor_copy(TOT[:, :, :], PS[:, 1, 0:TILES * EXPERTS].rearrange("p (t e) -> p e t", e=EXPERTS)))
            for e in range(EXPERTS):
                own_.link(dve.tensor_tensor_scan(INC[:, e, :], onesT[:, :], TOT[:, e, :], 0.0, ALU.mult, ALU.add))
            own_.link(dve.tensor_tensor(INC[:, :, :], INC[:, :, :], TOT[:, :, :], ALU.subtract))
            own_.link(dve.tensor_tensor(CU[:, :, :], PS[:, 0, 0:TILES * EXPERTS].rearrange("p (t e) -> p t e", e=EXPERTS),
                                        INC[:, :, :].rearrange("p e t -> p t e"), ALU.add))
            own_.link(dve.tensor_tensor(CU[:, :, :], CU[:, :, :], OH[:, :, :], ALU.mult))
            own_.link(dve.tensor_reduce(place[:, :], CU[:, :, :], X, ALU.add))
            own_.link(dve.tensor_scalar(kept[:, :], place[:, :], float(CAP), None, ALU.is_lt))
            own_.link(dve.tensor_scalar(place[:, :], place[:, :], float(CAP - 1), None, ALU.min))
            own_.link(dve.scalar_tensor_tensor(place[:, :], choice[:, :], float(CAP), place[:, :], ALU.mult, ALU.add))
            own_.link(dve.tensor_copy(take[:, :], place[:, :]))
            own_.link(dve.tensor_scalar(full[:, :], kept[:, :], -NOWHERE, NOWHERE, ALU.mult, ALU.add))
            own_.link(dve.tensor_tensor(place[:, :], place[:, :], full[:, :], ALU.add))
            own_.link(dve.tensor_scalar(lane[:, :], lane[:, :], float(LAST), NOWHERE, ALU.is_ge, ALU.mult))
            own_.link(dve.tensor_tensor(place[:, TILES - 1:TILES], place[:, TILES - 1:TILES], lane[:, :], ALU.add))
            own_.link(dve.tensor_copy(put[:, :], place[:, :]))
            dve.wait_ge(exped, 1)
            own_.link(dve.tensor_reduce(psum_[:, :], EXL[:, :, :], X, ALU.add))
            own_.link(dve.reciprocal(psum_[:, :], psum_[:, :]))
            own_.link(dve.tensor_tensor(weight[:, :], psum_[:, :], kept[:, :], ALU.mult))


def dispatch(nc, allocator, dev, X1, m1, r1, put):
    xbuf = dev["xbuf"]
    with ExitStack() as st:
        sb, sem = allocator(st)
        XN = sb("XNd", [P, 4, D])
        idx = sb("putx", [P, 4], I32)
        ready, placed = sem("d_ready"), [sem(f"d_placed{r}") for r in range(4)]
        staged, released = sem("d_staged"), sem("d_released")
        block = st.enter_context(nc.Block())

        def landed(t, r):
            return rounds(t, r, 4) - 16

        @block.vector
        def _(dve):
            for t, r in ring4(dve):
                if not isinstance(t, int) or t >= 4:
                    dve.wait_ge(placed[r], landed(t, r))
                dve.tensor_scalar(XN[:, r, :], X1[:, bass.ds(t, 1), :].rearrange("p a b -> p (a b)"),
                                  m1[:, bass.ds(t, 1)], r1[:, bass.ds(t, 1)], ALU.subtract, ALU.mult).then_inc(ready, 1)

        @block.scalar
        def _(act):
            for t, r in ring4(act):
                if not isinstance(t, int) or t >= 4:
                    act.wait_ge(placed[r], landed(t, r))
                act.activation(idx[:, r:r + 1], put[:, bass.ds(t, 1)], ACT.Copy).then_inc(staged, 1)

        @block.gpsimd
        def _(pool):
            for t, r in tiles(pool, 0, TILES, 4):
                pool.wait_ge(ready, t + 1)
                pool.wait_ge(staged, t + 1)
                pool.sem_inc(released, 1)
                pool.indirect_dma_start(xbuf, IndexOn(ap=idx[:, r:r + 1], axis=0), XN[:, r, :], None,
                                        bounds_check=EXPERTS * CAP - 1, oob_is_err=False).then_inc(placed[r], 16)
            for r in range(4):
                pool.wait_ge(placed[r], 16 * len(range(r, TILES, 4)))


def experts(nc, allocator, dev):
    PS, ident, xbuf, ybuf = (dev[k] for k in ("PS", "ident", "xbuf", "ybuf"))
    ew1, eb1, ew2, eb2 = (dev[k] for k in ("ew1", "eb1", "ew2", "eb2"))
    KF = FF // P
    CH = [(0, 512), (512, CAP - 512)]
    with ExitStack() as st:
        sb, sem = allocator(st)
        w1 = sb("w1", [P, 2, 2, FF])
        w2 = sb("w2", [P, 2, KF, D])
        c1 = sb("c1", [P, 2, KF])
        c2 = sb("c2", [P, 2, D])
        XB = sb("XB", [P, 2, CT, D])
        XT = sb("XT", [P, 2, CT * P])
        HT = sb("HT", [P, KF, CAP])
        YS = sb("YS", [P, 2, CT, D])
        loaded = [sem(f"e_loaded{u}") for u in range(2)]
        stored = [sem(f"e_stored{u}") for u in range(2)]
        turned, copied, up, relu, down, y_ready = (sem("e_" + n) for n in ("turned", "copied", "up", "relu", "down", "y_ready"))
        block = st.enter_context(nc.Block())
        REST = CAP - (CT - 1) * P

        def rows_of(j):
            return P if j < CT - 1 else REST

        @block.sync
        def _(sp):
            def load(e, u):
                def at(a):
                    return a[bass.ds(e, 1)]
                sp.dma_start(XB[:, u, :, :], xbuf[bass.ds(e * CAP, CT * P), :].rearrange("(j p) n -> p j n", p=P)).then_inc(loaded[u], 16)
                sp.dma_start(w1[:, u, :, :], at(ew1).rearrange("a (k p) f -> p (a k) f", p=P)).then_inc(loaded[u], 16)
                with nc.allow_non_contiguous_dma(reason="a bias per partition"):
                    sp.dma_start(c1[:, u, :], at(eb1).rearrange("a (k p) -> p (a k)", p=P)).then_inc(loaded[u], 16)
                sp.dma_start(c2[:, u, :], at(eb2).rearrange("a n -> (a n)").partition_broadcast(P)).then_inc(loaded[u], 16)
                sp.dma_start(w2[:, u, :, :], at(ew2).rearrange("a (k p) n -> p (a k) n", p=P)).then_inc(loaded[u], 16)

            def store(e, u):
                sp.wait_ge(y_ready, CT * e + CT)
                sp.dma_start(ybuf[bass.ds(e * CAP, (CT - 1) * P), :].rearrange("(j p) n -> p j n", p=P), YS[:, u, 0:CT - 1, :]).then_inc(stored[u], 16)
                sp.dma_start(ybuf[bass.ds(e * CAP + (CT - 1) * P, REST), :], YS[0:REST, u, CT - 1, :]).then_inc(stored[u], 16)

            load(0, 0)
            load(1, 1)
            for e, u in tiles(sp, 0, EXPERTS - 2, 2):
                store(e, u)
                sp.wait_ge(down, CT * (e + 1))
                load(e + 2, u)
            for e in (EXPERTS - 2, EXPERTS - 1):
                store(e, e % 2)
            for u in range(2):
                sp.wait_ge(stored[u], 32 + 32 * (EXPERTS // 2))

        @block.tensor
        def _(pe):
            def turn(e, u):
                pe.wait_ge(loaded[u], (e - u) * 40 + 80)
                for i in range(4):
                    n = 4 * e + i
                    if not isinstance(e, int) or n > 1:
                        pe.wait_ge(copied, n - 1)
                    for j in range(2):
                        for k in range(2):
                            last = pe.transpose(PS[:, i % 2, (2 * j + k) * P:(2 * j + k + 1) * P],
                                                XB[:, u, 2 * i + j, k * P:(k + 1) * P], ident[:, :])
                    last.then_inc(turned, 1)

            def widen(e, u):
                pe.wait_ge(copied, 4 * e + 4)
                for c, (at, n) in enumerate(CH):
                    for f in range(KF):
                        i = 2 * KF * e + KF * c + f
                        if not isinstance(e, int) or i > 1:
                            pe.wait_ge(relu, i - 1)
                        for k in range(2):
                            last = pe.matmul(PS[:, 2 + f % 2, 0:n], w1[:, u, k, f * P:(f + 1) * P], XT[:, k, at:at + n],
                                             start=k == 0, stop=k == 1)
                        last.then_inc(up, 1)

            def narrow(e, u):
                for j in range(CT):
                    i = CT * e + j
                    pe.wait_ge(relu, 2 * KF * e + (KF if j < 4 else 2 * KF))
                    if not isinstance(e, int) or i > 1:
                        pe.wait_ge(y_ready, i - 1)
                    for f in range(KF):
                        last = pe.matmul(PS[0:rows_of(j), 4 + j % 2, 0:D], HT[:, f, j * P:j * P + rows_of(j)], w2[:, u, f, :],
                                         start=f == 0, stop=f == KF - 1)
                    last.then_inc(down, 1)

            turn(0, 0)
            widen(0, 0)
            turn(1, 1)
            narrow(0, 0)
            for e, u in tiles(pe, 1, EXPERTS - 1, 2):
                widen(e, u)
                turn(e + 1, 1 - u)
                narrow(e, u)
            e = EXPERTS - 1
            widen(e, e % 2)
            narrow(e, e % 2)

        @block.scalar
        def _(act):
            for e, u in tiles(act, 0, EXPERTS, 2):
                for c, (at, n) in enumerate(CH):
                    for f in range(KF):
                        act.wait_ge(up, 2 * KF * e + KF * c + f + 1)
                        act.activation(HT[:, f, at:at + n], PS[:, 2 + f % 2, 0:n], ACT.Relu, bias=c1[:, u, f:f + 1]).then_inc(relu, 1)

        @block.vector
        def _(dve):
            def copy(e):
                for i in range(4):
                    dve.wait_ge(turned, 4 * e + i + 1)
                    dve.tensor_copy(XT[:, :, 2 * i * P:2 * (i + 1) * P].rearrange("p k (j q) -> p j k q", j=2),
                                    PS[:, i % 2, :].rearrange("p (j k q) -> p j k q", j=2, k=2)).then_inc(copied, 1)

            def finish(e, u):
                dve.wait_ge(stored[u], (e - u) * 16 + 32)
                for j in range(CT):
                    n = rows_of(j)
                    dve.wait_ge(down, CT * e + j + 1)
                    dve.tensor_tensor(YS[0:n, u, j, :], PS[0:n, 4 + j % 2, 0:D], c2[0:n, u, :], ALU.add).then_inc(y_ready, 1)

            for u in range(2):
                dve.sem_inc(stored[u], 32)
            copy(0)
            copy(1)
            finish(0, 0)
            for e, u in tiles(dve, 1, EXPERTS - 1, 2):
                copy(e + 1)
                finish(e, u)
            finish(EXPERTS - 1, (EXPERTS - 1) % 2)


def combine(nc, allocator, dev, X1, weight, take):
    ybuf, out = dev["ybuf"], dev["out"]
    with ExitStack() as st:
        sb, sem = allocator(st)
        YG = sb("YG", [P, 4, D])
        idx = sb("takex", [P, 4], I32)
        C = sb("C", [P, 2, D])
        number = sb("number", [P, 2, D], I32)
        finite = sb("finite", [P, 2, D], I32)
        OT = sb("OT", [P, 2, D])
        staged, released, own, taken, o_ready = (sem("c_" + n) for n in ("staged", "released", "own", "taken", "o_ready"))
        passed = sem("c_passed")
        fetched = [sem(f"c_fetched{r}") for r in range(4)]
        stored = [sem(f"c_stored{u}") for u in range(2)]
        block = st.enter_context(nc.Block())

        @block.scalar
        def _(act):
            for t, r in ring4(act):
                if not isinstance(t, int) or t >= 4:
                    act.wait_ge(fetched[r], rounds(t, r, 4) - 16)
                act.activation(idx[:, r:r + 1], take[:, bass.ds(t, 1)], ACT.Copy).then_inc(staged, 1)

        @block.gpsimd
        def _(pool):
            pool.sem_inc(taken, 4)
            for t, r in tiles(pool, 0, TILES, 4):
                pool.wait_ge(staged, t + 1)
                pool.wait_ge(taken, t + 1)
                pool.sem_inc(released, 1)
                pool.indirect_dma_start(YG[:, r, :], None, ybuf, IndexOn(ap=idx[:, r:r + 1], axis=0)).then_inc(fetched[r], 16)

        @block.vector
        def _(dve):
            own_ = Chain(dve, own)
            for t, r in tiles(dve, 0, TILES, 4):
                u = r % 2
                own_.at(5 * t)
                y, c, o = YG[:, r, :], C[:, u, :], OT[:, u, :]
                dve.wait_ge(stored[u], rounds(t, u))
                dve.wait_ge(fetched[r], rounds(t, r, 4))
                own_.link(dve.tensor_scalar(y, y, weight[:, bass.ds(t, 1)], None, ALU.mult))
                dve.tensor_scalar(c, y, -10000.0, 10000.0, ALU.max, ALU.min)
                dve.tensor_tensor(number[:, u, :], y, y, ALU.is_equal)
                dve.tensor_scalar(finite[:, u, :], y, 0.0, 0.0, ALU.mult, ALU.is_equal)
                own_.link(dve.memset(o, 0.0))
                dve.sem_inc(passed, 1)
                own_.link(dve.copy_predicated(o, number[:, u, :], c))
                dve.sem_inc(passed, 1)
                own_.link(dve.copy_predicated(o, finite[:, u, :], y))
                own_.link(dve.tensor_tensor(o, o, X1[:, bass.ds(t, 1), :].rearrange("p a b -> p (a b)"), ALU.add))
                dve.sem_inc(taken, 1)
                dve.sem_inc(o_ready, 1)
                own_.closed(5)

        @block.sync
        def _(sp):
            for u in range(2):
                sp.sem_inc(stored[u], 16)
            for t, u in tiles(sp, 0, TILES - 1, 2):
                sp.wait_ge(o_ready, t + 1)
                sp.dma_start(out[bass.ds(t * P, P), :], OT[:, u, :]).then_inc(stored[u], 16)
            t = TILES - 1
            sp.wait_ge(o_ready, TILES)
            sp.dma_start(out[t * P:N, :], OT[0:LAST, t % 2, :]).then_inc(stored[t % 2], 16)
            for u in range(2):
                sp.wait_ge(stored[u], 16 + 16 * len(range(u, TILES, 2)))


INS = ["x", "src", "dst", "L0_gnn_ln_w", "L0_gnn_ln_b", "L0_gnn_W1", "L0_gnn_att_src1", "L0_gnn_att_dst1",
       "L0_gnn_b1", "L0_gnn_W2", "L0_gnn_att_src2", "L0_gnn_att_dst2", "L0_gnn_b2", "L0_mix_w_qkv",
       "L0_mix_mem_kv", "L0_mix_w_out", "L0_mix_b_out", "L0_mix_g_out", "L0_mix_g_pre", "L0_ffn_gate_w",
       "L0_ffn_gate_b", "L0_ffn_w1", "L0_ffn_b1", "L0_ffn_w2", "L0_ffn_b2"]


def laid_out(inputs):
    import numpy as np

    arrays = {}
    for name in INS:
        a = np.ascontiguousarray(inputs[name])
        if name in ("src", "dst"):
            fill = np.full(GROUPS * GROUP - E, 0 if name == "src" else NP - 1, a.dtype)
            a = np.concatenate([a, fill]).reshape(GROUPS, GROUP)
        arrays[f"in_{name}"] = a
    return arrays


def kernel(**inputs):
    import numpy as np
    import concourse.bacc as bacc
    from concourse.bass_utils import run_bass_kernel_spmd

    nc = bacc.Bacc("TRN2", target_bir_lowering=False, num_devices=1)
    arrays = laid_out(inputs)
    args = [nc.dram_tensor(n, a.shape, mybir.dt.from_np(a.dtype), kind="ExternalInput").ap() for n, a in arrays.items()]
    out = nc.dram_tensor("out", [N, D], F32, kind="ExternalOutput").ap()
    gps_program(nc, *args, out)
    got = run_bass_kernel_spmd(nc, [arrays], core_ids=[0])
    return np.asarray(got.results[0]["out"])
```

```python
from contextlib import ExitStack

import concourse.bass as bass
from concourse import mybir

F32 = mybir.dt.float32
I32 = mybir.dt.int32
BF16 = mybir.dt.bfloat16
ALU = mybir.AluOpType
ACT = mybir.ActivationFunctionType
X = mybir.AxisListType.X
RMAX = bass.bass_isa.ReduceOp.max
IndexOn = bass.IndirectOffsetOnAxis

P = 128
N, D = 6250, 256
TILES = -(-N // P)
NP = TILES * P
LAST = N - (TILES - 1) * P
E = 106250
GROUP = 2 * P
GROUPS = -(-E // GROUP)
STEPS = GROUPS + TILES - 1
SLOTS = 2 * STEPS
KT = -(-STEPS // P)
H1, C1 = 8, 64
F1 = H1 * C1
HALF = 4 * C1 + 4
ROW1 = 2 * HALF
ROW2 = D + 2
SLOPE = 0.2
EPS = 1e-5
SPREAD = 60.0
BIG = 2.0 ** 100
MH, MD, MEM = 4, 32, 4
QK = MH * MD
KCH = -(-N // 512)
EXPERTS, FF = 8, 1024
CAP = -(-5 * N // (4 * EXPERTS))
CT = -(-CAP // P)


def tiles(eng, first, last, unroll):
    whole = (last - first) // unroll
    if whole > 1:
        with eng.Fori(0, whole) as i:
            for u in range(unroll):
                yield i * unroll + (first + u), (first + u) % unroll
    else:
        whole = 0
    for s in range(first + whole * unroll, last):
        yield s, s % unroll


def turns(eng, first, last, ring):
    whole = (last - first) // ring
    with eng.Fori(0, whole) as i:
        for u in range(ring):
            yield i * ring + (first + u), (first + u) % ring, i + (first + u) // ring
    for s in range(first + whole * ring, last):
        yield s, s % ring, s // ring


def ring4(eng):
    yield from ((t, t) for t in range(4))
    yield from tiles(eng, 4, TILES, 4)


class Chain:

    def __init__(self, eng, sem):
        self.eng, self.sem, self.base, self.n = eng, sem, 0, 0

    def at(self, base):
        self.base, self.n = base, 0

    def link(self, ins):
        self.n += 1
        ins.then_inc(self.sem, 1)
        self.eng.wait_ge(self.sem, self.base + self.n)

    def closed(self, per_step):
        assert self.n == per_step, self.n


def one(ap, axis, n):
    shape = list(ap.shape)
    shape.insert(axis, n)
    return ap.unsqueeze(axis).to_broadcast(shape)


def gps_program(nc, x, src, dst, ln_w, ln_b, W1, att_s1, att_d1, b1, W2, att_s2, att_d2, b2,
                w_qkv, mem_kv, w_out, b_out, g_out, g_pre,
                gate_w, gate_b, ew1, eb1, ew2, eb2, out):
    root = ExitStack()
    with root:
        def dram(name, shape):
            return nc.dram_tensor(name, shape, F32).ap()

        table1 = dram("table1", [NP, ROW1])
        table2 = dram("table2", [NP, ROW2])
        resid = dram("resid", [NP, D])
        xbuf = dram("xbuf", [EXPERTS * CT * P, D])
        ybuf = dram("ybuf", [EXPERTS * CAP, D])

        taken = []

        def recycle():
            nc.all_engine_barrier()
            nc.clear_and_free_semaphores(taken)
            taken.clear()
            nc.all_engine_barrier()

        def allocator(stack):
            def sb(name, shape, dt=F32):
                return stack.enter_context(nc.sbuf_tensor(name, shape, dt))

            def sem(name):
                taken.append(nc.alloc_semaphore(name=name))
                return taken[-1]
            return sb, sem

        sb, sem = allocator(root)
        PS = root.enter_context(nc.psum_tensor("PS", [P, 8, 512], F32))
        ident = sb("ident", [P, P])
        iota_row = sb("iota_row", [P, P])
        ones = sb("ones", [P, P])
        mean = sb("mean", [P, TILES])
        rstd = sb("rstd", [P, TILES])
        SRC = sb("SRC", [P, SLOTS], I32)
        DST = sb("DST", [P, SLOTS])
        TK = sb("TK", [1, KT * P], I32)
        AD1 = sb("AD1", [P, TILES, 16])
        AD2 = sb("AD2", [P, TILES, 2])
        dev = locals()

        edge_tables(nc, allocator, dev)
        node_phase(nc, allocator, dev)
        with ExitStack() as mid:
            sb1, _ = allocator(mid)
            ADM = sb1("ADM1", [P, TILES, 2 * H1])
            SELF = sb1("SELF1", [P, TILES, H1])
            ACC = sb1("ACC1", [P, TILES, ROW1])
            bounds(nc, allocator, dev, LAYER1, table1, AD1, ADM, SELF, ACC)
            walk(nc, allocator, dev, LAYER1, table1, ADM, ACC)
            between(nc, allocator, dev, ACC, SELF, AD2)
        X1 = sb("X1", [P, TILES, D])
        bn1 = sb("bn1", [P, TILES, 6])
        with ExitStack() as mid:
            sb2, _ = allocator(mid)
            ADM = sb2("ADM2", [P, TILES, 2])
            SELF = sb2("SELF2", [P, TILES, 1])
            ACC = sb2("ACC2", [P, TILES, D + 1])
            bounds(nc, allocator, dev, LAYER2, table2, AD2, ADM, SELF, ACC)
            walk(nc, allocator, dev, LAYER2, table2, ADM, ACC)
            residual(nc, allocator, dev, ACC, SELF, X1, bn1)
        recycle()
        m1 = sb("m1", [P, TILES])
        r1 = sb("r1_", [P, TILES])
        weight = sb("weight", [P, TILES])
        put = sb("put", [P, TILES], I32)
        take = sb("take", [P, TILES], I32)
        with ExitStack() as mid:
            LG = allocator(mid)[0]("LG", [P, TILES, EXPERTS])
            gate(nc, allocator, dev, X1, bn1, m1, r1, LG)
            route(nc, allocator, dev, LG, weight, put, take)
        dispatch(nc, allocator, dev, X1, m1, r1, put)
        ysum = sb("ysum", [P, EXPERTS * CT])
        experts(nc, allocator, dev, ysum)
        combine(nc, allocator, dev, X1, weight, take, ysum)
        return dev


def edge_tables(nc, allocator, dev):
    PS, ident, iota_row, ones, SRC, DST, TK = (dev[k] for k in (
        "PS", "ident", "iota_row", "ones", "SRC", "DST", "TK"))
    src, dst = dev["src"], dev["dst"]
    with ExitStack() as st:
        sb, sem = allocator(st)
        last_i = sb("last_i", [1, GROUPS], I32)
        tile_i = sb("tile_i", [1, GROUPS], I32)
        tile_f = sb("tile_f", [1, GROUPS])
        grp = sb("grp", [P, GROUPS])
        leave = sb("leave", [P, GROUPS])
        junk = sb("junk", [P, GROUPS])
        step_f = sb("step_f", [P, KT])
        c_f = sb("c_f", [P, KT])
        c_i = sb("c_i", [P, KT], I32)
        t_f = sb("t_f", [P, KT])
        first_f = sb("first_f", [P, KT])
        SE = sb("SE", [P, KT, GROUP], I32)
        DE = sb("DE", [P, KT, GROUP], I32)
        SF = sb("SF", [P, KT, GROUP])
        DF = sb("DF", [P, KT, GROUP])
        ends_loaded = sem("ends_loaded")
        zeroed, consts = sem("zeroed"), sem("consts")
        own = sem("edge_vector_own")
        tiles_ready, tiles_spread = sem("tiles_ready"), sem("tiles_spread")
        groups_ready, edges_in, edges_float = sem("groups_ready"), sem("edges_in"), sem("edges_float")
        turned, copied = sem("turned"), sem("turned_copied")

        block = st.enter_context(nc.Block())

        @block.sync
        def _(sp):
            with nc.allow_non_contiguous_dma(reason="one destination per group"):
                sp.dma_start(last_i[:, :], dst[:, GROUP - 1:GROUP].rearrange("g a -> a g")).then_inc(ends_loaded, 16)

        @block.gpsimd
        def _(pool):
            pool.memset(ident[:, :], 0.0).then_inc(zeroed, 1)
            pool.memset(ones[:, :], 1.0).then_inc(consts, 1)
            pool.iota(iota_row[:, :], [[1, P]], base=0, channel_multiplier=0,
                      allow_small_or_imprecise_dtypes=True).then_inc(consts, 1)
            pool.iota(grp[:, :], [[1, GROUPS]], base=0, channel_multiplier=0,
                      allow_small_or_imprecise_dtypes=True).then_inc(consts, 1)
            pool.iota(step_f[:, :], [[P, KT]], base=0, channel_multiplier=1,
                      allow_small_or_imprecise_dtypes=True).then_inc(consts, 1)
            pool.wait_ge(zeroed, 1)
            pool.affine_select(out=ident[:, :], in_=ident[:, :], compare_op=ALU.not_equal, fill=1.0,
                               base=0, pattern=[[-1, P]], channel_multiplier=1).then_inc(consts, 1)
            pool.wait_ge(groups_ready, 1)
            for k in range(KT):
                pool.indirect_dma_start(SE[:, k, :], None, src, IndexOn(ap=c_i[:, k:k + 1], axis=0)).then_inc(edges_in, 16)
                pool.indirect_dma_start(DE[:, k, :], None, dst, IndexOn(ap=c_i[:, k:k + 1], axis=0)).then_inc(edges_in, 16)

        @block.vector
        def _(dve):
            own_ = Chain(dve, own)
            dve.wait_ge(ends_loaded, 16)
            own_.link(dve.tensor_scalar(tile_i[:, :], last_i[:, :], 7, None, ALU.arith_shift_right))
            dve.tensor_copy(tile_f[:, :], tile_i[:, :]).then_inc(tiles_ready, 1)
            dve.wait_ge(tiles_spread, 1)
            dve.wait_ge(consts, 5)
            own_.link(dve.tensor_tensor(leave[:, :], PS[:, 0, 0:GROUPS], grp[:, :], ALU.add))
            for k in range(KT):
                own_.link(dve.tensor_scalar(junk[:, :], leave[:, :], step_f[:, k:k + 1], None, ALU.is_lt,
                                            ALU.add, accum_out=c_f[:, k:k + 1]))
            own_.link(dve.tensor_scalar(c_f[:, :], c_f[:, :], float(GROUPS - 1), None, ALU.min))
            own_.link(dve.tensor_tensor(t_f[:, :], step_f[:, :], c_f[:, :], ALU.subtract))
            own_.link(dve.tensor_scalar(t_f[:, :], t_f[:, :], float(TILES - 1), None, ALU.min))
            own_.link(dve.tensor_scalar(first_f[:, :], t_f[:, :], float(P), None, ALU.mult))
            dve.tensor_copy(c_i[:, :], c_f[:, :]).then_inc(groups_ready, 1)
            dve.wait_ge(edges_in, 32 * KT)
            own_.link(dve.tensor_copy(SF[:, :, :], SE[:, :, :]))
            own_.link(dve.tensor_copy(DF[:, :, :], DE[:, :, :]))
            for k in range(KT):
                own_.link(dve.tensor_scalar(DF[:, k, :], DF[:, k, :], first_f[:, k:k + 1], None, ALU.subtract))
            dve.engine_nop().then_inc(edges_float, 1)
            for k in range(KT):
                n = min(P, STEPS - k * P)
                dve.wait_ge(turned, k + 1)
                part = slice(2 * k * P, 2 * (k * P + n))
                dve.tensor_copy(SRC[:, part].rearrange("p (k h) -> p h k", h=2), PS[:, k % 2, 0:256].rearrange("p (h k) -> p h k", h=2)[:, :, 0:n])
                dve.tensor_copy(DST[:, part].rearrange("p (k h) -> p h k", h=2), PS[:, k % 2, 256:512].rearrange("p (h k) -> p h k", h=2)[:, :, 0:n]).then_inc(copied, 1)
            dve.wait_ge(turned, KT + 1)
            dve.tensor_copy(TK[:, :], PS[0:1, 2, 0:KT * P])

        @block.tensor
        def _(pe):
            pe.wait_ge(consts, 5)
            pe.wait_ge(tiles_ready, 1)
            pe.matmul(PS[:, 0, 0:GROUPS], ones[0:1, :], tile_f[:, :], start=True, stop=True).then_inc(tiles_spread, 1)
            pe.wait_ge(edges_float, 1)
            for k in range(KT):
                if k >= 2:
                    pe.wait_ge(copied, k - 1)
                for j, half in ((0, SF[:, k, 0:P]), (1, SF[:, k, P:GROUP]), (2, DF[:, k, 0:P]), (3, DF[:, k, P:GROUP])):
                    last = pe.transpose(PS[:, k % 2, j * P:(j + 1) * P], half, ident[:, :])
                last.then_inc(turned, 1)
            for k in range(KT):
                last = pe.transpose(PS[0:1, 2, k * P:(k + 1) * P], t_f[:, k:k + 1], ident[:, :])
            last.then_inc(turned, 1)


def node_phase(nc, allocator, dev):
    PS, ident, ones, mean, rstd, AD1 = (dev[k] for k in ("PS", "ident", "ones", "mean", "rstd", "AD1"))
    with ExitStack() as outer:
        sb, _ = allocator(outer)
        xt = sb("xt", [P, TILES, D])
        QT = sb("QT", [P, NP])
        V = sb("V", [P, TILES, QK])
        KE = sb("KE", [P, N + MEM])
        with ExitStack() as inner:
            sb, _ = allocator(inner)
            WA = sb("WA", [P, 2, ROW1 + 16])
            WQ = sb("WQ", [P, 2, 3 * QK])
            BA = sb("BA", [P, ROW1 + 16])
            unit = sb("unit", [P, TILES])
            back = sb("back", [P, TILES])
            fold_weights(nc, allocator, dev, WA, WQ, BA, KE, V, xt)
            normalise(nc, allocator, dev, xt, unit, back)
            project(nc, allocator, dev, xt, WA, WQ, BA, unit, back, QT, V, KE)
        mixer(nc, allocator, dev, xt, QT, V, KE)


def fold_weights(nc, allocator, dev, WA, WQ, BA, KE, V, xt):
    PS, ones = dev["PS"], dev["ones"]
    W1, w_qkv, mem_kv, x = dev["W1"], dev["w_qkv"], dev["mem_kv"], dev["x"]
    with ExitStack() as st:
        sb, sem = allocator(st)
        att = sb("att", [P, 2, F1])
        lw = sb("lw", [P, 2])
        lb = sb("lb", [P, 2])
        gp = sb("gp", [P, 2])
        prod = sb("prod", [P, 2, F1])
        lbw = sb("lbw", [P, 2, P])
        w1_in, rest_in, x_in = sem("w1_in"), sem("rest_in"), sem("x_in")
        own, bias_cols, bias_done = sem("fold_own"), sem("bias_cols"), sem("bias_done")
        block = st.enter_context(nc.Block())

        @block.sync
        def _(sp):
            with nc.allow_non_contiguous_dma(reason="small vectors"):
                for k in range(2):
                    for a in range(2):
                        sp.dma_start(WA[:, k, a * HALF:a * HALF + 256],
                                     W1[k * P:(k + 1) * P, a * 256:(a + 1) * 256]).then_inc(w1_in, 16)
                for j, v in enumerate((dev["att_s1"], dev["att_d1"])):
                    sp.dma_start(att[:, j, :], v.rearrange("h c -> (h c)").partition_broadcast(P)).then_inc(w1_in, 16)
                for tile, v in ((lw, dev["ln_w"]), (lb, dev["ln_b"]), (gp, dev["g_pre"])):
                    sp.dma_start(tile[:, :], v.rearrange("(k p) -> p k", p=P)).then_inc(rest_in, 16)
                sp.dma_start(WQ[:, :, :], w_qkv.rearrange("(k p) n -> p k n", p=P)).then_inc(rest_in, 16)
                sp.dma_start(KE[:, N:N + MEM], mem_kv[0].rearrange("h d m -> (h d) m")).then_inc(rest_in, 16)
                for h in range(MH):
                    sp.dma_start(V[LAST:LAST + MEM, TILES - 1, h * MD:(h + 1) * MD],
                                 mem_kv[1, h].rearrange("d m -> m d")).then_inc(rest_in, 16)
            for c in range(6):
                sp.dma_start(xt[:, 8 * c:8 * (c + 1), :],
                             x[8 * c * P:8 * (c + 1) * P, :].rearrange("(t p) n -> p t n", p=P)).then_inc(x_in, 16)
            sp.wait_ge(own, 1)
            sp.dma_start(xt[0:LAST, TILES - 1, :], x[(TILES - 1) * P:N, :]).then_inc(x_in, 16)
            sp.wait_ge(x_in, 7 * 16)
            sp.wait_ge(rest_in, 9 * 16)

        @block.vector
        def _(dve):
            own_ = Chain(dve, own)
            own_.link(dve.memset(xt[:, TILES - 1, :], 0.0))
            dve.wait_ge(w1_in, 6 * 16)
            cols = [WA[:, k, 0:ROW1].rearrange("p (a b) -> p a b", a=2) for k in range(2)]
            for k in range(2):
                for j in range(2):
                    own_.link(dve.tensor_tensor(prod[:, j, :].rearrange("p (a b) -> p a b", a=2), cols[k][:, :, 0:256],
                                                att[:, j, :].rearrange("p (a b) -> p a b", a=2), ALU.mult))
                    own_.link(dve.tensor_reduce(WA[:, k, ROW1 + 8 * j:ROW1 + 8 * j + 8],
                                                prod[:, j, :].rearrange("p (h c) -> p h c", c=C1), X, ALU.add))
                own_.link(dve.tensor_copy(cols[k][:, :, 256:260], WA[:, k, ROW1:ROW1 + 8].rearrange("p (a b) -> p a b", a=2)))
            dve.wait_ge(rest_in, 9 * 16)
            for k in range(2):
                own_.link(dve.tensor_scalar(lbw[:, k, :], ones[:, :], lb[:, k:k + 1], None, ALU.mult))
            dve.engine_nop().then_inc(bias_cols, 1)
            dve.wait_ge(bias_done, 1)
            half = (ROW1 + 16) // 2
            for a in range(2):
                own_.link(dve.tensor_copy(BA[:, a * half:(a + 1) * half], PS[:, a, 0:half]))
            for k in range(2):
                own_.link(dve.tensor_scalar(WA[:, k, :], WA[:, k, :], lw[:, k:k + 1], None, ALU.mult))
                own_.link(dve.tensor_scalar(WQ[:, k, :], WQ[:, k, :], gp[:, k:k + 1], None, ALU.mult))

        @block.tensor
        def _(pe):
            half = (ROW1 + 16) // 2
            pe.wait_ge(bias_cols, 1)
            for a in range(2):
                for k in range(2):
                    last = pe.matmul(PS[:, a, 0:half], lbw[:, k, :], WA[:, k, a * half:(a + 1) * half],
                                     start=k == 0, stop=k == 1)
            last.then_inc(bias_done, 1)


def normalise(nc, allocator, dev, xt, unit, back):
    PS, ident, mean, rstd = dev["PS"], dev["ident"], dev["mean"], dev["rstd"]
    with ExitStack() as st:
        sb, sem = allocator(st)
        bn = sb("bn", [P, TILES, 6])
        va = sb("va", [P, TILES])
        v2 = sb("v2", [P, TILES])
        ta = sb("ta", [P, TILES])
        tb = sb("tb", [P, TILES])
        own, to_root, rooted = sem("norm_own"), sem("to_root"), sem("rooted")
        block = st.enter_context(nc.Block())

        @block.vector
        def _(dve):
            own_ = Chain(dve, own)
            for t, u in tiles(dve, 0, TILES, 4):
                last = dve.bn_stats(bn[:, bass.ds(t, 1), :].rearrange("p a b -> p (a b)"),
                                    xt[:, bass.ds(t, 1), :].rearrange("p a b -> p (a b)"))
            own_.link(last)
            moments(dve, own_, bn, mean, va, ta)
            own_.link(dve.tensor_scalar(ta[:, :], va[:, :], EPS, None, ALU.add))
            dve.engine_nop().then_inc(to_root, 1)
            dve.wait_ge(rooted, 1)
            own_.link(dve.reciprocal(rstd[:, :], ta[:, :]))
            own_.link(dve.tensor_tensor(v2[:, :], rstd[:, :], rstd[:, :], ALU.mult))
            own_.link(dve.tensor_tensor(v2[:, :], v2[:, :], va[:, :], ALU.mult))
            own_.link(dve.tensor_scalar(ta[:, :], v2[:, :], EPS, None, ALU.add))
            own_.link(dve.tensor_scalar(tb[:, :], v2[:, :], float(D), None, ALU.mult))
            dve.engine_nop().then_inc(to_root, 1)
            dve.wait_ge(rooted, 3)
            own_.link(dve.tensor_scalar(tb[:, :], tb[:, :], 1e-12, 1.0 / 16.0, ALU.max, ALU.mult))
            own_.link(dve.reciprocal(unit[:, :], tb[:, :]))
            own_.link(dve.tensor_tensor(unit[:, :], unit[:, :], rstd[:, :], ALU.mult))
            own_.link(dve.reciprocal(ta[:, :], ta[:, :]))
            own_.link(dve.tensor_tensor(back[:, :], tb[:, :], ta[:, :], ALU.mult))

        @block.scalar
        def _(act):
            act.wait_ge(to_root, 1)
            act.activation(ta[:, :], ta[:, :], ACT.Sqrt).then_inc(rooted, 1)
            act.wait_ge(to_root, 2)
            act.activation(ta[:, :], ta[:, :], ACT.Sqrt).then_inc(rooted, 1)
            act.activation(tb[:, :], tb[:, :], ACT.Sqrt).then_inc(rooted, 1)


def moments(dve, own_, bn, mean, va, ta):
    me, mo, ve, vo = bn[:, :, 1], bn[:, :, 4], bn[:, :, 2], bn[:, :, 5]
    own_.link(dve.tensor_tensor(mean[:, :], me, mo, ALU.add))
    own_.link(dve.tensor_scalar(mean[:, :], mean[:, :], 0.5, None, ALU.mult))
    own_.link(dve.tensor_tensor(ta[:, :], me, mo, ALU.subtract))
    own_.link(dve.tensor_tensor(ta[:, :], ta[:, :], ta[:, :], ALU.mult))
    own_.link(dve.tensor_tensor(va[:, :], ve, vo, ALU.add))
    own_.link(dve.tensor_scalar(va[:, :], va[:, :], 1.0 / D, None, ALU.mult))
    own_.link(dve.tensor_scalar(ta[:, :], ta[:, :], 0.25, None, ALU.mult))
    own_.link(dve.tensor_tensor(va[:, :], va[:, :], ta[:, :], ALU.add))


def project(nc, allocator, dev, xt, WA, WQ, BA, unit, back, QT, V, KE):
    PS, ident, AD1, table1, mean = (dev[k] for k in ("PS", "ident", "AD1", "table1", "mean"))
    with ExitStack() as st:
        sb, sem = allocator(st)
        Y = sb("Y", [P, 4, D])
        YT = sb("YT", [P, 4, 2, P])
        row = sb("row", [P, 2, ROW1])
        q = sb("q", [P, 2, QK])
        qm = sb("qm", [P, 2, MH])
        qs = sb("qs", [P, 2, MH])
        y_ready, y_turned, y_copied = sem("y_ready"), sem("y_turned"), sem("y_copied")
        tile_done = sem("tile_done")
        rows_ready = sem("rows_ready")
        rows_stored = [sem(f"rows_stored{u}") for u in range(2)]
        max_own, norm_own = sem("qmax_own"), sem("qnorm_own")
        q_ready, q_exp, q_normed = sem("q_ready"), sem("q_exp"), sem("q_normed")
        vk_copied, q_turned, q_copied = sem("vk_copied"), sem("q_turned"), sem("q_copied")
        block = st.enter_context(nc.Block())

        @block.tensor
        def _(pe):
            def turn_y(t, u):
                pe.wait_ge(y_ready, t + 1)
                pe.wait_ge(y_copied, t + 1)
                for k in range(2):
                    last = pe.transpose(PS[:, 6, k * P:(k + 1) * P], Y[:, u, k * P:(k + 1) * P], ident[:, :])
                last.then_inc(y_turned, 1)

            def tile(t, u):
                pe.wait_ge(y_copied, t + 2)
                pe.wait_ge(q_ready, t + 1)
                pe.wait_ge(vk_copied, t + 1)
                for k in range(2):
                    pe.matmul(PS[:, 3 * (u % 2), 0:HALF], YT[:, u, k, :], WA[:, k, 0:HALF], start=k == 0, stop=k == 1)
                for k in range(2):
                    pe.matmul(PS[:, 3 * (u % 2) + 1, 0:HALF + 16], YT[:, u, k, :], WA[:, k, HALF:ROW1 + 16], start=k == 0, stop=k == 1)
                for k in range(2):
                    pe.matmul(PS[:, 3 * (u % 2) + 2, 0:2 * QK].rearrange("p (a b) -> p a b", b=QK), YT[:, u, k, :],
                              WQ[:, k, :].rearrange("p (a b) -> p a b", b=QK)[:, 0:3:2, :], start=k == 0, stop=k == 1)
                for k in range(2):
                    last = pe.matmul(PS[:, 3 * (u % 2) + 2, 2 * QK:2 * QK + P], WQ[:, k, QK:2 * QK], YT[:, u, k, :],
                                     start=k == 0, stop=k == 1)
                last.then_inc(tile_done, 1)

            def turn_q(t, u):
                pe.wait_ge(q_normed, t + 1)
                pe.wait_ge(q_copied, t + 1)
                pe.transpose(PS[:, 7, 0:P], q[:, u % 2, :], ident[:, :]).then_inc(q_turned, 1)

            for free in (q_ready, vk_copied):
                pe.sem_inc(free, 2)
            for free in (y_copied, q_copied):
                pe.sem_inc(free, 1)
            turn_y(0, 0)
            turn_y(1, 1)
            for t in range(2):
                tile(t, t)
                turn_y(t + 2, t + 2)
            for t, u in tiles(pe, 2, TILES - 2, 4):
                tile(t, u)
                turn_y(t + 2, (u + 2) % 4)
                turn_q(t - 2, u)
            for t in (TILES - 2, TILES - 1):
                tile(t, t % 4)
                turn_q(t - 2, t % 2)
            for t in (TILES - 2, TILES - 1):
                turn_q(t, t % 2)

        @block.vector
        def _(dve):
            mx, nm = Chain(dve, max_own), Chain(dve, norm_own)

            def rms(t, u):
                dve.wait_ge(y_turned, t + 1)
                dve.tensor_scalar(Y[:, u, :], xt[:, bass.ds(t, 1), :].rearrange("p a b -> p (a b)"),
                                  mean[:, bass.ds(t, 1)], unit[:, bass.ds(t, 1)], ALU.subtract, ALU.mult).then_inc(y_ready, 1)

            def first(t, u):
                u = u % 2
                mx.at(t)
                dve.wait_ge(tile_done, t + 1)
                dve.wait_ge(rows_stored[u], rounds(t, u))
                g = back[:, bass.ds(t, 1)]
                dve.scalar_tensor_tensor(row[:, u, :].rearrange("p (a b) -> p a b", a=2), PS[:, 3 * u:3 * u + 2, 0:HALF], g,
                                         BA[:, 0:ROW1].rearrange("p (a b) -> p a b", a=2), ALU.mult, ALU.add).then_inc(rows_ready, 1)
                dve.scalar_tensor_tensor(AD1[:, bass.ds(t, 1), :].rearrange("p a b -> p (a b)"), PS[:, 3 * u + 1, HALF:HALF + 16], g,
                                         BA[:, ROW1:ROW1 + 16], ALU.mult, ALU.add)
                qq = PS[:, 3 * u + 2, 0:QK].rearrange("p (h d) -> p h d", h=MH)
                mx.link(dve.tensor_reduce(qm[:, u, :], qq, X, ALU.max))
                dve.wait_ge(q_turned, t + 1)
                dve.tensor_tensor(q[:, u, :].rearrange("p (h d) -> p h d", h=MH), qq, one(qm[:, u, :], 2, MD),
                                  ALU.subtract).then_inc(q_ready, 1)

            def second(t, u):
                u = u % 2
                nm.at(t * 2)
                qv = q[:, u, :].rearrange("p (h d) -> p h d", h=MH)
                dve.wait_ge(q_exp, t + 1)
                nm.link(dve.tensor_reduce(qs[:, u, :], qv, X, ALU.add))
                nm.link(dve.reciprocal(qs[:, u, :], qs[:, u, :]))
                dve.tensor_tensor(qv, qv, one(qs[:, u, :], 2, MD), ALU.mult).then_inc(q_normed, 1)

            dve.sem_inc(y_turned, 4)
            dve.sem_inc(q_turned, 2)
            for t in range(4):
                rms(t, t)
            first(0, 0)
            for t, u in tiles(dve, 1, TILES - 3, 4):
                rms(t + 3, (u + 3) % 4)
                first(t, u)
                second(t - 1, (u + 3) % 4)
            for t in range(TILES - 3, TILES):
                first(t, t)
                second(t - 1, t - 1)
            second(TILES - 1, TILES - 1)

        @block.scalar
        def _(act):
            def copy_y(t, u):
                act.wait_ge(y_turned, t + 5)
                if not isinstance(t, int) or t > 3:
                    act.wait_ge(tile_done, t - 3)
                act.activation(YT[:, u, :, :], PS[:, 6, 0:2 * P].rearrange("p (k q) -> p k q", k=2), ACT.Copy).then_inc(y_copied, 1)

            def first(t, u, rows=P):
                u = u % 2
                act.wait_ge(q_ready, t + 3)
                act.activation(q[:, u, :], q[:, u, :], ACT.Exp).then_inc(q_exp, 1)
                act.activation(KE[:, bass.ds(t * P, rows)], PS[:, 3 * u + 2, 2 * QK:2 * QK + rows], ACT.Copy)
                act.activation(V[0:rows, bass.ds(t, 1), :].rearrange("p a b -> p (a b)"), PS[0:rows, 3 * u + 2, QK:2 * QK],
                               ACT.Copy).then_inc(vk_copied, 1)

            def second(t, u):
                act.wait_ge(q_turned, t + 3)
                act.activation(QT[:, bass.ds(t * P, P)], PS[:, 7, 0:P], ACT.Copy).then_inc(q_copied, 1)

            copy_y(0, 0)
            copy_y(1, 1)
            for t in range(2):
                copy_y(t + 2, t + 2)
                first(t, t)
            for t, u in tiles(act, 2, TILES - 2, 4):
                copy_y(t + 2, (u + 2) % 4)
                first(t, u)
                second(t - 2, u)
            for t in (TILES - 2, TILES - 1):
                first(t, t, P if t < TILES - 1 else LAST)
                second(t - 2, t)
            for t in (TILES - 2, TILES - 1):
                second(t, t)

        @block.sync
        def _(sp):
            for u in range(2):
                sp.sem_inc(rows_stored[u], 16)
            for t, u in tiles(sp, 0, TILES, 2):
                sp.wait_ge(rows_ready, t + 1)
                sp.dma_start(table1[bass.ds(t * P, P), :], row[:, u, :]).then_inc(rows_stored[u], 16)
            for u in range(2):
                sp.wait_ge(rows_stored[u], 16 + 16 * len(range(u, TILES, 2)))


def rounds(t, u, ring=2):
    return 16 * ((t - u) // ring) + 16 if isinstance(t, int) else (t - u) * (16 // ring) + 16


def rounds4(t, u):
    return (t - u) * 4 + 16


def mixer(nc, allocator, dev, xt, QT, V, KE):
    PS, ident, mean, rstd, resid = (dev[k] for k in ("PS", "ident", "mean", "rstd", "resid"))
    with ExitStack() as st:
        sb, sem = allocator(st)
        O = sb("O", [P, TILES, D])
        EK = sb("EK", [P, 2, 4, QK])
        nkm = sb("nkm", [P, 1])
        ks = sb("ks", [P, 1])
        kg = sb("kg", [P, TILES // 4 + 1])
        KX = sb("KX", [P, 2, 512])
        QX = sb("QX", [P, 2, 512])
        mask = sb("mask", [P, P])
        ctx = sb("ctx", [P, P])
        WO = sb("WO", [P, D])
        CW = sb("CW", [P, D])
        bo, go, bb2 = (sb(n, [P, D]) for n in ("bo", "go", "bb2"))
        sq = sb("sq", [P, 2, D])
        ss = sb("ss", [P, TILES])
        r1 = sb("r1", [P, TILES])
        nmr = sb("nmr", [P, TILES])
        loaded, own, max_ready, exped = sem("mix_loaded"), sem("mix_own"), sem("kmax_ready"), sem("keys_exped")
        k_turned, k_copied, ctx_done = sem("k_turned"), sem("k_copied"), sem("ctx_done")
        ctx_ready, cw_done, cw_ready = sem("ctx_ready"), sem("cw_done"), sem("cw_ready")
        o_done, o_ready, squared = sem("o_done"), sem("o_ready"), sem("squared")
        norm_in, rooted, x_ready, r_ready, stored = sem("norm_in"), sem("rooted2"), sem("x_ready"), sem("r_ready"), sem("r_stored")
        scales, k_used, q_staged = sem("scales"), sem("k_used"), sem("q_staged")
        o_own, x_scaled = sem("o_normed"), sem("x_scaled")
        passed = sem("x_passed")
        block = st.enter_context(nc.Block())
        GRP = TILES // 4

        @block.sync
        def _(sp):
            sp.dma_start(WO[:, :], dev["w_out"]).then_inc(loaded, 16)
            for tile, v in ((bo, "b_out"), (go, "g_out"), (bb2, "b2")):
                sp.dma_start(tile[:, :], dev[v].partition_broadcast(P)).then_inc(loaded, 16)
            for c, _ in tiles(sp, 0, 7, 1):
                sp.wait_ge(r_ready, c * 7 + 7)
                sp.dma_start(resid[bass.ds(c * 7 * P, 7 * P), :].rearrange("(t p) n -> p t n", p=P),
                             xt[:, bass.ds(c * 7, 7), :]).then_inc(stored, 16)
            sp.wait_ge(stored, 7 * 16)

        @block.vector
        def _(dve):
            own_ = Chain(dve, own)
            own_.link(dve.tensor_reduce(nkm[:, :], KE[:, :], X, ALU.max, negate=True))
            dve.engine_nop().then_inc(max_ready, 1)
            own_.link(dve.memset(mask[:, :], 0.0))
            for h in range(MH):
                own_.link(dve.memset(mask[h * MD:(h + 1) * MD, h * MD:(h + 1) * MD], 1.0))
            own_.link(dve.tensor_scalar(r1[:, :], rstd[:, :], 1.0, None, ALU.add))
            own_.link(dve.tensor_tensor(nmr[:, :], mean[:, :], rstd[:, :], ALU.mult))
            own_.link(dve.tensor_scalar(nmr[:, :], nmr[:, :], -1.0, None, ALU.mult))
            dve.engine_nop().then_inc(scales, 1)
            dve.wait_ge(exped, GRP + 1)
            own_.link(dve.tensor_reduce(ks[:, :], kg[:, :], X, ALU.add))
            own_.link(dve.reciprocal(ks[:, :], ks[:, :]))
            dve.wait_ge(loaded, 4 * 16)
            own_.link(dve.tensor_scalar(go[:, :], go[:, :], 16.0, None, ALU.mult))
            dve.wait_ge(ctx_done, 1)
            dve.tensor_tensor(ctx[:, :], PS[:, 2, 0:P], mask[:, :], ALU.mult).then_inc(ctx_ready, 1)
            dve.wait_ge(ctx_done, 2)
            dve.tensor_copy(ctx[:, :], PS[:, 3, 0:P]).then_inc(ctx_ready, 1)
            dve.wait_ge(cw_done, 1)
            dve.tensor_scalar(CW[:, :], PS[:, 2, 0:D], ks[:, :], MD ** -0.5, ALU.mult, ALU.mult).then_inc(cw_ready, 1)
            for t, u in tiles(dve, 0, TILES, 2):
                dve.wait_ge(o_done, t + 1)
                dve.tensor_tensor(O[:, bass.ds(t, 1), :].rearrange("p a b -> p (a b)"), PS[:, 4 + u, 0:D], bo[:, :],
                                  ALU.add).then_inc(o_ready, 1)
            dve.wait_ge(squared, TILES + 3)
            own_.link(dve.tensor_scalar(ss[:, :], ss[:, :], 1e-12, None, ALU.max))
            own_.link(dve.reciprocal(ss[:, :], ss[:, :]))

            def row(what, t):
                return what[:, bass.ds(t, 1), :].rearrange("p a b -> p (a b)")

            def norm(t):
                o = row(O, t)
                dve.scalar_tensor_tensor(o, o, ss[:, bass.ds(t, 1)], go[:, :], ALU.mult, ALU.mult).then_inc(o_own, 1)

            def add(t):
                dve.wait_ge(o_own, t + 1)
                dve.wait_ge(x_ready, t + 1)
                dve.scalar_tensor_tensor(row(xt, t), row(O, t), nmr[:, bass.ds(t, 1)], row(xt, t), ALU.add, ALU.add).then_inc(r_ready, 1)

            norm(0)
            for t, _ in tiles(dve, 0, TILES - 1, 4):
                norm(t + 1)
                add(t)
            add(TILES - 1)

        @block.gpsimd
        def _(pool):
            pool.wait_ge(scales, 1)
            pool.wait_ge(loaded, 4 * 16)

            def scale(t):
                r = xt[:, bass.ds(t, 1), :]
                pool.tensor_tensor(r, r, one(r1[:, bass.ds(t, 1)], 2, D), ALU.mult).then_inc(x_scaled, 1)

            def add(t):
                r = xt[:, bass.ds(t, 1), :]
                pool.wait_ge(x_scaled, t + 1)
                pool.sem_inc(passed, 1)
                pool.tensor_tensor(r, r, one(bb2[:, :], 1, 1), ALU.add).then_inc(x_ready, 1)

            scale(0)
            for t, _ in tiles(pool, 0, TILES - 1, 4):
                scale(t + 1)
                add(t)
            add(TILES - 1)

        @block.scalar
        def _(act):
            act.wait_ge(max_ready, 1)

            def exps(g, u, n=512):
                if not isinstance(g, int) or g > 1:
                    act.wait_ge(k_turned, g - 1)
                act.activation(KX[:, u, 0:n], KE[:, bass.ds(g * 512, n)], ACT.Exp, bias=nkm[:, :],
                               accum_out=kg[:, bass.ds(g, 1)]).then_inc(exped, 1)

            def copy(g, u, rows=P, n=4):
                act.wait_ge(k_turned, g + 1)
                if not isinstance(g, int) or g > 1:
                    act.wait_ge(k_used, g - 1)
                act.activation(EK[0:rows, u, 0:n, :], PS[0:rows, u, 0:n * P].rearrange("p (j c) -> p j c", j=n), ACT.Copy).then_inc(k_copied, 1)

            exps(0, 0)
            exps(1, 1)
            copy(0, 0)
            for g, u in tiles(act, 2, GRP, 2):
                exps(g, u)
                copy(g - 1, 1 - u)
            exps(GRP, GRP % 2, N + MEM - GRP * 512)
            copy(GRP - 1, (GRP - 1) % 2)
            copy(GRP, GRP % 2, LAST + MEM, 1)

            def stage(g, u, n=512):
                if not isinstance(g, int) or g > 1:
                    act.wait_ge(o_done, 4 * g - 4)
                act.activation(QX[:, u, 0:n], QT[:, bass.ds(g * 512, n)], ACT.Copy).then_inc(q_staged, 1)

            def square(t, u):
                act.wait_ge(o_ready, t + 1)
                act.wait_ge(squared, t + 1)
                act.activation(sq[:, u, :], O[:, bass.ds(t, 1), :].rearrange("p a b -> p (a b)"), ACT.Square,
                               accum_out=ss[:, bass.ds(t, 1)]).then_inc(squared, 1)

            act.sem_inc(squared, 2)
            stage(0, 0)
            stage(1, 1)
            for g, u in tiles(act, 2, GRP, 2):
                for j in range(4):
                    square(g * 4 - 8 + j, j % 2)
                stage(g, u)
            for t in range(4 * GRP - 8, 4 * GRP - 4):
                square(t, t % 2)
            stage(GRP, GRP % 2, P)
            for t in range(4 * GRP - 4, TILES):
                square(t, t % 2)
            act.wait_ge(squared, TILES + 2)
            act.activation(ss[:, :], ss[:, :], ACT.Sqrt).then_inc(squared, 1)

        @block.tensor
        def _(pe):
            def turn(g, u):
                pe.wait_ge(exped, g + 1)
                if not isinstance(g, int) or g > 1:
                    pe.wait_ge(k_copied, g - 1)
                for j in range(4):
                    last = pe.transpose(PS[:, u, j * P:(j + 1) * P], KX[:, u, j * P:(j + 1) * P], ident[:, :])
                last.then_inc(k_turned, 1)

            def gather(g, u, start=False):
                pe.wait_ge(k_copied, g + 1)
                for j in range(4):
                    last = pe.matmul(PS[:, 2, 0:P], EK[:, u, j, :], V[:, bass.ds(g * 4 + j, 1), :].rearrange("p a b -> p (a b)"),
                                     start=start and j == 0, stop=False)
                last.then_inc(k_used, 1)

            turn(0, 0)
            turn(1, 1)
            gather(0, 0, start=True)
            for g, u in tiles(pe, 2, GRP, 2):
                turn(g, u)
                gather(g - 1, 1 - u)
            rows = LAST + MEM
            pe.wait_ge(exped, GRP + 1)
            pe.wait_ge(k_copied, GRP - 1)
            pe.transpose(PS[0:rows, GRP % 2, 0:P], KX[:, GRP % 2, 0:rows], ident[:, :]).then_inc(k_turned, 1)
            gather(GRP - 1, (GRP - 1) % 2)
            pe.wait_ge(k_copied, GRP + 1)
            pe.matmul(PS[:, 2, 0:P], EK[0:rows, GRP % 2, 0, :], V[0:rows, TILES - 1, :], start=False, stop=True).then_inc(ctx_done, 1)
            pe.wait_ge(ctx_ready, 1)
            pe.transpose(PS[:, 3, 0:P], ctx[:, :], ident[:, :]).then_inc(ctx_done, 1)
            pe.wait_ge(ctx_ready, 2)
            pe.wait_ge(loaded, 4 * 16)
            pe.matmul(PS[:, 2, 0:D], ctx[:, :], WO[:, :], start=True, stop=True).then_inc(cw_done, 1)
            pe.wait_ge(cw_ready, 1)

            def out_tile(t, u, ring, j):
                if not isinstance(t, int) or t > 1:
                    pe.wait_ge(o_ready, t - 1)
                pe.matmul(PS[:, 4 + u, 0:D], QX[:, ring, j * P:(j + 1) * P], CW[:, :], start=True, stop=True).then_inc(o_done, 1)

            for g in range(2):
                pe.wait_ge(q_staged, g + 1)
                for j in range(4):
                    out_tile(4 * g + j, j % 2, g, j)
            for g, u in tiles(pe, 2, GRP, 2):
                pe.wait_ge(q_staged, g + 1)
                for j in range(4):
                    out_tile(4 * g + j, j % 2, u, j)
            pe.wait_ge(q_staged, GRP + 1)
            out_tile(4 * GRP, 0, GRP % 2, 0)


class Layer:

    def __init__(self, heads, row, wide, banks, logit_cols):
        self.heads = heads
        self.row = row
        self.wide = wide
        self.banks = banks
        self.logit_cols = logit_cols


LAYER1 = Layer(H1, ROW1, ROW1, 2, [256 + a * HALF + j for a in range(2) for j in range(4)])
LAYER2 = Layer(1, ROW2, D + 1, 1, [D + 1])


def bounds(nc, allocator, dev, layer, table, AD, ADM, SELF, ACC):
    PS, ident, iota_row, ones, SRC, DST, TK = (dev[k] for k in (
        "PS", "ident", "iota_row", "ones", "SRC", "DST", "TK"))
    H = layer.heads
    tag = f"h{H}_"
    with ExitStack() as st:
        sb, sem = allocator(st)
        ext = sb(tag + "ext", [P, 2 * H])
        exta = sb(tag + "exta", [P, 2 * H])
        MX = sb(tag + "MX", [P, TILES, H])
        Z = sb(tag + "Zb", [P, TILES, H])
        spread = sb(tag + "spread", [P, H])
        widest = sb(tag + "widest", [P, 1])
        wide = sb(tag + "wide", [P, 1], I32)
        ext_ready, ext_all, own = sem(tag + "ext_ready"), sem(tag + "ext_all"), sem(tag + "bound_own")
        flag_ready, z_ready = sem(tag + "flag_ready"), sem(tag + "self_logits")
        G = sb(tag + "Gx", [P, layer.row])
        idx = sb(tag + "idx", [P, 1], I32)
        S = sb(tag + "Sx", [P, P])
        off = sb(tag + "off", [P, P])
        diag = sb(tag + "diag", [P, H, P])
        mxs = sb(tag + "mxs", [P, H])
        released = sem(tag + "x_released")
        staged, fetched, used = sem(tag + "x_staged"), sem(tag + "x_fetched"), sem(tag + "x_used")
        cols, spread_out, xown = sem(tag + "x_cols"), sem(tag + "x_ps"), sem(tag + "x_own")
        block = st.enter_context(nc.Block())

        @block.gpsimd
        def _(pool):
            pool.wait_ge(ext_ready, 1)
            pool.partition_all_reduce(exta[:, :], ext[:, :], P, RMAX).then_inc(ext_all, 1)
            pool.memset(ACC[:, :, :], 0.0)
            pool.wait_ge(flag_ready, 1)
            with pool.If(pool.value_load(wide[0:1, 0:1], min_val=0, max_val=1) > 0):
                for s, _ in tiles(pool, 0, SLOTS, 1):
                    pool.wait_ge(used, s + 1)
                    pool.wait_ge(staged, s + 1)
                    pool.sem_inc(released, 1)
                    pool.indirect_dma_start(G[:, :], None, table, IndexOn(ap=idx[:, 0:1], axis=0)).then_inc(fetched, 16)

        @block.scalar
        def _(act):
            act.wait_ge(flag_ready, 1)
            with act.If(act.value_load(wide[0:1, 0:1], min_val=0, max_val=1) > 0):
                act.activation(idx[:, :], SRC[:, 0:1], ACT.Copy).then_inc(staged, 1)
                for s, _ in tiles(act, 1, SLOTS, 1):
                    act.wait_ge(fetched, 16 * s)
                    act.activation(idx[:, :], SRC[:, bass.ds(s, 1)], ACT.Copy).then_inc(staged, 1)
            act.wait_ge(z_ready, 1)
            act.activation(SELF[:, :, :], Z[:, :, :], ACT.Exp)

        @block.tensor
        def _(pe):
            pe.wait_ge(flag_ready, 1)
            with pe.If(pe.value_load(wide[0:1, 0:1], min_val=0, max_val=1) > 0):
                for s, _ in tiles(pe, 0, SLOTS, 1):
                    pe.wait_ge(cols, s + 1)
                    for h in range(H):
                        o = PS[:, h // 4, (h % 4) * P:(h % 4 + 1) * P]
                        pe.matmul(o, ones[:, :], diag[:, h, :], start=True, stop=False)
                        last = pe.matmul(o, off[:, :], ident[:, :], start=False, stop=True)
                    last.then_inc(spread_out, 1)

        @block.vector
        def _(dve):
            own_ = Chain(dve, own)
            by_head = AD[:, :, 0:H].rearrange("p t h -> p h t")
            dve.tensor_reduce(ext[:, 0:H], by_head, X, ALU.max)
            dve.tensor_reduce(ext[:, H:2 * H], by_head, X, ALU.min, negate=True).then_inc(ext_ready, 1)
            dve.wait_ge(ext_all, 1)
            own_.link(dve.tensor_copy(MX[:, :, :], one(exta[:, 0:H], 1, TILES)))
            own_.link(dve.tensor_tensor(spread[:, :], exta[:, 0:H], exta[:, H:2 * H], ALU.add))
            own_.link(dve.tensor_reduce(widest[:, :], spread[:, :], X, ALU.max))
            dve.tensor_scalar(wide[:, :], widest[:, :], SPREAD, None, ALU.is_gt).then_inc(flag_ready, 1)
            dve.wait_ge(flag_ready, 1)
            with dve.If(dve.value_load(wide[0:1, 0:1], min_val=0, max_val=1) > 0):
                xown_ = Chain(dve, xown)
                xown_.link(dve.tensor_copy(MX[:, :, :], AD[:, :, 0:H]))
                dve.sem_inc(used, 1)
                per = H + 4
                for k, _ in tiles(dve, 0, STEPS, 1):
                    t = dve.value_load(TK[0:1, bass.ds(k, 1)], min_val=0, max_val=TILES - 1)
                    xown_.at(1 + k * 2 * per)
                    for j in range(2):
                        s = 2 * k + j
                        dve.wait_ge(fetched, 16 * s + 16)
                        xown_.link(dve.tensor_scalar(S[:, :], iota_row[:, :], DST[:, bass.ds(s, 1)], None, ALU.is_equal))
                        xown_.link(dve.tensor_scalar(off[:, :], S[:, :], 1.0, BIG, ALU.subtract, ALU.mult))
                        for h, c in enumerate(layer.logit_cols):
                            xown_.link(dve.tensor_scalar(diag[:, h, :], ident[:, :], G[:, c:c + 1], None, ALU.mult))
                        dve.sem_inc(used, 1)
                        dve.sem_inc(cols, 1)
                        dve.wait_ge(spread_out, s + 1)
                        if H == 8:
                            xown_.link(dve.tensor_reduce(mxs[:, :].rearrange("p (a b) -> p a b", a=2),
                                                         PS[:, 0:2, :].rearrange("p a (b e) -> p a b e", b=4), X, ALU.max))
                        else:
                            xown_.link(dve.tensor_reduce(mxs[:, :], PS[:, 0, 0:P], X, ALU.max))
                        m = MX[:, bass.ds(t, 1), :].rearrange("p a b -> p (a b)")
                        xown_.link(dve.tensor_tensor(m, m, mxs[:, :], ALU.max))
                    xown_.closed(2 * per)
            own_.link(dve.tensor_copy(ADM[:, :, 0:H], AD[:, :, H:2 * H]))
            own_.link(dve.tensor_tensor(Z[:, :, :], MX[:, :, :], AD[:, :, H:2 * H], ALU.add))
            own_.link(dve.scalar_tensor_tensor(ADM[:, :, H:2 * H], Z[:, :, :], SLOPE, Z[:, :, :], ALU.mult, ALU.max))
            own_.link(dve.tensor_tensor(Z[:, :, :], AD[:, :, 0:H], AD[:, :, H:2 * H], ALU.add))
            own_.link(dve.scalar_tensor_tensor(Z[:, :, :], Z[:, :, :], SLOPE, Z[:, :, :], ALU.mult, ALU.max))
            dve.tensor_tensor(Z[:, :, :], Z[:, :, :], ADM[:, :, H:2 * H], ALU.subtract).then_inc(z_ready, 1)


def walk(nc, allocator, dev, layer, table, ADM, ACC):
    PS, ident, iota_row, SRC, DST, TK = (dev[k] for k in ("PS", "ident", "iota_row", "SRC", "DST", "TK"))
    H, W = layer.heads, layer.wide
    tag = f"w{H}_"
    B = 4
    NB = SLOTS // B
    RING = 6
    assert SLOTS % B == 0
    with ExitStack() as st:
        sb, sem = allocator(st)
        G = sb(tag + "G", [P, RING, B, layer.row])
        idx = sb(tag + "idx", [P, RING, B], I32)
        S = sb(tag + "S", [P, RING, B, P])
        ident16 = sb(tag + "ident16", [P, P], BF16)
        ST = sb(tag + "ST", [P, 2, B, P], BF16)
        parts = sb(tag + "parts", [P, 3, TILES, 2 * H], BF16)
        rest = sb(tag + "rest", [P, TILES, 2 * H])
        Z = sb(tag + "Z", [P, 2, B, H])
        PW = sb(tag + "PW", [P, RING, B, H])
        SW = None if H > 1 else sb(tag + "SW", [P, 2, B, P])
        fetched = [sem(f"{tag}fetched{r}") for r in range(RING)]
        staged = sem(tag + "staged")
        hot = sem(tag + "hot")
        turned, st_ready = sem(tag + "turned"), sem(tag + "st_ready")
        spread = sem(tag + "spread")
        z_ready, weighed = sem(tag + "z_ready"), sem(tag + "weighed")
        scaled = sem(tag + "scaled")
        summed = sem(tag + "summed")
        merged = sem(tag + "merged")
        own = sem(tag + "logit_own")
        ident_ready = sem(tag + "ident16_ready")
        split, parts_ready = sem(tag + "split"), sem(tag + "parts_ready")
        act_scaled = sem(tag + "act_scaled")
        released = sem(tag + "released")
        block = st.enter_context(nc.Block())

        def filled(q):
            return q * (16 * B) + 16 * B

        def tile_of(eng, k):
            return eng.value_load(TK[0:1, bass.ds(k, 1)], min_val=0, max_val=TILES - 1)

        def tiles_of(eng, n):
            return tile_of(eng, 2 * n), tile_of(eng, 2 * n + 1)

        @block.gpsimd
        def _(pool):
            def fetch(n, r):
                pool.wait_ge(staged, n + 1)
                if not isinstance(n, int) or n >= RING:
                    pool.wait_ge(summed, 2 * (n - RING) + 2)
                pool.sem_inc(released, 1)
                for b in range(B):
                    pool.indirect_dma_start(G[:, r, b, :], None, table, IndexOn(ap=idx[:, r, b:b + 1], axis=0)).then_inc(fetched[r], 16)

            for n in range(RING):
                fetch(n, n)
            for n, r in tiles(pool, RING, NB, RING):
                fetch(n, r)

        @block.scalar
        def _(act):
            def stage(n, r):
                act.activation(idx[:, r, :], SRC[:, bass.ds(n * B, B)], ACT.Copy).then_inc(staged, 1)

            def copy_turned(n, r):
                act.wait_ge(turned, n + 1)
                if not isinstance(n, int) or n > 1:
                    act.wait_ge(spread, n - 1)
                act.activation(ST[:, r % 2, :, :], PS[:, 4 + r % 2, :].bitcast(BF16)[:, 0:B * P].rearrange("p (b q) -> p b q", b=B), ACT.Copy).then_inc(st_ready, 1)

            def weigh(n, r):
                act.wait_ge(z_ready, n + 1)
                if H == 8:
                    out = G[:, r, :, :].rearrange("p b (a c) -> p b a c", a=2)[:, :, :, 4 * C1:]
                    act.activation(out, Z[:, r % 2, :, :].rearrange("p b (a c) -> p b a c", a=2), ACT.Exp).then_inc(weighed, 1)
                else:
                    act.activation(PW[:, r, :, :], Z[:, r % 2, :, :], ACT.Exp).then_inc(weighed, 1)

            def scale_last(n, r):
                if H == 8:
                    act.wait_ge(weighed, n + 1)
                    for h in range(H):
                        at, w = h // 4 * HALF + h % 4 * C1, h // 4 * HALF + 4 * C1 + h % 4
                        feat = G[:, r, B - 1, at:at + C1]
                        last = act.activation(feat, feat, ACT.Copy, scale=G[:, r, B - 1, w:w + 1])
                    last.then_inc(act_scaled, 1)

            for n in range(RING):
                stage(n, n)
            copy_turned(0, 0)
            copy_turned(1, 1)
            weigh(0, 0)
            copy_turned(2, 2)
            weigh(1, 1)
            scale_last(0, 0)

            def step(n, r):
                scale_last(n + 1, (r + 1) % RING)
                weigh(n + 2, (r + 2) % RING)
                copy_turned(n + 3, (r + 3) % RING)

            for n, r, q in turns(act, 0, NB - RING, RING):
                step(n, r)
                act.wait_ge(fetched[r], filled(q))
                stage(n + RING, r)
            for n in range(NB - RING, NB - 3):
                step(n, n % RING)
            scale_last(NB - 2, (NB - 2) % RING)
            weigh(NB - 1, (NB - 1) % RING)
            scale_last(NB - 1, (NB - 1) % RING)

        @block.tensor
        def _(pe):
            def turn(n, r):
                pe.wait_ge(hot, n + 1)
                if not isinstance(n, int) or n > 1:
                    pe.wait_ge(st_ready, n - 1)
                out = PS[:, 4 + r % 2, :].bitcast(BF16)
                for b in range(B):
                    upper = S[:, r, b, :].bitcast(BF16).rearrange("p (q two) -> p q two", two=2)[:, :, 1]
                    last = pe.transpose(out[:, b * P:(b + 1) * P], upper, ident16[:, :])
                last.then_inc(turned, 1)

            def spread_nodes(n, r, t=None):
                t = tiles_of(pe, n) if t is None else t
                pe.wait_ge(st_ready, n + 1)
                if not isinstance(n, int) or n > 1:
                    pe.wait_ge(z_ready, n - 1)
                for j in range(2):
                    for b in (2 * j, 2 * j + 1):
                        for i in range(3):
                            last = pe.matmul(PS[:, 6 + r % 2, b * 2 * H:(b + 1) * 2 * H], ST[:, r % 2, b, :],
                                             parts[:, i, bass.ds(t[j], 1), :].rearrange("p a b -> p (a b)"), start=i == 0, stop=i == 2)
                last.then_inc(spread, 1)

            def sum_up(n, r, j):
                k = 2 * n + j
                pe.wait_ge(scaled, k + 1)
                if H == 8 and j == 1:
                    pe.wait_ge(act_scaled, n + 1)
                if not isinstance(n, int) or k > 1:
                    pe.wait_ge(merged, k)
                for b in (2 * j, 2 * j + 1):
                    for a in range(layer.banks):
                        if H == 8:
                            lhsT, rhs = S[:, r, b, :], G[:, r, b, a * HALF:(a + 1) * HALF]
                        else:
                            lhsT, rhs = SW[:, r % 2, b, :], G[:, r, b, 0:W]
                        last = pe.matmul(PS[:, 2 * j + a, 0:W // layer.banks], lhsT, rhs, start=b % 2 == 0, stop=b % 2 == 1)
                last.then_inc(summed, 1)

            def step(n, r):
                t = tiles_of(pe, n + 2)
                sum_up(n, r, 0)
                spread_nodes(n + 2, (r + 2) % RING, t)
                sum_up(n, r, 1)
                turn(n + 3, (r + 3) % RING)

            pe.wait_ge(ident_ready, 1)
            turn(0, 0)
            turn(1, 1)
            pe.wait_ge(parts_ready, 1)
            spread_nodes(0, 0)
            turn(2, 2)
            spread_nodes(1, 1)
            step(0, 0)
            for n, r in tiles(pe, 1, NB - 3, RING):
                step(n, r)
            spread_nodes(NB - 1, (NB - 1) % RING)
            for n in range(NB - 3, NB):
                for j in range(2):
                    sum_up(n, n % RING, j)

        @block.vector
        def _(dve):
            def one_hot(n, r, slots=range(B)):
                for b in slots:
                    last = dve.tensor_scalar(S[:, r, b, :], iota_row[:, :], DST[:, bass.ds(n * B + b, 1)], None, ALU.is_equal)
                if B - 1 in slots:
                    last.then_inc(hot, 1)

            def logits(n, r, q, between=lambda b: None):
                dve.wait_ge(spread, n + 1)
                dve.wait_ge(fetched[r], filled(q))
                node = PS[:, 6 + r % 2, 0:B * 2 * H].rearrange("p (b c) -> p b c", b=B)
                if H == 8:
                    a_src = G[:, r, :, :].rearrange("p b (a c) -> p b a c", a=2)[:, :, :, 4 * C1:]
                    a_dst = node[:, :, 0:H].rearrange("p b (a c) -> p b a c", a=2)
                    z4 = Z[:, r % 2, :, :].rearrange("p b (a c) -> p b a c", a=2)
                else:
                    a_src, a_dst, z4 = G[:, r, :, D + 1:D + 2], node[:, :, 0:H], Z[:, r % 2, :, :]
                z = Z[:, r % 2, :, :]
                dve.tensor_tensor(z4, a_src, a_dst, ALU.add).then_inc(own, 1)
                between(0)
                dve.wait_ge(own, 3 * n + 1)
                dve.scalar_tensor_tensor(z, z, SLOPE, z, ALU.mult, ALU.max).then_inc(own, 1)
                between(1)
                dve.wait_ge(own, 3 * n + 2)
                dve.tensor_tensor(z, z, node[:, :, H:2 * H], ALU.subtract).then_inc(own, 1)
                between(2)
                dve.wait_ge(own, 3 * n + 3)
                dve.tensor_scalar(z, z, 1.0, None, ALU.min).then_inc(z_ready, 1)
                between(3)

            def scale(n, r, j):
                dve.wait_ge(weighed, n + 1)
                for b in (2 * j, 2 * j + 1)[:1 if H == 8 and j == 1 else 2]:
                    if H == 8:
                        row = G[:, r, b, :].rearrange("p (a c) -> p a c", a=2)
                        feat = row[:, :, 0:4 * C1].rearrange("p a (h c) -> p a h c", h=4)
                        last = dve.tensor_tensor(feat, feat, one(row[:, :, 4 * C1:], 3, C1), ALU.mult)
                    else:
                        last = dve.tensor_scalar(SW[:, r % 2, b, :], iota_row[:, :], DST[:, bass.ds(n * B + b, 1)],
                                                 PW[:, r, b, :], ALU.is_equal, ALU.mult)
                last.then_inc(scaled, 1)

            def merge(k, j):
                t = tile_of(dve, k)
                dve.wait_ge(summed, k + 1)
                dve.wait_ge(merged, k + 1)
                if H == 8:
                    acc = ACC[:, bass.ds(t, 1), :].rearrange("p t (a c) -> p (t a) c", a=2)
                    dve.tensor_tensor(acc, acc, PS[:, 2 * j:2 * j + 2, 0:HALF], ALU.add).then_inc(merged, 1)
                else:
                    acc = ACC[:, bass.ds(t, 1), :].rearrange("p t c -> p (t c)")
                    dve.tensor_tensor(acc, acc, PS[:, 2 * j, 0:W], ALU.add).then_inc(merged, 1)

            def step(n, r, q, hots=True, more=True):
                scale(n + 1, (r + 1) % RING, 0)
                if not isinstance(n, int) or n > 0:
                    merge(2 * n - 1, 1)
                scale(n + 1, (r + 1) % RING, 1)
                merge(2 * n, 0)
                if more:
                    logits(n + 2, (r + 2) % RING, q + (r + 2) // RING,
                           (lambda b: one_hot(n + 4, (r + 4) % RING, (b,))) if hots else lambda b: None)

            dve.sem_inc(merged, 1)
            dve.tensor_copy(ident16[:, :], ident[:, :]).then_inc(ident_ready, 1)
            for n in range(4):
                one_hot(n, n)
                if n == 1:
                    split_ = Chain(dve, split)
                    split_.link(dve.tensor_copy(parts[:, 0, :, :], ADM[:, :, :]))
                    split_.link(dve.tensor_tensor(rest[:, :, :], ADM[:, :, :], parts[:, 0, :, :], ALU.subtract))
                    split_.link(dve.tensor_copy(parts[:, 1, :, :], rest[:, :, :]))
                    split_.link(dve.tensor_tensor(rest[:, :, :], rest[:, :, :], parts[:, 1, :, :], ALU.subtract))
                    dve.tensor_copy(parts[:, 2, :, :], rest[:, :, :]).then_inc(parts_ready, 1)
            logits(0, 0, 0)
            logits(1, 1, 0)
            scale(0, 0, 0)
            scale(0, 0, 1)
            step(0, 0, 0)
            for n, r, q in turns(dve, 1, NB - 4, RING):
                step(n, r, q)
            for n in (NB - 4, NB - 3):
                step(n, n % RING, n // RING, hots=False)
            step(NB - 2, (NB - 2) % RING, 0, more=False)
            merge(2 * NB - 3, 1)
            merge(2 * NB - 2, 0)
            merge(2 * NB - 1, 1)


def between(nc, allocator, dev, ACC, SELF, AD2):
    PS, ident, table1, table2 = (dev[k] for k in ("PS", "ident", "table1", "table2"))
    FT = F1 // P
    with ExitStack() as st:
        sb, sem = allocator(st)
        W2A = sb("W2A", [P, FT, ROW2 + 1])
        att2 = sb("att2", [P, 2, D])
        prod = sb("prod2", [P, D])
        b1b = sb("b1b", [P, F1])
        unit_col = sb("unit_col", [P, ROW2])
        RD = sb("RD", [P, TILES, H1])
        HR = sb("HR", [P, 4, ROW1])
        HP = sb("HP", [P, 4, F1])
        EX = sb("EX", [P, 4, F1])
        EL = sb("EL", [P, 4, F1])
        ELT = sb("ELT", [P, 2, FT, P])
        row = sb("row2", [P, 4, ROW2])
        loaded, own, folded = sem("f_loaded"), sem("f_own"), sem("f_folded")
        mine_in = [sem(f"mine_in{u}") for u in range(4)]
        mine_scaled, mine_added, o_ready, o_exp, el_ready, fown = sem("mine_scaled"), sem("mine_added"), sem("f_o_ready"), sem("f_o_exp"), sem("el_ready"), sem("fo_own")
        el_turned, elt_ready, rows_done, rows_ready = sem("el_turned"), sem("elt_ready"), sem("rows2_done"), sem("rows2_ready")
        stored = [sem(f"rows2_stored{u}") for u in range(4)]
        block = st.enter_context(nc.Block())

        @block.sync
        def _(sp):
            sp.dma_start(W2A[:, :, 0:D], dev["W2"].rearrange("(k p) n -> p k n", p=P)).then_inc(loaded, 16)
            for j, v in enumerate(("att_s2", "att_d2")):
                sp.dma_start(att2[:, j, :], dev[v].rearrange("a c -> (a c)").partition_broadcast(P)).then_inc(loaded, 16)
            sp.dma_start(b1b[:, :], dev["b1"].partition_broadcast(P)).then_inc(loaded, 16)
            def fetch(t, u):
                sp.dma_start(HR[:, u, :], table1[bass.ds(t * P, P), :]).then_inc(mine_in[u], 16)

            for t in range(4):
                fetch(t, t)
            for t, u in tiles(sp, 4, TILES, 4):
                sp.wait_ge(mine_scaled, t - 3)
                fetch(t, u)

        @block.gpsimd
        def _(pool):
            def scale_mine(t, u):
                pool.wait_ge(mine_in[u], rounds4(t, u))
                pool.tensor_tensor(HP[:, u, :].rearrange("p (a h c) -> p a h c", a=2, h=4),
                                   HR[:, u, :].rearrange("p (a c) -> p a c", a=2)[:, :, 0:4 * C1].rearrange("p a (h c) -> p a h c", h=4),
                                   one(SELF[:, bass.ds(t, 1), :].rearrange("p t (a h) -> p (t a) h", a=2), 3, C1),
                                   ALU.mult).then_inc(mine_scaled, 1)

            def add_others(t, u):
                pool.wait_ge(mine_scaled, t + 1)
                o4 = HP[:, u, :].rearrange("p (a h c) -> p a h c", a=2, h=4)
                acc = ACC[:, bass.ds(t, 1), :].rearrange("p t (a c) -> p (t a) c", a=2)[:, :, 0:4 * C1].rearrange("p a (h c) -> p a h c", h=4)
                pool.tensor_tensor(o4, o4, acc, ALU.add).then_inc(mine_added, 1)

            scale_mine(0, 0)
            for t in range(1, 4):
                scale_mine(t, t)
                add_others(t - 1, t - 1)
            for t, u in tiles(pool, 4, TILES, 4):
                pool.wait_ge(o_exp, t - 3)
                scale_mine(t, u)
                add_others(t - 1, (u + 3) % 4)
            add_others(TILES - 1, (TILES - 1) % 4)

        @block.vector
        def _(dve):
            own_ = Chain(dve, own)
            own_.link(dve.memset(W2A[:, :, D:D + 1], 0.0))
            own_.link(dve.memset(unit_col[:, :], 0.0))
            own_.link(dve.memset(unit_col[:, D:D + 1], 1.0))
            dve.wait_ge(loaded, 4 * 16)
            for k in range(FT):
                for j in range(2):
                    own_.link(dve.tensor_tensor(prod[:, :], W2A[:, k, 0:D], att2[:, j, :], ALU.mult))
                    own_.link(dve.tensor_reduce(W2A[:, k, D + 1 + j:D + 2 + j], prod[:, :], X, ALU.add))
            sums = ACC[:, :, :].rearrange("p t (a c) -> p t a c", a=2)[:, :, :, 4 * C1:]
            own_.link(dve.tensor_tensor(RD[:, :, :].rearrange("p t (a h) -> p t a h", a=2), sums,
                                        SELF[:, :, :].rearrange("p t (a h) -> p t a h", a=2), ALU.add))
            own_.link(dve.reciprocal(RD[:, :, :], RD[:, :, :]))
            dve.engine_nop().then_inc(folded, 1)

            def quotient(t, u):
                o4 = HP[:, u, :].rearrange("p (a h c) -> p a h c", a=2, h=4)
                dve.wait_ge(mine_added, t + 1)
                dve.tensor_tensor(o4, o4, one(RD[:, bass.ds(t, 1), :].rearrange("p t (a h) -> p (t a) h", a=2), 3, C1),
                                  ALU.mult).then_inc(fown, 1)

            def bias(t, u):
                dve.wait_ge(fown, t + 1)
                dve.tensor_tensor(HP[:, u, :], HP[:, u, :], b1b[:, :], ALU.add).then_inc(o_ready, 1)

            def elu(t, u):
                dve.wait_ge(o_exp, t + 1)
                dve.scalar_tensor_tensor(EL[:, u, :], EX[:, u, :], 1.0, EL[:, u, :], ALU.min, ALU.add).then_inc(el_ready, 1)

            def rows(t, u):
                dve.wait_ge(rows_done, t + 1)
                dve.wait_ge(stored[u], rounds4(t, u))
                dve.tensor_copy(AD2[:, bass.ds(t, 1), :].rearrange("p a b -> p (a b)"), PS[:, 2 + u % 2, D + 1:D + 3])
                dve.tensor_tensor(row[:, u, :], PS[:, 2 + u % 2, 0:ROW2], unit_col[:, :], ALU.add).then_inc(rows_ready, 1)

            for t in range(4):
                quotient(t, t)
                if t > 1:
                    elu(t - 2, t - 2)
                bias(t, t)
            for t, u in tiles(dve, 4, TILES, 4):
                quotient(t, u)
                elu(t - 2, (u + 2) % 4)
                bias(t, u)
                rows(t - 4, u)
            for t in range(TILES, TILES + 2):
                elu(t - 2, (t - 2) % 4)
                rows(t - 4, t % 4)
            for t in (TILES - 2, TILES - 1):
                rows(t, t % 4)

        @block.scalar
        def _(act):
            def curve(t, u):
                act.wait_ge(o_ready, t + 1)
                if not isinstance(t, int) or t > 3:
                    act.wait_ge(el_turned, t - 3)
                act.activation(EX[:, u, :], HP[:, u, :], ACT.Exp)
                act.activation(EL[:, u, :], HP[:, u, :], ACT.Relu).then_inc(o_exp, 1)

            def copy(t, u):
                act.wait_ge(el_turned, t + 1)
                if not isinstance(t, int) or t > 1:
                    act.wait_ge(rows_done, t - 1)
                act.activation(ELT[:, u, :, :], PS[:, u, :].rearrange("p (k q) -> p k q", k=FT), ACT.Copy, bias=-1.0).then_inc(elt_ready, 1)

            def store(t, u):
                act.wait_ge(rows_ready, t + 1)
                act.dma_start(table2[bass.ds(t * P, P), :], row[:, u, :]).then_inc(stored[u], 16)

            for u in range(4):
                act.sem_inc(stored[u], 16)
            for t in range(6):
                curve(t, t % 4)
                if t > 2:
                    copy(t - 3, (t - 3) % 2)
            for t, u in tiles(act, 6, TILES, 4):
                curve(t, u)
                copy(t - 3, (u + 1) % 2)
                store(t - 6, (u + 2) % 4)
            for t in range(TILES - 6, TILES):
                if t > TILES - 4:
                    copy(t, t % 2)
                store(t, t % 4)
            for u in range(4):
                act.wait_ge(stored[u], 16 + 16 * len(range(u, TILES, 4)))

        @block.tensor
        def _(pe):
            def turn(t, u):
                pe.wait_ge(el_ready, t + 1)
                if not isinstance(t, int) or t > 1:
                    pe.wait_ge(elt_ready, t - 1)
                for k in range(FT):
                    last = pe.transpose(PS[:, u % 2, k * P:(k + 1) * P], EL[:, u, k * P:(k + 1) * P], ident[:, :])
                last.then_inc(el_turned, 1)

            def product(t, u):
                pe.wait_ge(elt_ready, t + 1)
                if not isinstance(t, int) or t > 1:
                    pe.wait_ge(rows_ready, t - 1)
                for k in range(FT):
                    last = pe.matmul(PS[:, 2 + u, 0:ROW2 + 1], ELT[:, u, k, :], W2A[:, k, :], start=k == 0, stop=k == FT - 1)
                last.then_inc(rows_done, 1)

            pe.wait_ge(folded, 1)
            turn(0, 0)
            turn(1, 1)
            product(0, 0)
            for t, u in tiles(pe, 2, TILES, 4):
                turn(t, u)
                product(t - 1, (u + 1) % 2)
            product(TILES - 1, (TILES - 1) % 2)


def residual(nc, allocator, dev, ACC, SELF, X1, bn):
    table2, resid, xbuf = dev["table2"], dev["resid"], dev["xbuf"]
    with ExitStack() as st:
        sb, sem = allocator(st)
        HR = sb("HR2", [P, 4, ROW2])
        RS = sb("RS", [P, 4, D])
        T = sb("T", [P, 4, D + 1])
        RD = sb("RD2", [P, TILES])
        zero = sb("zero", [P, 8, D])
        own, blank = sem("r_own"), sem("blank")
        summed, x1_ready = sem("r_summed"), sem("r_x1_ready")
        mine_in = [sem(f"r_mine_in{u}") for u in range(4)]
        cleared = sem("cleared")
        block = st.enter_context(nc.Block())

        @block.sync
        def _(sp):
            def fetch(t, u):
                sp.dma_start(HR[:, u, :], table2[bass.ds(t * P, P), :]).then_inc(mine_in[u], 16)
                sp.dma_start(RS[:, u, :], resid[bass.ds(t * P, P), :]).then_inc(mine_in[u], 16)

            for t in range(4):
                fetch(t, t)
            for t, u in tiles(sp, 4, TILES, 4):
                sp.wait_ge(x1_ready, t - 3)
                fetch(t, u)

        @block.gpsimd
        def _(pool):
            pool.memset(zero[:, :, :], 0.0).then_inc(blank, 1)

        @block.scalar
        def _(act):
            act.wait_ge(blank, 1)
            for e in range(EXPERTS):
                act.dma_start(xbuf[e * CT * P:(e + 1) * CT * P, :].rearrange("(p j) n -> p j n", p=P), zero[:, :, :]).then_inc(cleared, 16)
            act.wait_ge(cleared, 16 * EXPERTS)

        @block.vector
        def _(dve):
            own_ = Chain(dve, own)
            own_.link(dve.tensor_tensor(RD[:, :], ACC[:, :, D], SELF[:, :, 0], ALU.add))
            own_.link(dve.reciprocal(RD[:, :], RD[:, :]))

            def row(what, t):
                return what[:, bass.ds(t, 1), :].rearrange("p a b -> p (a b)")

            def total(t, u):
                dve.wait_ge(mine_in[u], (t - u) * 8 + 32)
                dve.scalar_tensor_tensor(T[:, u, :], HR[:, u, 0:D + 1], row(SELF, t), row(ACC, t), ALU.mult, ALU.add).then_inc(summed, 1)

            def quotient(t, u):
                dve.wait_ge(summed, t + 1)
                dve.scalar_tensor_tensor(row(X1, t), T[:, u, 0:D], RD[:, bass.ds(t, 1)], RS[:, u, :], ALU.mult, ALU.add).then_inc(x1_ready, 1)

            def statistics(t):
                dve.wait_ge(x1_ready, t + 1)
                dve.bn_stats(row(bn, t), row(X1, t))

            total(0, 0)
            total(1, 1)
            quotient(0, 0)
            for t, u in tiles(dve, 2, TILES, 4):
                total(t, u)
                quotient(t - 1, (u + 3) % 4)
                statistics(t - 2)
            quotient(TILES - 1, (TILES - 1) % 4)
            statistics(TILES - 2)
            statistics(TILES - 1)


def gate(nc, allocator, dev, X1, bn, m1, r1, LG):
    PS, ident = dev["PS"], dev["ident"]
    with ExitStack() as st:
        sb, sem = allocator(st)
        va = sb("va1", [P, TILES])
        ta = sb("ta1", [P, TILES])
        GW = sb("GW", [P, 2, EXPERTS])
        gb = sb("gb", [P, EXPERTS])
        XN = sb("XN", [P, 4, D])
        XNT = sb("XNT", [P, 4, 2, P])
        own, to_root, rooted, loaded = sem("g_own"), sem("g_to_root"), sem("g_rooted"), sem("g_loaded")
        xn_ready, xn_turned, xnt_ready = sem("xn_ready"), sem("xn_turned"), sem("xnt_ready")
        lg_done, lg_ready = sem("lg_done"), sem("lg_ready")
        block = st.enter_context(nc.Block())

        @block.sync
        def _(sp):
            sp.dma_start(GW[:, :, :], dev["gate_w"].rearrange("(k p) e -> p k e", p=P)).then_inc(loaded, 16)
            sp.dma_start(gb[:, :], dev["gate_b"].partition_broadcast(P)).then_inc(loaded, 16)

        @block.vector
        def _(dve):
            own_ = Chain(dve, own)
            moments(dve, own_, bn, m1, va, ta)
            own_.link(dve.tensor_scalar(ta[:, :], va[:, :], EPS, None, ALU.add))
            dve.engine_nop().then_inc(to_root, 1)
            dve.wait_ge(rooted, 1)
            own_.link(dve.reciprocal(r1[:, :], ta[:, :]))

            def norm(t, u):
                if not isinstance(t, int) or t > 3:
                    dve.wait_ge(xn_turned, t - 3)
                dve.tensor_scalar(XN[:, u, :], X1[:, bass.ds(t, 1), :].rearrange("p a b -> p (a b)"),
                                  m1[:, bass.ds(t, 1)], r1[:, bass.ds(t, 1)], ALU.subtract, ALU.mult).then_inc(xn_ready, 1)

            def logits(t, u):
                dve.wait_ge(lg_done, t + 1)
                dve.tensor_tensor(LG[:, bass.ds(t, 1), :].rearrange("p a b -> p (a b)"), PS[:, 2 + u % 2, 0:EXPERTS], gb[:, :],
                                  ALU.add).then_inc(lg_ready, 1)

            for t in range(4):
                norm(t, t)
            dve.wait_ge(loaded, 32)
            for t, u in tiles(dve, 4, TILES, 4):
                norm(t, u)
                logits(t - 4, u)
            for t in range(TILES - 4, TILES):
                logits(t, t % 4)

        @block.scalar
        def _(act):
            act.wait_ge(to_root, 1)
            act.activation(ta[:, :], ta[:, :], ACT.Sqrt).then_inc(rooted, 1)

            def copy(t, u):
                act.wait_ge(xn_turned, t + 1)
                if not isinstance(t, int) or t > 3:
                    act.wait_ge(lg_done, t - 3)
                act.activation(XNT[:, u, :, :], PS[:, u % 2, 0:2 * P].rearrange("p (k q) -> p k q", k=2), ACT.Copy).then_inc(xnt_ready, 1)

            for t in range(4):
                copy(t, t)
            for t, u in tiles(act, 4, TILES, 4):
                copy(t, u)

        @block.tensor
        def _(pe):
            def turn(t, u):
                pe.wait_ge(xn_ready, t + 1)
                if not isinstance(t, int) or t > 1:
                    pe.wait_ge(xnt_ready, t - 1)
                for k in range(2):
                    last = pe.transpose(PS[:, u % 2, k * P:(k + 1) * P], XN[:, u, k * P:(k + 1) * P], ident[:, :])
                last.then_inc(xn_turned, 1)

            def product(t, u):
                pe.wait_ge(xnt_ready, t + 1)
                if not isinstance(t, int) or t > 1:
                    pe.wait_ge(lg_ready, t - 1)
                for k in range(2):
                    last = pe.matmul(PS[:, 2 + u % 2, 0:EXPERTS], XNT[:, u, k, :], GW[:, k, :], start=k == 0, stop=k == 1)
                last.then_inc(lg_done, 1)

            pe.wait_ge(loaded, 32)
            turn(0, 0)
            turn(1, 1)
            for t in (2, 3):
                turn(t, t)
                product(t - 2, t - 2)
            for t, u in tiles(pe, 4, TILES, 4):
                turn(t, u)
                product(t - 2, (u + 2) % 4)
            for t in (TILES - 2, TILES - 1):
                product(t, t % 4)


def route(nc, allocator, dev, LG, weight, put, take):
    PS, ones, iota_row = dev["PS"], dev["ones"], dev["iota_row"]
    with ExitStack() as st:
        sb, sem = allocator(st)
        lmax = sb("lmax", [P, TILES])
        EXL = sb("EXL", [P, TILES, EXPERTS])
        OH = sb("OH", [P, TILES, EXPERTS])
        CU = sb("CU", [P, TILES, EXPERTS])
        TOT = sb("TOT", [P, EXPERTS, TILES])
        INC = sb("INC", [P, EXPERTS, TILES])
        onesT = sb("onesT", [P, TILES])
        tri = sb("tri", [P, P])
        lane = sb("lane", [P, 1])
        choice, psum_, place, kept, full = (sb(n, [P, TILES]) for n in ("choice", "psum_", "place", "kept", "full"))
        own, consts, shifted, exped = sem("t_own"), sem("t_consts"), sem("t_shifted"), sem("t_exped")
        hot, counted = sem("t_hot"), sem("counted")
        block = st.enter_context(nc.Block())
        NOWHERE = float(1 << 20)

        @block.gpsimd
        def _(pool):
            pool.memset(onesT[:, :], 1.0).then_inc(consts, 1)
            pool.iota(lane[:, :], [[0, 1]], base=0, channel_multiplier=1, allow_small_or_imprecise_dtypes=True).then_inc(consts, 1)
            pool.affine_select(out=tri[:, :], in_=ones[:, :], compare_op=ALU.is_gt, fill=0.0,
                               base=0, pattern=[[1, P]], channel_multiplier=-1).then_inc(consts, 1)

        @block.scalar
        def _(act):
            act.wait_ge(shifted, 1)
            act.activation(EXL[:, :, :], EXL[:, :, :], ACT.Exp).then_inc(exped, 1)

        @block.tensor
        def _(pe):
            pe.wait_ge(consts, 3)
            pe.wait_ge(hot, 1)
            oh = OH[:, :, :].rearrange("p t e -> p (t e)")
            pe.matmul(PS[:, 0, 0:TILES * EXPERTS], tri[:, :], oh, start=True, stop=True)
            pe.matmul(PS[:, 1, 0:TILES * EXPERTS], ones[:, :], oh, start=True, stop=True).then_inc(counted, 1)

        @block.vector
        def _(dve):
            own_ = Chain(dve, own)
            own_.link(dve.tensor_reduce(lmax[:, :], LG[:, :, :], X, ALU.max))
            dve.tensor_tensor(EXL[:, :, :], LG[:, :, :], one(lmax[:, :], 2, EXPERTS), ALU.subtract).then_inc(shifted, 1)
            own_.link(dve.tensor_tensor(OH[:, :, :], LG[:, :, :], one(lmax[:, :], 2, EXPERTS), ALU.is_equal))
            number = one(iota_row[:, 0:EXPERTS], 1, TILES)
            own_.link(dve.tensor_scalar(CU[:, :, :], OH[:, :, :], -float(EXPERTS), float(EXPERTS), ALU.mult, ALU.add))
            own_.link(dve.tensor_tensor(CU[:, :, :], CU[:, :, :], number, ALU.add))
            own_.link(dve.tensor_reduce(choice[:, :], CU[:, :, :], X, ALU.min))
            own_.link(dve.tensor_tensor(OH[:, :, :], number, one(choice[:, :], 2, EXPERTS), ALU.is_equal))
            dve.engine_nop().then_inc(hot, 1)
            dve.wait_ge(consts, 3)
            dve.wait_ge(counted, 1)
            own_.link(dve.tensor_copy(TOT[:, :, :], PS[:, 1, 0:TILES * EXPERTS].rearrange("p (t e) -> p e t", e=EXPERTS)))
            for e in range(EXPERTS):
                own_.link(dve.tensor_tensor_scan(INC[:, e, :], onesT[:, :], TOT[:, e, :], 0.0, ALU.mult, ALU.add))
            own_.link(dve.tensor_tensor(INC[:, :, :], INC[:, :, :], TOT[:, :, :], ALU.subtract))
            own_.link(dve.tensor_tensor(CU[:, :, :], PS[:, 0, 0:TILES * EXPERTS].rearrange("p (t e) -> p t e", e=EXPERTS),
                                        INC[:, :, :].rearrange("p e t -> p t e"), ALU.add))
            own_.link(dve.tensor_tensor(CU[:, :, :], CU[:, :, :], OH[:, :, :], ALU.mult))
            own_.link(dve.tensor_reduce(place[:, :], CU[:, :, :], X, ALU.add))
            own_.link(dve.tensor_scalar(kept[:, :], place[:, :], float(CAP), None, ALU.is_lt))
            own_.link(dve.tensor_scalar(place[:, :], place[:, :], float(CAP - 1), None, ALU.min))
            own_.link(dve.scalar_tensor_tensor(place[:, :], choice[:, :], float(CAP), place[:, :], ALU.mult, ALU.add))
            own_.link(dve.tensor_copy(take[:, :], place[:, :]))
            own_.link(dve.tensor_scalar(full[:, :], kept[:, :], -NOWHERE, NOWHERE, ALU.mult, ALU.add))
            own_.link(dve.tensor_tensor(place[:, :], place[:, :], full[:, :], ALU.add))
            own_.link(dve.tensor_scalar(lane[:, :], lane[:, :], float(LAST), NOWHERE, ALU.is_ge, ALU.mult))
            own_.link(dve.tensor_tensor(place[:, TILES - 1:TILES], place[:, TILES - 1:TILES], lane[:, :], ALU.add))
            own_.link(dve.tensor_copy(put[:, :], place[:, :]))
            dve.wait_ge(exped, 1)
            own_.link(dve.tensor_reduce(psum_[:, :], EXL[:, :, :], X, ALU.add))
            own_.link(dve.reciprocal(psum_[:, :], psum_[:, :]))
            own_.link(dve.tensor_tensor(weight[:, :], psum_[:, :], kept[:, :], ALU.mult))


def dispatch(nc, allocator, dev, X1, m1, r1, put):
    xbuf = dev["xbuf"]
    with ExitStack() as st:
        sb, sem = allocator(st)
        XN = sb("XNd", [P, 4, D])
        idx = sb("putx", [P, 4], I32)
        ready, placed = sem("d_ready"), [sem(f"d_placed{r}") for r in range(4)]
        staged, released = sem("d_staged"), sem("d_released")
        block = st.enter_context(nc.Block())

        def landed(t, r):
            return rounds(t, r, 4) - 16

        @block.vector
        def _(dve):
            for t, r in ring4(dve):
                if not isinstance(t, int) or t >= 4:
                    dve.wait_ge(placed[r], landed(t, r))
                dve.tensor_scalar(XN[:, r, :], X1[:, bass.ds(t, 1), :].rearrange("p a b -> p (a b)"),
                                  m1[:, bass.ds(t, 1)], r1[:, bass.ds(t, 1)], ALU.subtract, ALU.mult).then_inc(ready, 1)

        @block.scalar
        def _(act):
            for t, r in ring4(act):
                if not isinstance(t, int) or t >= 4:
                    act.wait_ge(placed[r], landed(t, r))
                act.activation(idx[:, r:r + 1], put[:, bass.ds(t, 1)], ACT.Copy).then_inc(staged, 1)

        @block.gpsimd
        def _(pool):
            for t, r in tiles(pool, 0, TILES, 4):
                pool.wait_ge(ready, t + 1)
                pool.wait_ge(staged, t + 1)
                pool.sem_inc(released, 1)
                pool.indirect_dma_start(xbuf, IndexOn(ap=idx[:, r:r + 1], axis=0), XN[:, r, :], None,
                                        bounds_check=EXPERTS * CAP - 1, oob_is_err=False).then_inc(placed[r], 16)
            for r in range(4):
                pool.wait_ge(placed[r], 16 * len(range(r, TILES, 4)))


def experts(nc, allocator, dev, ysum):
    PS, ident, xbuf, ybuf = (dev[k] for k in ("PS", "ident", "xbuf", "ybuf"))
    ew1, eb1, ew2, eb2 = (dev[k] for k in ("ew1", "eb1", "ew2", "eb2"))
    KF = FF // P
    CH = [(0, 512), (512, CAP - 512)]
    with ExitStack() as st:
        sb, sem = allocator(st)
        w1 = sb("w1", [P, 2, 2, FF])
        w2 = sb("w2", [P, 2, KF, D])
        c1 = sb("c1", [P, 2, KF])
        c2 = sb("c2", [P, 2, D])
        XB = sb("XB", [P, 2, CT, D])
        XT = sb("XT", [P, 2, CT * P])
        HT = sb("HT", [P, KF, CAP])
        YS = sb("YS", [P, 2, CT, D])
        loaded = [sem(f"e_loaded{u}") for u in range(2)]
        stored = [sem(f"e_stored{u}") for u in range(2)]
        cleared = sem("e_cleared")
        turned, copied, up, relu, down, y_ready = (sem("e_" + n) for n in ("turned", "copied", "up", "relu", "down", "y_ready"))
        block = st.enter_context(nc.Block())
        REST = CAP - (CT - 1) * P

        def rows_of(j):
            return P if j < CT - 1 else REST

        @block.sync
        def _(sp):
            def load(e, u):
                def at(a):
                    return a[bass.ds(e, 1)]
                sp.dma_start(XB[:, u, :, :], xbuf[bass.ds(e * CAP, CT * P), :].rearrange("(j p) n -> p j n", p=P)).then_inc(loaded[u], 16)
                sp.dma_start(w1[:, u, :, :], at(ew1).rearrange("a (k p) f -> p (a k) f", p=P)).then_inc(loaded[u], 16)
                with nc.allow_non_contiguous_dma(reason="a bias per partition"):
                    sp.dma_start(c1[:, u, :], at(eb1).rearrange("a (k p) -> p (a k)", p=P)).then_inc(loaded[u], 16)
                sp.dma_start(c2[:, u, :], at(eb2).rearrange("a n -> (a n)").partition_broadcast(P)).then_inc(loaded[u], 16)
                sp.dma_start(w2[:, u, :, :], at(ew2).rearrange("a (k p) n -> p (a k) n", p=P)).then_inc(loaded[u], 16)

            def store(e, u):
                sp.wait_ge(y_ready, CT * e + CT)
                sp.dma_start(ybuf[bass.ds(e * CAP, (CT - 1) * P), :].rearrange("(j p) n -> p j n", p=P), YS[:, u, 0:CT - 1, :]).then_inc(stored[u], 16)
                sp.dma_start(ybuf[bass.ds(e * CAP + (CT - 1) * P, REST), :], YS[0:REST, u, CT - 1, :]).then_inc(stored[u], 16)

            load(0, 0)
            load(1, 1)
            for e, u in tiles(sp, 0, EXPERTS - 2, 2):
                store(e, u)
                sp.wait_ge(down, CT * (e + 1))
                load(e + 2, u)
            for e in (EXPERTS - 2, EXPERTS - 1):
                store(e, e % 2)
            for u in range(2):
                sp.wait_ge(stored[u], 32 + 32 * (EXPERTS // 2))

        @block.tensor
        def _(pe):
            def turn(e, u):
                pe.wait_ge(loaded[u], (e - u) * 40 + 80)
                for i in range(4):
                    n = 4 * e + i
                    if not isinstance(e, int) or n > 1:
                        pe.wait_ge(copied, n - 1)
                    for j in range(2):
                        for k in range(2):
                            last = pe.transpose(PS[:, i % 2, (2 * j + k) * P:(2 * j + k + 1) * P],
                                                XB[:, u, 2 * i + j, k * P:(k + 1) * P], ident[:, :])
                    last.then_inc(turned, 1)

            def widen(e, u):
                pe.wait_ge(copied, 4 * e + 4)
                for c, (at, n) in enumerate(CH):
                    for f in range(KF):
                        i = 2 * KF * e + KF * c + f
                        if not isinstance(e, int) or i > 1:
                            pe.wait_ge(relu, i - 1)
                        for k in range(2):
                            last = pe.matmul(PS[:, 2 + f % 2, 0:n], w1[:, u, k, f * P:(f + 1) * P], XT[:, k, at:at + n],
                                             start=k == 0, stop=k == 1)
                        last.then_inc(up, 1)

            def narrow(e, u):
                for j in range(CT):
                    i = CT * e + j
                    pe.wait_ge(relu, 2 * KF * e + (KF if j < 4 else 2 * KF))
                    if not isinstance(e, int) or i > 1:
                        pe.wait_ge(y_ready, i - 1)
                    for f in range(KF):
                        last = pe.matmul(PS[0:rows_of(j), 4 + j % 2, 0:D], HT[:, f, j * P:j * P + rows_of(j)], w2[:, u, f, :],
                                         start=f == 0, stop=f == KF - 1)
                    last.then_inc(down, 1)

            turn(0, 0)
            widen(0, 0)
            turn(1, 1)
            narrow(0, 0)
            for e, u in tiles(pe, 1, EXPERTS - 1, 2):
                widen(e, u)
                turn(e + 1, 1 - u)
                narrow(e, u)
            e = EXPERTS - 1
            widen(e, e % 2)
            narrow(e, e % 2)

        @block.scalar
        def _(act):
            for e, u in tiles(act, 0, EXPERTS, 2):
                for c, (at, n) in enumerate(CH):
                    for f in range(KF):
                        act.wait_ge(up, 2 * KF * e + KF * c + f + 1)
                        act.activation(HT[:, f, at:at + n], PS[:, 2 + f % 2, 0:n], ACT.Relu, bias=c1[:, u, f:f + 1]).then_inc(relu, 1)

        @block.vector
        def _(dve):
            def copy(e):
                for i in range(4):
                    dve.wait_ge(turned, 4 * e + i + 1)
                    dve.tensor_copy(XT[:, :, 2 * i * P:2 * (i + 1) * P].rearrange("p k (j q) -> p j k q", j=2),
                                    PS[:, i % 2, :].rearrange("p (j k q) -> p j k q", j=2, k=2)).then_inc(copied, 1)

            def finish(e, u):
                dve.wait_ge(stored[u], (e - u) * 16 + 32)
                for j in range(CT):
                    n = rows_of(j)
                    dve.wait_ge(down, CT * e + j + 1)
                    dve.scalar_tensor_tensor(YS[0:n, u, j, :], PS[0:n, 4 + j % 2, 0:D], 1.0, c2[0:n, u, :], ALU.mult, ALU.add,
                                             accum_out=ysum[0:n, bass.ds(CT * e + j, 1)]).then_inc(y_ready, 1)

            for u in range(2):
                dve.sem_inc(stored[u], 32)
            dve.memset(ysum[:, :], 0.0).then_inc(cleared, 1)
            dve.wait_ge(cleared, 1)
            copy(0)
            copy(1)
            finish(0, 0)
            for e, u in tiles(dve, 1, EXPERTS - 1, 2):
                copy(e + 1)
                finish(e, u)
            finish(EXPERTS - 1, (EXPERTS - 1) % 2)


def combine(nc, allocator, dev, X1, weight, take, ysum):
    ybuf, out = dev["ybuf"], dev["out"]
    with ExitStack() as st:
        sb, sem = allocator(st)
        YG = sb("YG", [P, 4, D])
        idx = sb("takex", [P, 4], I32)
        C = sb("C", [P, 2, D])
        number = sb("number", [P, 2, D], I32)
        finite = sb("finite", [P, 2, D], I32)
        OT = sb("OT", [P, 2, D])
        staged, released, own, taken, o_ready = (sem("c_" + n) for n in ("staged", "released", "own", "taken", "o_ready"))
        passed = sem("c_passed")
        wsum = sb("wsum", [P, 1])
        odd = sb("odd", [P, EXPERTS * CT + 1])
        odds = sb("odds", [P, 1])
        odd_any = sb("odd_any", [P, 1])
        general = sb("general", [P, 1], I32)
        sums_own, odds_ready, odds_all, general_ready = (sem("c_" + n) for n in ("sums_own", "odds_ready", "odds_all", "general_ready"))
        fetched = [sem(f"c_fetched{r}") for r in range(4)]
        stored = [sem(f"c_stored{u}") for u in range(2)]
        block = st.enter_context(nc.Block())

        @block.scalar
        def _(act):
            for t, r in ring4(act):
                if not isinstance(t, int) or t >= 4:
                    act.wait_ge(fetched[r], rounds(t, r, 4) - 16)
                act.activation(idx[:, r:r + 1], take[:, bass.ds(t, 1)], ACT.Copy).then_inc(staged, 1)

        @block.gpsimd
        def _(pool):
            pool.wait_ge(odds_ready, 1)
            pool.partition_all_reduce(odd_any[:, :], odds[:, :], P, RMAX).then_inc(odds_all, 1)
            pool.sem_inc(taken, 4)
            for t, r in tiles(pool, 0, TILES, 4):
                pool.wait_ge(staged, t + 1)
                pool.wait_ge(taken, t + 1)
                pool.sem_inc(released, 1)
                pool.indirect_dma_start(YG[:, r, :], None, ybuf, IndexOn(ap=idx[:, r:r + 1], axis=0)).then_inc(fetched[r], 16)

        @block.vector
        def _(dve):
            so_ = Chain(dve, sums_own)
            so_.link(dve.tensor_reduce(wsum[:, :], weight[:, :], X, ALU.add))
            so_.link(dve.tensor_scalar(odd[:, 0:EXPERTS * CT], ysum[:, :], 0.0, 0.0, ALU.mult, ALU.is_equal))
            so_.link(dve.tensor_scalar(odd[:, EXPERTS * CT:], wsum[:, :], 0.0, 0.0, ALU.mult, ALU.is_equal))
            so_.link(dve.tensor_scalar(odd[:, :], odd[:, :], -1.0, 1.0, ALU.mult, ALU.add))
            so_.link(dve.tensor_reduce(odds[:, :], odd[:, :], X, ALU.max))
            dve.engine_nop().then_inc(odds_ready, 1)
            dve.wait_ge(odds_all, 1)
            dve.tensor_copy(general[:, :], odd_any[:, :]).then_inc(general_ready, 1)
            dve.wait_ge(general_ready, 1)
            flag = dve.value_load(general[0:1, 0:1], min_val=0, max_val=1)
            with dve.If(flag > 0):
                own_ = Chain(dve, own)
                for t, r in tiles(dve, 0, TILES, 4):
                    u = r % 2
                    own_.at(5 * t)
                    y, c, o = YG[:, r, :], C[:, u, :], OT[:, u, :]
                    dve.wait_ge(stored[u], rounds(t, u))
                    dve.wait_ge(fetched[r], rounds(t, r, 4))
                    own_.link(dve.tensor_scalar(y, y, weight[:, bass.ds(t, 1)], None, ALU.mult))
                    dve.tensor_scalar(c, y, -10000.0, 10000.0, ALU.max, ALU.min)
                    dve.tensor_tensor(number[:, u, :], y, y, ALU.is_equal)
                    dve.tensor_scalar(finite[:, u, :], y, 0.0, 0.0, ALU.mult, ALU.is_equal)
                    own_.link(dve.memset(o, 0.0))
                    dve.sem_inc(passed, 1)
                    own_.link(dve.copy_predicated(o, number[:, u, :], c))
                    dve.sem_inc(passed, 1)
                    own_.link(dve.copy_predicated(o, finite[:, u, :], y))
                    own_.link(dve.tensor_tensor(o, o, X1[:, bass.ds(t, 1), :].rearrange("p a b -> p (a b)"), ALU.add))
                    dve.sem_inc(taken, 1)
                    dve.sem_inc(o_ready, 1)
                    own_.closed(5)
            with dve.If(flag < 1):
                for t, r in tiles(dve, 0, TILES, 4):
                    u = r % 2
                    dve.wait_ge(stored[u], rounds(t, u))
                    dve.wait_ge(fetched[r], rounds(t, r, 4))
                    dve.scalar_tensor_tensor(OT[:, u, :], YG[:, r, :], weight[:, bass.ds(t, 1)],
                                             X1[:, bass.ds(t, 1), :].rearrange("p a b -> p (a b)"), ALU.mult, ALU.add).then_inc(own, 1)
                    dve.wait_ge(own, t + 1)
                    dve.sem_inc(taken, 1)
                    dve.sem_inc(o_ready, 1)

        @block.sync
        def _(sp):
            for u in range(2):
                sp.sem_inc(stored[u], 16)
            for t, u in tiles(sp, 0, TILES - 1, 2):
                sp.wait_ge(o_ready, t + 1)
                sp.dma_start(out[bass.ds(t * P, P), :], OT[:, u, :]).then_inc(stored[u], 16)
            t = TILES - 1
            sp.wait_ge(o_ready, TILES)
            sp.dma_start(out[t * P:N, :], OT[0:LAST, t % 2, :]).then_inc(stored[t % 2], 16)
            for u in range(2):
                sp.wait_ge(stored[u], 16 + 16 * len(range(u, TILES, 2)))


INS = ["x", "src", "dst", "L0_gnn_ln_w", "L0_gnn_ln_b", "L0_gnn_W1", "L0_gnn_att_src1", "L0_gnn_att_dst1",
       "L0_gnn_b1", "L0_gnn_W2", "L0_gnn_att_src2", "L0_gnn_att_dst2", "L0_gnn_b2", "L0_mix_w_qkv",
       "L0_mix_mem_kv", "L0_mix_w_out", "L0_mix_b_out", "L0_mix_g_out", "L0_mix_g_pre", "L0_ffn_gate_w",
       "L0_ffn_gate_b", "L0_ffn_w1", "L0_ffn_b1", "L0_ffn_w2", "L0_ffn_b2"]


def laid_out(inputs):
    import numpy as np

    arrays = {}
    for name in INS:
        a = np.ascontiguousarray(inputs[name])
        if name in ("src", "dst"):
            fill = np.full(GROUPS * GROUP - E, 0 if name == "src" else NP - 1, a.dtype)
            a = np.concatenate([a, fill]).reshape(GROUPS, GROUP)
        arrays[f"in_{name}"] = a
    return arrays


def kernel(**inputs):
    import numpy as np
    import concourse.bacc as bacc
    from concourse.bass_utils import run_bass_kernel_spmd

    nc = bacc.Bacc("TRN2", target_bir_lowering=False, num_devices=1)
    arrays = laid_out(inputs)
    args = [nc.dram_tensor(n, a.shape, mybir.dt.from_np(a.dtype), kind="ExternalInput").ap() for n, a in arrays.items()]
    out = nc.dram_tensor("out", [N, D], F32, kind="ExternalOutput").ap()
    gps_program(nc, *args, out)
    got = run_bass_kernel_spmd(nc, [arrays], core_ids=[0])
    return np.asarray(got.results[0]["out"])
```
